# Optimizing a Trainium2 kernel written in Bass

```python
import numpy as np
import jax
import jax.numpy as jnp

def _softmax(x, axis=-1):
    return jax.nn.softmax(x, axis=axis)

def _gelu(x):
    return jax.nn.gelu(x, approximate=True)

def _silu(x):
    return jax.nn.silu(x)

def _sigmoid(x):
    return jax.nn.sigmoid(x)

def _layernorm(x, axis=-1, eps=1e-05):
    m = jnp.mean(x, axis=axis, keepdims=True)
    v = jnp.var(x, axis=axis, keepdims=True)
    return (x - m) / jnp.sqrt(v + eps)

def _scatter_add(tgt, idx, src, axis=0):
    return tgt.at[idx].add(src)

def _segment_sum(src, seg, n):
    return jax.ops.segment_sum(src, seg, n)
kernel_name = 'mk_xattn_ffn_d1_seqx_r4_037027'

def setup_inputs(seed: int=0):
    np.random.seed(seed)
    _w = jnp.asarray

    def _rec_inputs():
        import jax
        import jax.numpy as jnp
        _rk = jax.random.key(seed)
        x = -0.0003929 + 0.9999 * jax.random.normal(jax.random.fold_in(_rk, 1), (4, 512, 256), jnp.float32)
        _lenS = 512 - jax.random.randint(jax.random.fold_in(_rk, 7), (4,), 0, max(1, 512 // 4) + 1, jnp.int32)
        _lenS2 = 1601 - jax.random.randint(jax.random.fold_in(_rk, 8), (4,), 0, max(1, 1601 // 4) + 1, jnp.int32)
        _ctx_2048P = jax.random.normal(jax.random.fold_in(_rk, 11), (4, 16, 512), jnp.float32)
        _ctx_2048c = jax.random.dirichlet(jax.random.fold_in(_rk, 511), 0.3 * jnp.ones((16,), jnp.float32), (4, 1601))
        _ctx_2048t = jnp.einsum('bsk,bkd->bsd', _ctx_2048c, _ctx_2048P)
        _ctx_2048t = _ctx_2048t * jax.lax.rsqrt(jnp.mean(jnp.square(_ctx_2048t)) + 1e-12) * 0.953939
        ctx_2048 = 4.13588e-05 + 0.999923 * (_ctx_2048t + 0.3 * jax.random.normal(jax.random.fold_in(_rk, 611), (4, 1601, 512), jnp.float32))
        _validS = jnp.arange(512)[None, :] < _lenS[:, None]
        _validS2 = jnp.arange(1601)[None, :] < _lenS2[:, None]
        _causal = jnp.tril(jnp.ones((512, 512), dtype=bool))
        mask_BxS2_if0 = jnp.where(jnp.ones((4, 1601), dtype=bool), 4, 0).astype(jnp.int32)
        return (x, ctx_2048, mask_BxS2_if0)
    x, ctx_2048, mask_BxS2_if0 = _rec_inputs()

    def _L0_xattn_setup():
        import jax, jax.numpy as jnp
        import numpy as np
        B, L, P = (4, 1024, 256)
        D_MODEL = 256
        D_GLOBAL = 512
        HEADDIM = 32
        EPSILON = 0.001
        RMS_EPS = 1e-05

        def rmsnorm(x, g, eps=RMS_EPS):
            var = jnp.mean(jnp.square(x), axis=-1, keepdims=True)
            return x * jax.lax.rsqrt(var + eps) * g

        def _hnet_depool(h, h_patch_full, patch_lens):
            h_patch = h_patch_full[..., :D_MODEL]
            bsz, plen = (h_patch.shape[0], h_patch.shape[1])
            seqlen = h.shape[1]
            logp = jnp.full((bsz, plen), -EPSILON, dtype=jnp.float32)
            bidx = jnp.cumsum(patch_lens, axis=1) - 1
            boundary_mask = jnp.zeros((bsz, seqlen), dtype=jnp.int32)
            boundary_mask = boundary_mask.at[jnp.arange(bsz)[:, None], bidx].set(1)
            dt = (-jnp.log(-jnp.expm1(logp))).astype(h_patch.dtype)
            x = h_patch / dt[..., None]
            n_heads = D_MODEL // HEADDIM
            A = -jnp.ones((n_heads,), dtype=jnp.float32)
            bcoef = jnp.exp(logp).astype(h_patch.dtype)
            x4 = x.reshape(bsz, plen, n_heads, HEADDIM)
            a = jnp.exp(dt[:, :, None] * A[None, None, :])
            u = (dt * bcoef)[:, :, None, None] * x4
            a_b = jnp.broadcast_to(a[..., None], u.shape)

            def comb(lft, rgt):
                aL, uL = lft
                aR, uR = rgt
                return (aL * aR, uL * aR + uR)
            _, s = jax.lax.associative_scan(comb, (a_b, u), axis=1)
            depool = s.reshape(bsz, plen, D_MODEL)
            plug = jnp.clip(jnp.cumsum(boundary_mask, axis=1) - 1, 0, plen - 1)
            depool_out = depool[jnp.arange(bsz)[:, None], plug]
            return depool_out + h
        key = jax.random.key(seed)
        k1, k2, k3, k4 = jax.random.split(key, 4)
        embeds = jax.random.normal(k1, (B, L, D_MODEL), dtype=jnp.float32)
        patch_embeds = jax.random.normal(k2, (B, P, D_GLOBAL), dtype=jnp.float32)
        patch_lens = jnp.full((B, P), L // P, dtype=jnp.int64)
        W_in = jax.random.normal(k3, (D_MODEL, D_MODEL), dtype=jnp.float32) * 0.02
        b_in = jnp.zeros((D_MODEL,), dtype=jnp.float32)
        g_res = jnp.ones((D_MODEL,), dtype=jnp.float32)
        g_init = jnp.ones((D_GLOBAL,), dtype=jnp.float32)
        return {'embeds': embeds, 'patch_embeds': patch_embeds, 'patch_lens': patch_lens, 'W_in': W_in, 'b_in': b_in, 'g_res': g_res, 'g_init': g_init}
    _L0_xattn_all = _L0_xattn_setup()
    _L0_xattn_in = {k: v for k, v in _L0_xattn_all.items() if k in ('W_in', 'b_in', 'g_res', 'g_init')}
    del _L0_xattn_all

    def _L0_ffn_setup():
        import jax, jax.numpy as jnp
        import numpy as np
        TOP_K = 2
        key = jax.random.key(seed)
        ks = jax.random.split(key, 5)
        B, T, D, F, E = (4, 512, 256, 1024, 8)
        s = 0.02
        return {'x': jax.random.normal(ks[0], (B, T, D), jnp.float32), 'gate_w': jax.random.normal(ks[1], (D, E), jnp.float32) * s, 'w1': jax.random.normal(ks[2], (E, D, F), jnp.float32) * s, 'w3': jax.random.normal(ks[3], (E, D, F), jnp.float32) * s, 'w2': jax.random.normal(ks[4], (E, F, D), jnp.float32) * s}
    _L0_ffn_all = _L0_ffn_setup()
    _L0_ffn_in = {k: v for k, v in _L0_ffn_all.items() if k in ('gate_w', 'w1', 'w3', 'w2')}
    del _L0_ffn_all
    return {'x': x, 'ctx_2048': ctx_2048, 'mask_BxS2_if0': mask_BxS2_if0, 'L0_xattn_W_in': _L0_xattn_in['W_in'], 'L0_xattn_b_in': _L0_xattn_in['b_in'], 'L0_xattn_g_res': _L0_xattn_in['g_res'], 'L0_xattn_g_init': _L0_xattn_in['g_init'], 'L0_ffn_gate_w': _L0_ffn_in['gate_w'], 'L0_ffn_w1': _L0_ffn_in['w1'], 'L0_ffn_w3': _L0_ffn_in['w3'], 'L0_ffn_w2': _L0_ffn_in['w2']}

def reference(x, ctx_2048, mask_BxS2_if0, L0_xattn_W_in, L0_xattn_b_in, L0_xattn_g_res, L0_xattn_g_init, L0_ffn_gate_w, L0_ffn_w1, L0_ffn_w3, L0_ffn_w2):
    import jax
    import jax.numpy as jnp

    def _L0_xattn_ref(embeds, patch_embeds, patch_lens, W_in, b_in, g_res, g_init):
        import jax, jax.numpy as jnp
        import numpy as np
        B, L, P = (4, 1024, 256)
        D_MODEL = 256
        D_GLOBAL = 512
        HEADDIM = 32
        EPSILON = 0.001
        RMS_EPS = 1e-05

        def rmsnorm(x, g, eps=RMS_EPS):
            var = jnp.mean(jnp.square(x), axis=-1, keepdims=True)
            return x * jax.lax.rsqrt(var + eps) * g

        def _hnet_depool(h, h_patch_full, patch_lens):
            h_patch = h_patch_full[..., :D_MODEL]
            bsz, plen = (h_patch.shape[0], h_patch.shape[1])
            seqlen = h.shape[1]
            logp = jnp.full((bsz, plen), -EPSILON, dtype=jnp.float32)
            bidx = jnp.cumsum(patch_lens, axis=1) - 1
            boundary_mask = jnp.zeros((bsz, seqlen), dtype=jnp.int32)
            boundary_mask = boundary_mask.at[jnp.arange(bsz)[:, None], bidx].set(1)
            dt = (-jnp.log(-jnp.expm1(logp))).astype(h_patch.dtype)
            x = h_patch / dt[..., None]
            n_heads = D_MODEL // HEADDIM
            A = -jnp.ones((n_heads,), dtype=jnp.float32)
            bcoef = jnp.exp(logp).astype(h_patch.dtype)
            x4 = x.reshape(bsz, plen, n_heads, HEADDIM)
            a = jnp.exp(dt[:, :, None] * A[None, None, :])
            u = (dt * bcoef)[:, :, None, None] * x4
            a_b = jnp.broadcast_to(a[..., None], u.shape)

            def comb(lft, rgt):
                aL, uL = lft
                aR, uR = rgt
                return (aL * aR, uL * aR + uR)
            _, s = jax.lax.associative_scan(comb, (a_b, u), axis=1)
            depool = s.reshape(bsz, plen, D_MODEL)
            plug = jnp.clip(jnp.cumsum(boundary_mask, axis=1) - 1, 0, plen - 1)
            depool_out = depool[jnp.arange(bsz)[:, None], plug]
            return depool_out + h
        h = rmsnorm(embeds, g_res)
        h = jnp.einsum('bld,ed->ble', h, W_in) + b_in
        h_patch = rmsnorm(patch_embeds, g_init)
        return _hnet_depool(h, h_patch, patch_lens)

    def _L0_ffn_ref(x, gate_w, w1, w3, w2):
        import jax, jax.numpy as jnp
        import numpy as np
        TOP_K = 2
        logits = jnp.einsum('btd,de->bte', x, gate_w)
        probs = jax.nn.softmax(logits, axis=-1)
        expert_weights, expert_indices = jax.lax.top_k(probs, TOP_K)
        expert_weights = expert_weights / expert_weights.sum(-1, keepdims=True)
        E = w1.shape[0]
        out = jnp.zeros_like(x)
        for i in range(E):
            wi = jnp.where(expert_indices == i, expert_weights, 0.0).sum(-1)
            h = jax.nn.silu(jnp.einsum('btd,df->btf', x, w1[i])) * jnp.einsum('btd,df->btf', x, w3[i])
            out = out + jnp.einsum('btf,fd->btd', h, w2[i]) * wi[..., None]
        return out
    x = x + _L0_xattn_ref(_layernorm(x, axis=-1), ctx_2048, mask_BxS2_if0, L0_xattn_W_in, L0_xattn_b_in, L0_xattn_g_res, L0_xattn_g_init)
    x = x + _L0_ffn_ref(_layernorm(x, axis=-1), L0_ffn_gate_w, L0_ffn_w1, L0_ffn_w3, L0_ffn_w2)
    return x

_drawn_inputs = setup_inputs


def setup_inputs(seed=0):
    import zlib

    import numpy as np

    out = dict(_drawn_inputs(seed))
    spreads = {'L0_xattn_b_in': (0.0, 0.1), 'L0_xattn_g_res': (1.0, 0.2), 'L0_xattn_g_init': (1.0, 0.2)}
    factors = {'L0_ffn_gate_w': 3.916, 'L0_ffn_w1': 3.502, 'L0_ffn_w3': 3.44, 'L0_ffn_w2': 3.447}
    for name, (base, spread) in spreads.items():
        noise = np.random.default_rng([zlib.crc32(name.encode()), seed]).standard_normal(out[name].shape)
        drawn = base * np.exp(spread * noise) if base else spread * noise
        out[name] = jnp.asarray(drawn.astype(out[name].dtype))
    for name, factor in factors.items():
        out[name] = (out[name] * factor).astype(out[name].dtype)
    return out
```

```python
import math
from contextlib import ExitStack

import numpy as np
import concourse.bass as bass
from concourse import mybir

P = 128
B, S, D = 4, 512, 256
S2, CD = 1601, 512
E, F = 8, 1024
T = B * S
TPB = S // P
PAIRS = TPB // 2
KD, KF = D // P, F // P
HALF = F // 2

EPS_LN, EPS_RMS, EPS_LOGP = 1e-5, 1e-5, 1e-3

REGION = T + P
ROW_W = D
ROW_ID = D + E
ROW = D + E + 1
PAD_ROW = E * REGION

STEPS = (2 * T + E * (P - 1) + E - 1) // P
assert STEPS == 39
TABLE = STEPS + 2
C_EXPERT, C_ROW, C_W1, C_W3, C_LOAD, C_LATER, C_NEED, COLS = range(8)
OUT_INIT = 16

CH = -(-S2 // P)
FULL = S2 // CH
RAW_SEM = 48


def build(nc, x, ctx, lens, w_in, b_in, g_res, g_init, gate_w, w1, w3, w2, out):
    f32, f32r, bf16 = mybir.dt.float32, mybir.dt.float32r, mybir.dt.bfloat16
    i32, u8, u32 = mybir.dt.int32, mybir.dt.uint8, mybir.dt.uint32
    ALU, ACT, AX = mybir.AluOpType, mybir.ActivationFunctionType, mybir.AxisListType
    ds = bass.ds

    logp = np.float32(-EPS_LOGP)
    dt = np.float32(-np.log(-np.expm1(logp)))
    a, c = float(np.exp(-dt)), float(np.exp(logp))
    decay = [c * a ** k for k in range(P) if c * a ** k >= float(np.finfo(np.float32).tiny)]

    stack = ExitStack()
    with stack:
        def sb(name, shape, dtype, on=stack):
            return on.enter_context(nc.sbuf_tensor(name, shape, dtype))

        def sem(name):
            return stack.enter_context(nc.semaphore(name))

        xs = nc.dram_tensor("expert_rows", (PAD_ROW + P, ROW), f32, kind="Internal").ap()
        depool_dram = [nc.dram_tensor(f"depool_rows{b}", (S, D), f32, kind="Internal").ap() for b in range(B)]

        ident = sb("ident", [P, P], f32)
        tri = sb("tri", [P, P], f32)
        ones = sb("ones", [P, P], f32)
        decayT = sb("decayT", [P, 2 * P], f32)
        iota_i = sb("iota_i", [P, P], i32)
        iota_f = sb("iota_f", [P, P], f32)
        ids_i = sb("ids_i", [P, T // P + 1], i32)
        ids_f = sb("ids_f", [P, T // P + 1], f32)
        neg_half = sb("neg_half", [P, 2 * TPB], f32)
        win = sb("win", [P, KD, D], f32)
        gres = sb("gres", [P, KD], f32)
        gate = sb("gate", [P, KD, E], f32)
        ginit = sb("ginit", [P, D], f32)
        bin_ = sb("bin", [P, D], f32)
        padrow = sb("padrow", [P, ROW], f32)

        UP = 2 * KD * F
        RAW = UP + KF * D
        raw = sb("raw", [P, 2, RAW], f32)
        raw_up = raw[:, :, 0:UP].rearrange("p s (m k f) -> p s m k f", m=2, k=KD)
        raw_dn = raw[:, :, UP:RAW].rearrange("p s (k d) -> p s k d", k=KF)

        scratch = raw[:, 1, :].rearrange("p (n j d) -> p n j d", j=TPB, d=D)
        hn, hnT, zT, dep, hp = scratch[:, 0], [scratch[:, 1], scratch[:, 2]], scratch[:, 3], scratch[:, 4], scratch[:, 5]

        with ExitStack() as early:
            sb("first_slot", [P, 2, RAW], f32, early)
            x_all = sb("x_all", [P, B * TPB, D], f32, early)
            ctx_sb = sb("ctx_sb", [P, 2, TPB, CD], f32, early)
            payload = sb("payload", [P, 2, TPB, ROW], f32, early)
            onehot_lo = sb("onehot_lo", [P, 2, CH, P], bf16, early)
        split = sb("split", [P, 2, 2, RAW], f32r)
        up_hi, up_lo = (split[:, :, n, 0:UP].rearrange("p s (m k f) -> p s m k f", m=2, k=KD) for n in range(2))
        dn_hi, dn_lo = (split[:, :, n, UP:RAW].rearrange("p s (k d) -> p s k d", k=KF) for n in range(2))

        regions = sb("regions", [P, E], f32)
        iota_m8 = sb("iota_m8", [P, TPB], f32)
        sumsq = sb("sumsq", [P, 2, TPB], f32)
        st1 = sb("st1", [P, TPB, 6], f32)
        mv1 = sb("mv1", [P, TPB, 2], f32)
        vin = sb("vin", [P, 2 * TPB], f32)
        rs = sb("rs", [P, 2, 2 * TPB], f32)
        nb1 = sb("nb1", [P, TPB], f32)
        st2 = sb("st2", [P, TPB, 6], f32)
        mv2 = sb("mv2", [P, TPB, 2], f32)
        vin2 = sb("vin2", [P, TPB], f32)
        rs2 = sb("rs2", [P, TPB], f32)
        nb2 = sb("nb2", [P, TPB], f32)
        logits = sb("logits", [P, TPB, E], f32)
        top = sb("top", [P, TPB, 8], f32)
        topi = sb("topi", [P, TPB, 8], u32)
        topf = sb("topf", [P, 2, TPB], f32)
        oh = sb("oh", [P, 2, TPB, E], f32)
        ohw = sb("ohw", [P, 2, TPB, E], f32)
        picked = sb("picked", [P, TPB, E], f32)
        gap = sb("gap", [P, TPB], f32)
        egap = sb("egap", [P, TPB], f32)
        den = sb("den", [P, TPB], f32)
        wts = sb("wts", [P, 2, TPB], f32)
        base = sb("base", [P, E], f32)
        posf = sb("posf", [P, TPB, E], f32)
        posm = sb("posm", [P, 2, TPB, E], f32)
        poss = sb("poss", [P, 2, TPB], f32)
        posi = sb("posi", [P, 2, 2, TPB], i32)
        padi = sb("padi", [P, E], i32)
        dg = sb("dg", [P, 2, TPB, D], f32)

        NBC = B * CH
        ln_i = sb("ln_i", [P, B, CH], i32)
        ln_f = sb("ln_f", [P, 4, B, CH], f32)
        keep = sb("keep", [P, 4 * NBC], f32)
        ln_s = sb("ln_s", [P, 4, B, CH], f32)
        ln_c = sb("ln_c", [P, 4, NBC], i32)
        ln_t = sb("ln_t", [P, NBC], i32)
        ln_b = sb("ln_b", [P, 4, NBC], i32)
        ln_v = sb("ln_v", [P, 8, NBC], f32)
        ln_p = sb("ln_p", [P, 3, NBC], i32)
        onehot_hi = sb("onehot_hi", [P, NBC, TPB], bf16)
        bmask = sb("bmask", [P, B, TPB], f32)
        plugf = sb("plugf", [P, B, TPB], f32)
        plugi = sb("plugi", [P, B * TPB], i32)

        n_i = sb("n_i", [1, E], i32)
        nblk = sb("nblk", [1, E], f32)
        cum = sb("cum", [1, E], f32)
        stepm = sb("stepm", [1, TABLE, E], f32)
        stepv = sb("stepv", [1, 12, TABLE], f32)
        table = sb("table", [1, TABLE, COLS], i32)
        wtok = sb("wtok", [P, 2], f32)
        itok = sb("itok", [P, 2], i32)

        xblk = sb("xblk", [P, 2, ROW], f32)
        xT_hi = sb("xT_hi", [P, 2, KD, P], f32r)
        xT_lo = sb("xT_lo", [P, 2, KD, P], f32r)
        gact = sb("gact", [P, F], f32)
        hmul = sb("hmul", [P, F], f32)
        hT_hi = sb("hT_hi", [P, 2, KF, P], f32r)
        hT_lo = sb("hT_lo", [P, 2, KF, P], f32r)
        yblk = sb("yblk", [P, 2, D], f32)

        bank = [stack.enter_context(nc.psum_tensor(f"bank{n}", [P, HALF], f32)) for n in range(8)]
        pT, pH, pD = bank[0:2], bank[2:4], bank[4:6]
        p_logit = bank[6][:, 0:TPB * E]
        p_rank = bank[6][:, 64:64 + TPB * E]
        p_total = bank[6][:, 128:128 + E]
        p_prefix = bank[7][:, 0:4 * B]
        p_count = bank[7][:, 64:64 + B * TPB]
        p_plug = bank[7][:, 128:128 + B * TPB]
        p_win = bank[4]
        p_gate, p_lin = [bank[0], bank[2]], [bank[1], bank[3]]
        p_hT = bank[4:6]
        p_xT = bank[6][:, 0:D]
        p_y = bank[7][:, 0:D]

        names = """lens_in small_in consts keep_ready bytes_ready iota_ready wT_ready scan_ready prefix_ready
            carry_step onehot_ready count_ready bmask_ready plugmm_ready plug_ready gw_ready pad_ready
            ids_ready base_step sq_ready st1_ready mv1_ready vin_ready rs_ready nb1_ready
            hn_ready tn_ready hnT_ready hp_ready depmm_ready dep_ready hmm_ready xd_ready x1_ready
            st2_ready mv2_ready vin2_ready rs2_ready nb2_ready z_ready tz_ready zT_ready logit_mm
            logit_ready top_ready topi_ready topf_ready gap_ready egap_ready den_ready w1st_ready
            wts_ready oh_ready picked_ready wi_step wi_ready rank_mm posf_ready posm_ready poss_ready
            posi_ready padf_ready padi_ready pad_rows tbl_step table_ready
            raw_first raw_ready uphi_ready uplo_ready dnhi_ready dn_ready x1_rows added_rows
            up0_done up1_done pad_step silu0_done silu1_done h0_done h1_done th0_done th1_done
            hT0hi_ready hT0lo_ready hT1hi_ready hT1lo_ready xT_done xThi_ready xTlo_ready
            meta_ready y_done y_ready affine_step
            settled_pool settled_sp""".split()
        s = {n: sem(n) for n in names}
        x_in = [sem(f"x_in{b}") for b in range(B)]
        ctx_in = [sem(f"ctx_in{b}") for b in range(B)]
        dep_rows = [sem(f"dep_rows{b}") for b in range(B)]
        dg_in = [sem(f"dg_in{b}") for b in range(B)]
        xs_rows = [sem(f"xs_rows{b}") for b in range(B)]
        blk_in = [sem(f"blk_in{q}") for q in range(2)]

        block = stack.enter_context(nc.Block())

        def pair(t, n):
            return t[:, 2 * n:2 * n + 2, :].rearrange("p j d -> p (j d)")

        def raw_load(eng, e, slot, signal):
            for m, w in enumerate((w1, w3)):
                eng.dma_start(raw_up[:, ds(slot, 1), m], w[ds(e, 1)].rearrange("o (k p) f -> p (o k) f", p=P))\
                   .then_inc(signal, 16)
            eng.dma_start(raw_dn[:, ds(slot, 1)], w2[ds(e, 1)].rearrange("o (k p) d -> p (o k) d", p=P))\
               .then_inc(signal, 16)

        def step_value(eng, i, col, low, high):
            return eng.value_load(table[0:1, ds(i, 1), col:col + 1].rearrange("a b c -> a (b c)"), min_val=low, max_val=high)

        def settle(eng):
            eng.sem_inc(s[f"settled_{'pool' if eng is nc.gpsimd else 'sp'}"], 1)

        def over_steps(eng, body):
            body(0, 0, 0)
            with eng.Fori(0, (STEPS - 1) // 2) as pair:
                body(pair * 2 + 1, 1, pair)
                body(pair * 2 + 2, 0, pair + 1)

        def split_down(pool, e):
            slot = ds(e & 1, 1)
            pool.tensor_copy(dn_hi[:, slot], raw_dn[:, slot]).then_inc(s["dnhi_ready"], 1)
            pool.wait_ge(s["dnhi_ready"], e + 1)
            pool.tensor_tensor(dn_lo[:, slot], raw_dn[:, slot], dn_hi[:, slot].bitcast(f32), ALU.subtract)\
                .then_inc(s["dn_ready"], 1)

        def split_up_hi(act, e, m):
            slot = ds(e & 1, 1)
            act.activation(up_hi[:, slot, m], raw_up[:, slot, m], ACT.Copy).then_inc(s["uphi_ready"], 1)

        def split_up_lo(dve, e, m):
            slot = ds(e & 1, 1)
            dve.wait_ge(s["uphi_ready"], 2 * e + m + 1)
            dve.tensor_tensor(up_lo[:, slot, m], raw_up[:, slot, m], up_hi[:, slot, m].bitcast(f32), ALU.subtract)\
               .then_inc(s["uplo_ready"], 1)

        @block.sync
        def _(sp):
            sp.wait_ge(s["keep_ready"], 1)
            sp.dma_start(ln_i[0:FULL, :, :], lens[:, 0:FULL * CH].rearrange("b (p c) -> p b c", c=CH))\
              .then_inc(s["lens_in"], 16)
            sp.dma_start(ln_i[FULL:FULL + 1, :, 0:S2 - FULL * CH],
                         lens[:, FULL * CH:S2].unsqueeze(0)).then_inc(s["lens_in"], 16)

            def load_batch(b):
                sp.dma_start(ctx_sb[:, b % 2], ctx[b, 0:S, :].rearrange("(j p) d -> p j d", p=P))\
                  .then_inc(ctx_in[b], 16)
                sp.dma_start(x_all[:, b * TPB:(b + 1) * TPB, :], x[b].rearrange("(j p) d -> p j d", p=P))\
                  .then_inc(x_in[b], 16)

            load_batch(0)
            sp.dma_start(win[:, :, :], w_in.rearrange("(k p) n -> p k n", p=P)).then_inc(s["small_in"], 16)
            sp.dma_start(ginit[:, :], g_init[0:D].unsqueeze(0).broadcast_to([P, D])).then_inc(s["small_in"], 16)
            sp.dma_start(bin_[:, :], b_in.unsqueeze(0).broadcast_to([P, D])).then_inc(s["small_in"], 16)
            with nc.allow_non_contiguous_dma(reason="256 elements"):
                sp.dma_start(gres[:, :], g_res.rearrange("(k p) -> p k", p=P)).then_inc(s["small_in"], 16)
            sp.dma_start(gate[:, :, :], gate_w.rearrange("(k p) n -> p k n", p=P)).then_inc(s["small_in"], 16)
            load_batch(1)
            raw_load(sp, 0, 0, s["raw_first"])

            for b in range(B):
                sp.wait_ge(s["dep_ready"], PAIRS * (b + 1))
                sp.dma_start(depool_dram[b].rearrange("(j p) d -> p j d", p=P), dep)\
                  .then_inc(dep_rows[b], 16)
                if b + 2 < B:
                    sp.wait_ge(s["hp_ready"], TPB * (b + 1))
                    sp.wait_ge(s["sq_ready"], TPB * (b + 1))
                    load_batch(b + 2)
            for b in range(B):
                sp.wait_ge(s["x1_ready"], PAIRS * (b + 1))
                sp.dma_start(out[b * S:(b + 1) * S, :].rearrange("(j p) d -> p j d", p=P),
                             x_all[:, b * TPB:(b + 1) * TPB, :]).then_inc(s["x1_rows"], 16)
                if b == 1:
                    sp.wait_ge(s["uplo_ready"], 2)
                    sp.wait_ge(s["dn_ready"], 1)
                    raw_load(sp, 2, 0, s["raw_ready"])

            sp.wait_ge(s["x1_rows"], 16 * B)
            sp.wait_ge(s["z_ready"], B * TPB)
            sp.wait_ge(s["table_ready"], 1)
            for b in range(B):
                sp.wait_ge(xs_rows[b], 2 * TPB * 16)
            sp.wait_ge(s["pad_rows"], 16 * (E + 1))

            def load_rows(i, q):
                row = step_value(sp, i, C_ROW, 0, PAD_ROW)
                sp.dma_start(xblk[:, q], xs[ds(row, P), :]).then_inc(blk_in[q], 16)

            load_rows(0, 0)
            load_rows(1, 1)
            sp.wait_ge(s["logit_mm"], B)
            sp.wait_ge(s["raw_ready"], RAW_SEM)
            raw_load(sp, 1, 1, s["raw_ready"])

            def step(i, q, half):
                sp.wait_ge(s["xT_done"], i + 1)
                sp.wait_ge(s["meta_ready"], i + 1)
                load_rows(i + 2, q)
                load = step_value(sp, i, C_LOAD, 0, 1)
                e = step_value(sp, i, C_LATER, 0, E - 4)
                with sp.If(load):
                    sp.wait_ge(s["uplo_ready"], 2 * e + 4)
                    settle(sp)
                    sp.wait_ge(s["dn_ready"], e + 2)
                    settle(sp)
                    sp.wait_ge(s["raw_ready"], RAW_SEM * (e + 2))
                    settle(sp)
                    raw_load(sp, e + 3, (e + 1) & 1, s["raw_ready"])

            over_steps(sp, step)
            sp.wait_ge(blk_in[0], 16 * ((TABLE + 1) // 2))
            sp.wait_ge(blk_in[1], 16 * (TABLE // 2))

        @block.gpsimd
        def _(pool):
            pool.memset(ident[:, :], 0.0).then_inc(s["affine_step"], 1)
            pool.memset(ones[:, :], 1.0).then_inc(s["affine_step"], 1)
            pool.memset(decayT[:, :], 0.0).then_inc(s["affine_step"], 1)
            pool.iota(iota_i[:, :], pattern=[[1, P]], base=0, channel_multiplier=0).then_inc(s["affine_step"], 1)
            pool.iota(ids_i[:, :], pattern=[[P, T // P + 1]], base=0, channel_multiplier=1)\
                .then_inc(s["affine_step"], 1)
            pool.memset(neg_half[:, :], -0.5).then_inc(s["affine_step"], 1)
            pool.wait_ge(s["affine_step"], 6)
            pool.affine_select(out=ident[:, :], in_=ident[:, :], compare_op=ALU.not_equal, fill=1.0,
                               base=0, pattern=[[-1, P]], channel_multiplier=1).then_inc(s["consts"], 1)
            pool.affine_select(out=tri[:, :], in_=ones[:, :], compare_op=ALU.is_gt, fill=0.0,
                               base=0, pattern=[[1, P]], channel_multiplier=-1).then_inc(s["consts"], 1)
            for k, v in enumerate(decay):
                if k:
                    pool.wait_ge(s["affine_step"], 6 + k)
                pool.affine_select(out=decayT[:, :], in_=decayT[:, :], compare_op=ALU.not_equal, fill=v,
                                   base=-k, pattern=[[1, 2 * P]], channel_multiplier=-1)\
                    .then_inc(s["affine_step"], 1)

            pool.wait_ge(s["pad_ready"], 1)
            pool.dma_start(xs[PAD_ROW:PAD_ROW + P, :], padrow[:, :]).then_inc(s["pad_rows"], 16)
            pool.dma_start(out[T:T + P, :], padrow[:, 0:D]).then_inc(s["added_rows"], 16)

            def pow1(b):
                pool.wait_ge(s["vin_ready"], 2 * (b + 1))
                pool.tensor_tensor(rs[:, b % 2], vin[:, :], neg_half[:, :], ALU.pow).then_inc(s["rs_ready"], 1)

            def gather(b):
                pool.wait_ge(s["plug_ready"], 1)
                pool.wait_ge(dep_rows[b], 16)
                if b >= 2:
                    pool.wait_ge(s["xd_ready"], b - 1)
                for j in range(TPB):
                    n = b * TPB + j
                    pool.indirect_dma_start(dg[:, b % 2, j, :], None, depool_dram[b][:, :],
                                            bass.IndirectOffsetOnAxis(ap=plugi[:, n:n + 1], axis=0))\
                        .then_inc(dg_in[b], 16)

            def pow2(b):
                pool.wait_ge(s["vin2_ready"], b + 1)
                pool.tensor_tensor(rs2[:, :], vin2[:, :], neg_half[:, 0:TPB], ALU.pow)\
                    .then_inc(s["rs2_ready"], 1)

            def scatter(b):
                pool.wait_ge(s["z_ready"], TPB * (b + 1))
                pool.wait_ge(s["wi_ready"], b + 1)
                pool.wait_ge(s["posi_ready"], b + 1)
                for j in range(TPB):
                    for r in range(2):
                        pool.indirect_dma_start(xs[:, :], bass.IndirectOffsetOnAxis(
                            ap=posi[:, b % 2, r, j:j + 1], axis=0), payload[:, b % 2, j, :], None)\
                            .then_inc(xs_rows[b], 16)

            pow1(0)
            for b in range(B):
                if b + 1 < B:
                    pow1(b + 1)
                gather(b)
                pow2(b)
                scatter(b)
                if b == 0:
                    pool.wait_ge(s["raw_first"], RAW_SEM)
                    split_down(pool, 0)
            pool.wait_ge(s["padi_ready"], 1)
            for e in range(E):
                pool.indirect_dma_start(xs[:, :], bass.IndirectOffsetOnAxis(ap=padi[:, e:e + 1], axis=0),
                                        padrow[:, :], None).then_inc(s["pad_rows"], 16)

            def add_rows(i, q):
                pool.wait_ge(s["y_ready"], i + 1)
                pool.wait_ge(s["added_rows"], OUT_INIT + 16 * i)
                settle(pool)
                pool.indirect_dma_start(out[:, :], bass.IndirectOffsetOnAxis(ap=itok[:, q:q + 1], axis=0),
                                        yblk[:, q, :], None, compute_op=ALU.add).then_inc(s["added_rows"], 16)

            def step(i, q, half):
                if not isinstance(i, int) or i > 0:
                    add_rows(i - 1, 1 - q)
                split = step_value(pool, i, C_W1, 0, 1)
                e = step_value(pool, i, C_EXPERT, 0, E - 1)
                need = step_value(pool, i, C_NEED, RAW_SEM, RAW_SEM * E)
                with pool.If(split):
                    pool.wait_ge(s["raw_ready"], need)
                    split_down(pool, e + 1)

            pool.wait_ge(s["table_ready"], 1)
            pool.wait_ge(s["x1_rows"], 16 * B)
            over_steps(pool, step)
            add_rows(STEPS - 1, (STEPS - 1) % 2)
            pool.wait_ge(s["added_rows"], OUT_INIT + 16 * STEPS)

        @block.scalar
        def _(act):
            def norm_first(b):
                act.wait_ge(ctx_in[b], 16)
                if b >= 1:
                    act.wait_ge(s["depmm_ready"], TPB * b)
                for j in range(TPB):
                    act.activation(hp[:, j, :].bitcast(bf16), ctx_sb[:, b % 2, j, :], ACT.Square,
                                   accum_out=sumsq[:, b % 2, j:j + 1]).then_inc(s["sq_ready"], 1)
                act.wait_ge(s["nb1_ready"], b + 1)
                for j in range(TPB):
                    if b >= 1:
                        act.wait_ge(s["tn_ready"], TPB * b)
                    act.activation(hn[:, j, :], x_all[:, b * TPB + j, :], ACT.Identity,
                                   scale=rs[:, b % 2, TPB + j:TPB + j + 1], bias=nb1[:, j:j + 1])\
                       .then_inc(s["hn_ready"], 1)
                for n in range(PAIRS):
                    act.wait_ge(s["tn_ready"], b * TPB + 2 * n + 2)
                    act.activation(pair(hnT[b % 2], n), pT[n][:, :], ACT.Copy)\
                       .then_inc(s["hnT_ready"], 1)

            def norm_second(b):
                act.wait_ge(s["nb2_ready"], b + 1)
                if b >= 2:
                    act.wait_ge(xs_rows[b - 2], 2 * TPB * 16)
                for j in range(TPB):
                    act.activation(payload[:, b % 2, j, 0:D], x_all[:, b * TPB + j, :], ACT.Identity,
                                   scale=rs2[:, j:j + 1], bias=nb2[:, j:j + 1]).then_inc(s["z_ready"], 1)
                for n in range(PAIRS):
                    act.wait_ge(s["tz_ready"], b * TPB + 2 * n + 2)
                    act.activation(pair(zT, n), pT[n][:, :], ACT.Copy)\
                       .then_inc(s["zT_ready"], 1)
                act.wait_ge(s["gap_ready"], b + 1)
                act.activation(egap[:, :], gap[:, :], ACT.Exp).then_inc(s["egap_ready"], 1)

            norm_first(0)
            for b in range(B):
                if b + 1 < B:
                    norm_first(b + 1)
                norm_second(b)
                if b == 0:
                    act.wait_ge(s["raw_first"], RAW_SEM)
                    split_up_hi(act, 0, 0)
                    split_up_hi(act, 0, 1)

            act.wait_ge(s["table_ready"], 1)
            act.wait_ge(s["x1_rows"], 16 * B)

            def xT(i, q):
                act.wait_ge(s["xT_done"], i + 1)
                act.activation(xT_hi[:, q], p_xT, ACT.Copy).then_inc(s["xThi_ready"], 1)

            def hT(i, q, half):
                act.wait_ge(s[f"th{half}_done"], i + 1)
                act.activation(hT_hi[:, q, half * KF // 2:(half + 1) * KF // 2], p_hT[half][:, :], ACT.Copy)\
                   .then_inc(s[f"hT{half}hi_ready"], 1)

            def silu(i, half):
                act.wait_ge(s[f"up{half}_done"], i + 1)
                act.activation(gact[:, half * HALF:(half + 1) * HALF], p_gate[half][:, :], ACT.Silu)\
                   .then_inc(s[f"silu{half}_done"], 1)

            def y(i, q):
                act.wait_ge(s["y_done"], i + 1)
                act.wait_ge(s["added_rows"], OUT_INIT + 16 * (i - 1) if not isinstance(i, int) or i > 0 else OUT_INIT)
                act.wait_ge(s["meta_ready"], i + 1)
                act.activation(yblk[:, q, :], p_y, ACT.Copy, scale=wtok[:, q:q + 1]).then_inc(s["y_ready"], 1)

            def step(i, q, half):
                later = not isinstance(i, int) or i > 0
                silu(i, 0)
                if later:
                    hT(i - 1, 1 - q, 1)
                xT(i + 1, 1 - q)
                silu(i, 1)
                hT(i, q, 0)
                if later:
                    y(i - 1, 1 - q)
                e = step_value(act, i, C_EXPERT, 0, E - 1)
                need = step_value(act, i, C_NEED, RAW_SEM, RAW_SEM * E)
                for m, col in enumerate((C_W1, C_W3)):
                    split = step_value(act, i, col, 0, 1)
                    with act.If(split):
                        act.wait_ge(s["raw_ready"], need)
                        split_up_hi(act, e + 1, m)

            xT(0, 0)
            over_steps(act, step)
            hT(STEPS - 1, (STEPS - 1) % 2, 1)
            y(STEPS - 1, (STEPS - 1) % 2)

        @block.vector
        def _(dve):
            dve.memset(ln_i[:, :, :], 0).then_inc(s["keep_ready"], 1)
            dve.memset(keep[:, :], 1.0).then_inc(s["keep_ready"], 1)
            dve.wait_ge(s["keep_ready"], 2)
            dve.memset(keep[:, :].rearrange("p (n c) -> p n c", c=CH)[:, :, 0:1], 0.0).then_inc(s["keep_ready"], 1)
            dve.memset(padrow[:, :], 0.0).then_inc(s["pad_step"], 1)
            dve.wait_ge(s["affine_step"], 5)
            dve.tensor_copy(iota_f[:, :], iota_i[:, :]).then_inc(s["iota_ready"], 1)
            dve.tensor_copy(ids_f[:, :], ids_i[:, :]).then_inc(s["ids_ready"], 1)
            dve.wait_ge(s["iota_ready"], 1)
            dve.wait_ge(s["ids_ready"], 1)
            dve.wait_ge(s["pad_step"], 1)
            dve.tensor_copy(padrow[:, ROW_ID:ROW_ID + 1], ids_f[:, T // P:T // P + 1]).then_inc(s["pad_ready"], 1)
            dve.tensor_scalar(iota_m8[:, :], iota_f[:, 0:TPB], -8.0, None, ALU.add).then_inc(s["iota_ready"], 1)
            dve.tensor_scalar(regions[:, :], iota_f[:, 0:E], float(REGION), None, ALU.mult).then_inc(s["base_step"], 1)
            dve.tensor_scalar(base[:, :], iota_f[:, 0:E], float(REGION), None, ALU.mult).then_inc(s["base_step"], 1)

            def lengths():
                dve.wait_ge(s["lens_in"], 32)
                dve.wait_ge(s["keep_ready"], 3)
                dve.tensor_copy(ln_f[:, :, :, :], ln_i[:, :, :].bitcast(u8).rearrange("p b (c k) -> p k b c", k=4))\
                   .then_inc(s["bytes_ready"], 1)
                dve.wait_ge(s["bytes_ready"], 1)
                dve.tensor_tensor_scan(ln_s[:, :, :, :].rearrange("p k b c -> p (k b c)"), keep[:, :],
                                       ln_f[:, :, :, :].rearrange("p k b c -> p (k b c)"), 0.0, ALU.mult, ALU.add)\
                   .then_inc(s["scan_ready"], 1)
                dve.wait_ge(s["prefix_ready"], 1)
                dve.tensor_tensor(ln_c[:, :, :].rearrange("p k (b c) -> p (k b) c", c=CH),
                                  ln_s[:, :, :, :].rearrange("p k b c -> p (k b) c"),
                                  p_prefix.unsqueeze(2).broadcast_to([P, 4 * B, CH]), ALU.add)\
                   .then_inc(s["carry_step"], 1)
                n = 1
                for k in range(4):
                    dve.wait_ge(s["carry_step"], n)
                    dve.tensor_scalar(ln_b[:, k, :], ln_c[:, k, :], 255, None, ALU.bitwise_and)\
                       .then_inc(s["carry_step"], 1)
                    n += 1
                    if k < 3:
                        dve.tensor_scalar(ln_t[:, :], ln_c[:, k, :], 8, None, ALU.logical_shift_right)\
                           .then_inc(s["carry_step"], 1)
                        dve.wait_ge(s["carry_step"], n + 1)
                        dve.tensor_tensor(ln_c[:, k + 1, :], ln_c[:, k + 1, :], ln_t[:, :], ALU.add)\
                           .then_inc(s["carry_step"], 1)
                        n += 2
                low, high, lowok, lowneg, ok0, ok1, ok, hif = (ln_v[:, n_, :] for n_ in range(8))
                idx, lo_i, hi_i = (ln_p[:, n_, :] for n_ in range(3))
                dve.wait_ge(s["carry_step"], n)
                dve.scalar_tensor_tensor(low, ln_b[:, 1, :], 256.0, ln_b[:, 0, :], ALU.mult, ALU.add)\
                   .then_inc(s["carry_step"], 1)
                dve.scalar_tensor_tensor(high, ln_b[:, 3, :], 256.0, ln_b[:, 2, :], ALU.mult, ALU.add)\
                   .then_inc(s["carry_step"], 1)
                dve.wait_ge(s["carry_step"], n + 2)
                dve.tensor_scalar(lowok, low, float(S), None, ALU.is_le).then_inc(s["carry_step"], 1)
                dve.tensor_scalar(lowneg, low, float(65536 + 1 - S), None, ALU.is_ge).then_inc(s["carry_step"], 1)
                dve.tensor_scalar(idx, low, float(S - 1), None, ALU.add).then_inc(s["carry_step"], 1)
                dve.wait_ge(s["carry_step"], n + 5)
                dve.scalar_tensor_tensor(ok0, high, 0.0, lowok, ALU.is_equal, ALU.mult).then_inc(s["carry_step"], 1)
                dve.scalar_tensor_tensor(ok1, high, 65535.0, lowneg, ALU.is_equal, ALU.mult)\
                   .then_inc(s["carry_step"], 1)
                dve.tensor_scalar(lo_i, idx, P - 1, None, ALU.bitwise_and).then_inc(s["carry_step"], 1)
                dve.tensor_scalar(hi_i, idx, 7, TPB - 1, ALU.logical_shift_right, ALU.bitwise_and)\
                   .then_inc(s["carry_step"], 1)
                dve.wait_ge(s["carry_step"], n + 9)
                dve.tensor_tensor(ok, ok0, ok1, ALU.add).then_inc(s["carry_step"], 1)
                dve.tensor_copy(low, lo_i).then_inc(s["carry_step"], 1)
                dve.wait_ge(s["carry_step"], n + 11)
                dve.scalar_tensor_tensor(hif, ok, -8.0, hi_i, ALU.mult, ALU.add).then_inc(s["carry_step"], 1)
                dve.wait_ge(s["carry_step"], n + 12)
                dve.wait_ge(s["iota_ready"], 2)
                dve.tensor_tensor(onehot_hi[:, :, :], iota_m8[:, :].unsqueeze(1).broadcast_to([P, NBC, TPB]),
                                  hif.unsqueeze(2).broadcast_to([P, NBC, TPB]), ALU.is_equal)\
                   .then_inc(s["onehot_ready"], 1)
                for b in range(B):
                    if b >= 2:
                        dve.wait_ge(s["count_ready"], b - 1)
                    dve.tensor_tensor(onehot_lo[:, b % 2], iota_f[:, :].unsqueeze(1).broadcast_to([P, CH, P]),
                                      low[:, b * CH:(b + 1) * CH].unsqueeze(2).broadcast_to([P, CH, P]),
                                      ALU.is_equal).then_inc(s["onehot_ready"], 1)
                dve.wait_ge(s["count_ready"], B)
                dve.tensor_scalar(bmask[:, :, :].rearrange("p b j -> p (b j)"), p_count, 0.5, None, ALU.is_gt)\
                   .then_inc(s["bmask_ready"], 1)
                dve.wait_ge(s["plugmm_ready"], 1)
                dve.tensor_scalar(plugf[:, :, :].rearrange("p b j -> p (b j)"), p_plug, -1.0, 0.0, ALU.add, ALU.max)\
                   .then_inc(s["bmask_ready"], 1)
                dve.wait_ge(s["bmask_ready"], 2)
                dve.tensor_scalar(plugi[:, :], plugf[:, :, :].rearrange("p b j -> p (b j)"), float(S2 - 1), None,
                                  ALU.min).then_inc(s["plug_ready"], 1)

            def first(b):
                dve.wait_ge(x_in[b], 16)
                for j in range(TPB):
                    dve.bn_stats(st1[:, j, :], x_all[:, b * TPB + j, :]).then_inc(s["st1_ready"], 1)
                dve.wait_ge(s["st1_ready"], TPB * (b + 1))
                for j in range(TPB):
                    dve.bn_aggr(mv1[:, j, :], st1[:, j, :]).then_inc(s["mv1_ready"], 1)
                dve.wait_ge(s["sq_ready"], TPB * (b + 1))
                if b >= 1:
                    dve.wait_ge(s["rs_ready"], b)
                dve.tensor_scalar(vin[:, 0:TPB], sumsq[:, b % 2, :], 1.0 / CD, EPS_RMS, ALU.mult, ALU.add)\
                   .then_inc(s["vin_ready"], 1)
                dve.wait_ge(s["mv1_ready"], TPB * (b + 1))
                dve.tensor_scalar(vin[:, TPB:2 * TPB], mv1[:, :, 1], 1.0 + EPS_RMS, EPS_LN * EPS_RMS,
                                  ALU.mult, ALU.add).then_inc(s["vin_ready"], 1)
                dve.wait_ge(s["rs_ready"], b + 1)
                if b >= 1:
                    dve.wait_ge(s["hn_ready"], TPB * b)
                dve.scalar_tensor_tensor(nb1[:, :], mv1[:, :, 0], -1.0, rs[:, b % 2, TPB:2 * TPB],
                                         ALU.mult, ALU.mult).then_inc(s["nb1_ready"], 1)
                dve.wait_ge(ctx_in[b], 16)
                dve.wait_ge(s["small_in"], 16 * 5)
                if b >= 1:
                    dve.wait_ge(s["depmm_ready"], TPB * b)
                for j in range(TPB):
                    dve.scalar_tensor_tensor(hp[:, j, :], ctx_sb[:, b % 2, j, 0:D], rs[:, b % 2, j:j + 1],
                                             ginit[:, :], ALU.mult, ALU.mult).then_inc(s["hp_ready"], 1)

            def depooled(b):
                if b >= 1:
                    dve.wait_ge(dep_rows[b - 1], 16)
                for n in range(PAIRS):
                    dve.wait_ge(s["depmm_ready"], b * TPB + 2 * n + 2)
                    dve.tensor_tensor(dep[:, 2 * n:2 * n + 2, :], pD[n][:, :].rearrange("p (j d) -> p j d", d=D),
                                      bin_[:, :].unsqueeze(1).broadcast_to([P, 2, D]), ALU.add)\
                       .then_inc(s["dep_ready"], 1)

            def second(b):
                dve.wait_ge(dg_in[b], 16 * TPB)
                dve.wait_ge(s["hn_ready"], TPB * (b + 1))
                flat = x_all[:, b * TPB:(b + 1) * TPB, :].rearrange("p j d -> p (j d)")
                dve.tensor_tensor(flat, flat, dg[:, b % 2].rearrange("p j d -> p (j d)"), ALU.add)\
                   .then_inc(s["xd_ready"], 1)
                dve.wait_ge(s["xd_ready"], b + 1)
                xb = x_all[:, b * TPB:(b + 1) * TPB, :]
                for n in range(PAIRS):
                    dve.wait_ge(s["hmm_ready"], b * TPB + 2 * n + 2)
                    dve.tensor_tensor(pair(xb, n), pair(xb, n), pH[n][:, :], ALU.add).then_inc(s["x1_ready"], 1)
                for j in range(TPB):
                    dve.wait_ge(s["x1_ready"], b * PAIRS + j // 2 + 1)
                    dve.bn_stats(st2[:, j, :], x_all[:, b * TPB + j, :]).then_inc(s["st2_ready"], 1)
                dve.wait_ge(s["st2_ready"], TPB * (b + 1))
                for j in range(TPB):
                    dve.bn_aggr(mv2[:, j, :], st2[:, j, :]).then_inc(s["mv2_ready"], 1)
                dve.wait_ge(s["mv2_ready"], TPB * (b + 1))
                if b >= 1:
                    dve.wait_ge(s["z_ready"], TPB * b)
                dve.tensor_scalar(vin2[:, :], mv2[:, :, 1], EPS_LN, None, ALU.add).then_inc(s["vin2_ready"], 1)
                dve.wait_ge(s["rs2_ready"], b + 1)
                dve.scalar_tensor_tensor(nb2[:, :], mv2[:, :, 0], -1.0, rs2[:, :], ALU.mult, ALU.mult)\
                   .then_inc(s["nb2_ready"], 1)

            def route(b):
                dve.wait_ge(s["logit_mm"], b + 1)
                dve.tensor_copy(logits[:, :, :].rearrange("p j e -> p (j e)"), p_logit).then_inc(s["logit_ready"], 1)
                dve.wait_ge(s["logit_ready"], b + 1)
                for j in range(TPB):
                    dve.max(top[:, j, :], logits[:, j, :]).then_inc(s["top_ready"], 1)
                dve.wait_ge(s["top_ready"], TPB * (b + 1))
                for j in range(TPB):
                    dve.max_index(topi[:, j, :], top[:, j, :], logits[:, j, :]).then_inc(s["topi_ready"], 1)
                dve.tensor_tensor(gap[:, :], top[:, :, 1], top[:, :, 0], ALU.subtract).then_inc(s["gap_ready"], 1)
                dve.wait_ge(s["topi_ready"], TPB * (b + 1))
                dve.tensor_copy(topf[:, :, :], topi[:, :, 0:2].rearrange("p j r -> p r j")).then_inc(s["topf_ready"], 1)
                dve.wait_ge(s["topf_ready"], b + 1)
                oh_v = oh[:, :, :, :].rearrange("p r j e -> p (r j) e")
                dve.tensor_tensor(oh_v, iota_f[:, 0:E].unsqueeze(1).broadcast_to([P, 2 * TPB, E]),
                                  topf[:, :, :].rearrange("p r j -> p (r j)").unsqueeze(2)
                                  .broadcast_to([P, 2 * TPB, E]), ALU.is_equal).then_inc(s["oh_ready"], 1)
                dve.wait_ge(s["oh_ready"], b + 1)
                dve.tensor_tensor(picked[:, :, :], oh[:, 0], oh[:, 1], ALU.add).then_inc(s["picked_ready"], 1)
                dve.wait_ge(s["egap_ready"], b + 1)
                dve.tensor_scalar(den[:, :], egap[:, :], 1.0, None, ALU.add).then_inc(s["den_ready"], 1)
                dve.wait_ge(s["den_ready"], b + 1)
                dve.reciprocal(wts[:, 0, :], den[:, :]).then_inc(s["wts_ready"], 1)
                dve.wait_ge(s["wts_ready"], 2 * b + 1)
                dve.tensor_tensor(wts[:, 1, :], egap[:, :], wts[:, 0, :], ALU.mult).then_inc(s["wts_ready"], 1)
                dve.wait_ge(s["wts_ready"], 2 * b + 2)
                dve.tensor_tensor(ohw[:, :, :, :].rearrange("p r j e -> p (r j) e"), oh_v,
                                  wts[:, :, :].rearrange("p r j -> p (r j)").unsqueeze(2)
                                  .broadcast_to([P, 2 * TPB, E]), ALU.mult).then_inc(s["wi_step"], 1)
                dve.wait_ge(s["wi_step"], b + 1)
                if b >= 2:
                    dve.wait_ge(xs_rows[b - 2], 2 * TPB * 16)
                dve.tensor_copy(payload[:, b % 2, :, ROW_ID], ids_f[:, b * TPB:(b + 1) * TPB])
                dve.tensor_tensor(payload[:, b % 2, :, ROW_W:ROW_W + E], ohw[:, 0], ohw[:, 1], ALU.add)\
                   .then_inc(s["wi_ready"], 1)
                dve.wait_ge(s["rank_mm"], b + 1)
                dve.wait_ge(s["base_step"], 2 + b)
                dve.tensor_tensor(posf[:, :, :], p_rank.rearrange("p (j e) -> p j e", e=E),
                                  base[:, :].unsqueeze(1).broadcast_to([P, TPB, E]), ALU.add)\
                   .then_inc(s["posf_ready"], 1)
                dve.wait_ge(s["posf_ready"], b + 1)
                dve.tensor_tensor(base[:, :], base[:, :], p_total, ALU.add).then_inc(s["base_step"], 1)
                for r in range(2):
                    dve.tensor_tensor(posm[:, r], oh[:, r], posf[:, :, :], ALU.mult).then_inc(s["posm_ready"], 1)
                dve.wait_ge(s["posm_ready"], 2 * (b + 1))
                dve.tensor_reduce(poss[:, :, :].rearrange("p r j -> p (r j)"),
                                  posm[:, :, :, :].rearrange("p r j e -> p (r j) e"), AX.X, ALU.add)\
                   .then_inc(s["poss_ready"], 1)
                dve.wait_ge(s["poss_ready"], b + 1)
                dve.tensor_copy(posi[:, b % 2, :, :], poss[:, :, :]).then_inc(s["posi_ready"], 1)

            lengths()
            dve.wait_ge(s["small_in"], 16 * 5)
            dve.wait_ge(s["wT_ready"], 1)
            for k in range(KD):
                dve.tensor_scalar(win[:, k, :], p_win[:, k * D:(k + 1) * D], gres[:, k:k + 1], None, ALU.mult)\
                   .then_inc(s["gw_ready"], 1)
            first(0)
            depooled(0)
            for b in range(B):
                if b + 1 < B:
                    first(b + 1)
                    depooled(b + 1)
                second(b)
                route(b)
                if b == 0:
                    split_up_lo(dve, 0, 0)
                    split_up_lo(dve, 0, 1)

            dve.wait_ge(s["base_step"], 2 + B)
            dve.tensor_scalar(padi[:, :], base[:, :], ids_f[:, 0:1], None, ALU.add).then_inc(s["padi_ready"], 1)
            count = [0]

            def tbl(ins):
                count[0] += 1
                ins.then_inc(s["tbl_step"], 1)
                dve.wait_ge(s["tbl_step"], count[0])

            tbl(dve.tensor_tensor(cum[:, :], base[0:1, :], regions[0:1, :], ALU.subtract))
            tbl(dve.tensor_scalar(n_i[:, :], cum[:, :], float(P - 1), None, ALU.add))
            tbl(dve.tensor_scalar(n_i[:, :], n_i[:, :], 7, None, ALU.logical_shift_right))
            tbl(dve.tensor_scalar(nblk[:, :], n_i[:, :], 1.0, None, ALU.max))
            tbl(dve.tensor_tensor_scan(cum[:, :], ones[0:1, 0:E], nblk[:, :], 0.0, ALU.mult, ALU.add))
            ef, stf, last, j_, j128, low6, low4, fst, two, flag, t0, i1 = (stepv[:, n, :] for n in range(12))
            i_all = iota_f[0:1, 0:TABLE]
            full = [1, TABLE, E]
            cum_b, nb_b = (v[:, :].unsqueeze(1).broadcast_to(full) for v in (cum, nblk))
            tbl(dve.tensor_tensor(stepm[:, :, :], i_all.unsqueeze(2).broadcast_to(full), cum_b, ALU.is_ge))
            tbl(dve.tensor_reduce(ef, stepm[:, :, :], AX.X, ALU.add))
            tbl(dve.tensor_tensor(stepm[:, :, :], stepm[:, :, :], nb_b, ALU.mult))
            tbl(dve.tensor_reduce(stf, stepm[:, :, :], AX.X, ALU.add))
            tbl(dve.tensor_scalar(i1, i_all, 1.0, None, ALU.add))
            tbl(dve.tensor_tensor(stepm[:, :, :], i1.unsqueeze(2).broadcast_to(full), cum_b, ALU.is_equal))
            tbl(dve.tensor_reduce(last, stepm[:, :, :], AX.X, ALU.add))
            tbl(dve.tensor_tensor(j_, i_all, stf, ALU.subtract))
            tbl(dve.tensor_scalar(j128, j_, float(P), None, ALU.mult))
            tbl(dve.scalar_tensor_tensor(t0, ef, float(REGION), j128, ALU.mult, ALU.add))
            tbl(dve.tensor_scalar(table[:, :, C_ROW], t0, float(PAD_ROW), None, ALU.min))
            tbl(dve.tensor_scalar(table[:, :, C_EXPERT], ef, float(E - 1), None, ALU.min))
            tbl(dve.tensor_scalar(low6, ef, float(E - 2), None, ALU.is_le))
            tbl(dve.tensor_scalar(low4, ef, float(E - 4), None, ALU.is_le))
            tbl(dve.tensor_scalar(fst, j_, 0.0, None, ALU.is_equal))
            tbl(dve.tensor_tensor(table[:, :, C_W1], fst, low6, ALU.mult))
            tbl(dve.tensor_tensor(fst, fst, last, ALU.mult))
            tbl(dve.scalar_tensor_tensor(two, j_, 1.0, fst, ALU.is_equal, ALU.add))
            tbl(dve.tensor_tensor(flag, two, low6, ALU.mult))
            tbl(dve.tensor_copy(table[:, :, C_W3], flag))
            tbl(dve.tensor_tensor(table[:, :, C_LOAD], flag, low4, ALU.mult))
            tbl(dve.tensor_scalar(table[:, :, C_LATER], ef, float(E - 4), None, ALU.min))
            tbl(dve.tensor_scalar(t0, ef, 1.0, 2.0, ALU.add, ALU.max))
            dve.tensor_scalar(table[:, :, C_NEED], t0, float(E), float(RAW_SEM), ALU.min, ALU.mult)\
               .then_inc(s["table_ready"], 1)

            def xT(i, q):
                dve.wait_ge(s["xThi_ready"], i + 1)
                dve.tensor_tensor(xT_lo[:, q].rearrange("p k t -> p (k t)"), p_xT,
                                  xT_hi[:, q].bitcast(f32).rearrange("p k t -> p (k t)"), ALU.subtract)\
                   .then_inc(s["xTlo_ready"], 1)

            def h(i, part):
                cols = slice(part * HALF, (part + 1) * HALF)
                dve.wait_ge(s[f"silu{part}_done"], i + 1)
                if not isinstance(i, int) or i > 0:
                    dve.wait_ge(s[f"th{part}_done"], i)
                dve.tensor_tensor(hmul[:, cols], gact[:, cols], p_lin[part][:, :], ALU.mult)\
                   .then_inc(s[f"h{part}_done"], 1)

            def hT(i, q, part):
                ks = slice(part * KF // 2, (part + 1) * KF // 2)
                dve.wait_ge(s[f"hT{part}hi_ready"], i + 1)
                dve.tensor_tensor(hT_lo[:, q, ks].rearrange("p k t -> p (k t)"), p_hT[part][:, :],
                                  hT_hi[:, q, ks].bitcast(f32).rearrange("p k t -> p (k t)"), ALU.subtract)\
                   .then_inc(s[f"hT{part}lo_ready"], 1)

            def step(i, q, half):
                later = not isinstance(i, int) or i > 0
                h(i, 0)
                if later:
                    hT(i - 1, 1 - q, 1)
                xT(i + 1, 1 - q)
                h(i, 1)
                e = step_value(dve, i, C_EXPERT, 0, E - 1)
                dve.wait_ge(s["added_rows"], OUT_INIT + 16 * (i - 1) if later else OUT_INIT)
                dve.tensor_copy(wtok[:, q:q + 1], xblk[:, q, ds(e + D, 1)])
                dve.tensor_copy(itok[:, q:q + 1], xblk[:, q, ROW_ID:ROW_ID + 1]).then_inc(s["meta_ready"], 1)
                hT(i, q, 0)
                for m, col in enumerate((C_W1, C_W3)):
                    split_now = step_value(dve, i, col, 0, 1)
                    with dve.If(split_now):
                        split_up_lo(dve, e + 1, m)

            dve.wait_ge(s["table_ready"], 1)
            dve.wait_ge(s["x1_rows"], 16 * B)
            xT(0, 0)
            over_steps(dve, step)
            hT(STEPS - 1, (STEPS - 1) % 2, 1)

        @block.tensor
        def _(pe):
            def lengths():
                pe.wait_ge(s["consts"], 2)
                pe.wait_ge(s["scan_ready"], 1)
                pe.matmul(p_prefix, tri[:, :], ln_s[:, :, :, CH - 1].rearrange("p k b -> p (k b)"),
                          start=True, stop=True).then_inc(s["prefix_ready"], 1)
                for b in range(B):
                    pe.wait_ge(s["onehot_ready"], b + 2)
                    for k in range(CH):
                        mm = pe.matmul(p_count[:, b * TPB:(b + 1) * TPB], onehot_lo[:, b % 2, k, :],
                                       onehot_hi[:, b * CH + k, :], start=(k == 0), stop=(k == CH - 1))
                    mm.then_inc(s["count_ready"], 1)
                pe.wait_ge(s["bmask_ready"], 1)
                flat = bmask[:, :, :].rearrange("p b j -> p (b j)")
                pe.matmul(p_plug, tri[:, :], flat, start=True, stop=False)
                pe.matmul(p_plug, ident[:, :], flat, start=False, stop=False)
                for j in range(TPB - 1):
                    more = TPB - 1 - j
                    mm = pe.matmul(p_plug.rearrange("p (b j) -> p b j", j=TPB)[:, :, j + 1:TPB], ones[:, :],
                                   bmask[:, :, j:j + 1].broadcast_to([P, B, more]),
                                   start=False, stop=(j == TPB - 2))
                mm.then_inc(s["plugmm_ready"], 1)

            def transposes(src, j, signal):
                for k in range(KD):
                    mm = pe.transpose(pT[j // 2][:, (j % 2) * D + k * P:(j % 2) * D + (k + 1) * P],
                                      src[:, j, k * P:(k + 1) * P], ident[:, :])
                mm.then_inc(signal, 1)

            def first(b):
                if b == 1:
                    pe.wait_ge(s["hnT_ready"], PAIRS)
                elif b >= 2:
                    pe.wait_ge(s["zT_ready"], PAIRS * (b - 1))
                for j in range(TPB):
                    pe.wait_ge(s["hn_ready"], b * TPB + j + 1)
                    transposes(hn, j, s["tn_ready"])
                if b == 0:
                    pe.wait_ge(s["gw_ready"], KD)
                    pe.wait_ge(s["affine_step"], 6 + len(decay))
                if b >= 1:
                    pe.wait_ge(s["dep_ready"], PAIRS * b)
                for j in range(TPB):
                    pe.wait_ge(s["hp_ready"], b * TPB + j + 1)
                    acc = pD[j // 2][:, (j % 2) * D:(j % 2 + 1) * D]
                    mm = pe.matmul(acc, decayT[:, 0:P], hp[:, j, :], start=True, stop=(j == 0))
                    if j:
                        mm = pe.matmul(acc, decayT[:, P:2 * P], hp[:, j - 1, :], start=False, stop=True)
                    mm.then_inc(s["depmm_ready"], 1)

            def second(b):
                if b == 0:
                    pe.wait_ge(s["gw_ready"], KD)
                else:
                    pe.wait_ge(s["x1_ready"], PAIRS * b)
                for j in range(TPB):
                    pe.wait_ge(s["hnT_ready"], b * PAIRS + j // 2 + 1)
                    for k in range(KD):
                        mm = pe.matmul(pH[j // 2][:, (j % 2) * D:(j % 2 + 1) * D],
                                       hnT[b % 2][:, j, k * P:(k + 1) * P], win[:, k, :],
                                       start=(k == 0), stop=(k == KD - 1))
                    mm.then_inc(s["hmm_ready"], 1)
                pe.wait_ge(s["hnT_ready"], PAIRS * min(b + 2, B))
                for j in range(TPB):
                    pe.wait_ge(s["z_ready"], b * TPB + j + 1)
                    transposes(payload[:, b % 2], j, s["tz_ready"])
                if b >= 1:
                    pe.wait_ge(s["base_step"], 2 + b)
                for j in range(TPB):
                    pe.wait_ge(s["zT_ready"], b * PAIRS + j // 2 + 1)
                    for k in range(KD):
                        mm = pe.matmul(p_logit[:, j * E:(j + 1) * E], zT[:, j, k * P:(k + 1) * P], gate[:, k, :],
                                       start=(k == 0), stop=(k == KD - 1))
                mm.then_inc(s["logit_mm"], 1)
                pe.wait_ge(s["picked_ready"], b + 1)
                pe.matmul(p_rank, tri[:, :], picked[:, :, :].rearrange("p j e -> p (j e)"), start=True, stop=False)
                for j in range(TPB - 1):
                    more = TPB - 1 - j
                    pe.matmul(p_rank.rearrange("p (j e) -> p j e", e=E)[:, j + 1:TPB, :], ones[:, :],
                              picked[:, j:j + 1, :].broadcast_to([P, more, E]), start=False, stop=(j == TPB - 2))
                for j in range(TPB):
                    mm = pe.matmul(p_total, ones[:, :], picked[:, j, :], start=(j == 0), stop=(j == TPB - 1))
                mm.then_inc(s["rank_mm"], 1)

            lengths()
            pe.wait_ge(s["small_in"], 16 * 5)
            for k in range(KD):
                for m in range(KD):
                    mm = pe.transpose(p_win[:, k * D + m * P:k * D + (m + 1) * P], win[:, m, k * P:(k + 1) * P],
                                      ident[:, :])
            mm.then_inc(s["wT_ready"], 1)
            first(0)
            for b in range(B):
                if b + 1 < B:
                    first(b + 1)
                second(b)

            def three(acc, x_hi, x_lo, w_hi, w_lo, start, stop):
                for n, (xp, wp) in enumerate(((x_hi, w_hi), (x_hi, w_lo), (x_lo, w_hi))):
                    for out_, w_ in zip(acc, wp):
                        mm = pe.matmul(out_, xp, w_, start=start and n == 0, stop=stop and n == 2)
                return mm

            def xT(i, q, half):
                pe.wait_ge(blk_in[q], 16 * (half + 1))
                for k in range(KD):
                    mm = pe.transpose(p_xT[:, k * P:(k + 1) * P], xblk[:, q, k * P:(k + 1) * P], ident[:, :])
                mm.then_inc(s["xT_done"], 1)

            def up(e, q, part):
                def weights(t, k):
                    return [t[:, ds(e & 1, 1), m, k, part * HALF:(part + 1) * HALF].rearrange("p o f -> p (o f)")
                            for m in range(2)]
                for k in range(KD):
                    mm = three((p_gate[part][:, :], p_lin[part][:, :]), xT_hi[:, q, k, :], xT_lo[:, q, k, :],
                               weights(up_hi, k), weights(up_lo, k), k == 0, k == KD - 1)
                mm.then_inc(s[f"up{part}_done"], 1)

            def hT(i, part):
                pe.wait_ge(s[f"h{part}_done"], i + 1)
                for k in range(KF // 2):
                    f0 = (part * KF // 2 + k) * P
                    mm = pe.transpose(p_hT[part][:, k * P:(k + 1) * P], hmul[:, f0:f0 + P], ident[:, :])
                mm.then_inc(s[f"th{part}_done"], 1)

            def down(i, q, e):
                pe.wait_ge(s["hT1lo_ready"], i + 1)
                pe.wait_ge(s["dn_ready"], e + 1)
                for k in range(KF):
                    w_hi, w_lo = ([t[:, ds(e & 1, 1), k, :].rearrange("p o d -> p (o d)")] for t in (dn_hi, dn_lo))
                    mm = three((p_y,), hT_hi[:, q, k, :], hT_lo[:, q, k, :], w_hi, w_lo, k == 0, k == KF - 1)
                mm.then_inc(s["y_done"], 1)

            def step(i, q, half):
                later = not isinstance(i, int) or i > 0
                e = step_value(pe, i, C_EXPERT, 0, E - 1)
                pe.wait_ge(s["xTlo_ready"], i + 1)
                pe.wait_ge(s["uplo_ready"], 2 * e + 2)
                if later:
                    pe.wait_ge(s["h0_done"], i)
                up(e, q, 0)
                if later:
                    hT(i - 1, 1)
                xT(i + 1, 1 - q, half + q)
                if later:
                    pe.wait_ge(s["h1_done"], i)
                up(e, q, 1)
                hT(i, 0)
                if later:
                    before = step_value(pe, i - 1, C_EXPERT, 0, E - 1)
                    down(i - 1, 1 - q, before)

            pe.wait_ge(s["table_ready"], 1)
            pe.wait_ge(s["posi_ready"], B)
            xT(0, 0, 0)
            over_steps(pe, step)
            hT(STEPS - 1, 1)
            down(STEPS - 1, (STEPS - 1) % 2, step_value(pe, STEPS - 1, C_EXPERT, 0, E - 1))


_INS = ["x", "ctx_2048", "mask_BxS2_if0", "L0_xattn_W_in", "L0_xattn_b_in", "L0_xattn_g_res", "L0_xattn_g_init",
        "L0_ffn_gate_w", "L0_ffn_w1", "L0_ffn_w3", "L0_ffn_w2"]


def kernel(**inputs):
    import numpy as _np
    import concourse.bacc as _bacc
    from concourse import mybir as _mybir
    from concourse.bass_utils import run_bass_kernel_spmd as _run

    nc = _bacc.Bacc("TRN2", target_bir_lowering=False, num_devices=1)
    arrays, args = {}, []
    for name in _INS:
        a = _np.ascontiguousarray(inputs[name])
        arrays[f"in_{name}"] = a
        args.append(nc.dram_tensor(f"in_{name}", a.shape, _mybir.dt.from_np(a.dtype), kind="ExternalInput").ap())
    args.append(nc.dram_tensor("out_0", (T + P, D), _mybir.dt.float32, kind="ExternalOutput").ap())
    build(nc, *args)
    r = _run(nc, [arrays], core_ids=[0])
    return r.results[0]["out_0"][0:T].reshape(B, S, D)
```

```python
import math
from contextlib import ExitStack

import numpy as np
import concourse.bass as bass
from concourse import mybir

P = 128
B, S, D = 4, 512, 256
S2, CD = 1601, 512
E, F = 8, 1024
T = B * S
TPB = S // P
PAIRS = TPB // 2
KD, KF = D // P, F // P
HALF = F // 2

EPS_LN, EPS_RMS, EPS_LOGP = 1e-5, 1e-5, 1e-3

REGION = T + P
ROW_W = D
ROW_ID = D + E
ROW = D + E + 1
PAD_ROW = E * REGION

BLOCKS = (2 * T + E * (P - 1) + E - 1) // P
assert BLOCKS == 39
STEP_PAIRS = BLOCKS // 2 + 1
TABLE = 1 + 2 * STEP_PAIRS + 3
C_WORD, C_ROW, C_END, COLS = range(4)
PREV_BIT = 3
F_CHUNK, F_W2, F_W3, F_LOAD, F_RUN = (1 << n for n in range(6, 11))
CHUNK_BIT = 11
OUT_INIT = 32

CH = -(-S2 // P)
FULL = S2 // CH
RAW_SEM = 48


def build(nc, x, ctx, lens, w_in, b_in, g_res, g_init, gate_w, w1, w3, w2, out):
    f32, f32r, bf16 = mybir.dt.float32, mybir.dt.float32r, mybir.dt.bfloat16
    i32, u8, u32 = mybir.dt.int32, mybir.dt.uint8, mybir.dt.uint32
    ALU, ACT, AX = mybir.AluOpType, mybir.ActivationFunctionType, mybir.AxisListType
    ds = bass.ds

    logp = np.float32(-EPS_LOGP)
    dt = np.float32(-np.log(-np.expm1(logp)))
    a, c = float(np.exp(-dt)), float(np.exp(logp))
    decay = [c * a ** k for k in range(P) if c * a ** k >= float(np.finfo(np.float32).tiny)]

    stack = ExitStack()
    with stack:
        def sb(name, shape, dtype, on=stack):
            return on.enter_context(nc.sbuf_tensor(name, shape, dtype))

        def sem(name):
            return stack.enter_context(nc.semaphore(name))

        xs = nc.dram_tensor("expert_rows", (PAD_ROW + P, ROW), f32, kind="Internal").ap()
        depool_dram = [nc.dram_tensor(f"depool_rows{b}", (S, D), f32, kind="Internal").ap() for b in range(B)]

        ident = sb("ident", [P, P], f32)
        tri = sb("tri", [P, P], f32)
        ones = sb("ones", [P, P], f32)
        decayT = sb("decayT", [P, 2 * P], f32)
        iota_i = sb("iota_i", [P, P], i32)
        iota_f = sb("iota_f", [P, P], f32)
        ids_i = sb("ids_i", [P, T // P + 1], i32)
        ids_f = sb("ids_f", [P, T // P + 1], f32)
        neg_half = sb("neg_half", [P, 2 * TPB], f32)
        win = sb("win", [P, KD, D], f32)
        gres = sb("gres", [P, KD], f32)
        gate = sb("gate", [P, KD, E], f32)
        ginit = sb("ginit", [P, D], f32)
        bin_ = sb("bin", [P, D], f32)
        padrow = sb("padrow", [P, ROW], f32)

        UP = 2 * KD * F
        RAW = UP + KF * D
        raw = sb("raw", [P, 2, RAW], f32)
        raw_up = raw[:, :, 0:UP].rearrange("p s (m k f) -> p s m k f", m=2, k=KD)
        raw_dn = raw[:, :, UP:RAW].rearrange("p s (k d) -> p s k d", k=KF)

        CHUNK = RAW // 3
        raw_chunk = raw[:, :, :].rearrange("p s (m c) -> p (s m) c", m=3)

        scratch = raw[:, 1, :].rearrange("p (n j d) -> p n j d", j=TPB, d=D)
        hn, hnT, zT, dep, hp = scratch[:, 0], [scratch[:, 1], scratch[:, 2]], scratch[:, 3], scratch[:, 4], scratch[:, 5]

        with ExitStack() as early:
            sb("first_slot", [P, 2, RAW], f32, early)
            x_all = sb("x_all", [P, B * TPB, D], f32, early)
            ctx_sb = sb("ctx_sb", [P, 2, TPB, CD], f32, early)
            payload = sb("payload", [P, 2, TPB, ROW], f32, early)
            onehot_lo = sb("onehot_lo", [P, 2, CH, P], bf16, early)
        split = sb("split", [P, 2, 2, RAW], f32r)
        up_hi, up_lo = (split[:, :, n, 0:UP].rearrange("p s (m k f) -> p s m k f", m=2, k=KD) for n in range(2))
        split_chunk = split[:, :, :, :].rearrange("p s n (m c) -> p (s n m) c", m=3)
        dn_hi, dn_lo = (split[:, :, n, UP:RAW].rearrange("p s (k d) -> p s k d", k=KF) for n in range(2))

        regions = sb("regions", [P, E], f32)
        iota_m8 = sb("iota_m8", [P, TPB], f32)
        sumsq = sb("sumsq", [P, 2, TPB], f32)
        st1 = sb("st1", [P, TPB, 6], f32)
        mv1 = sb("mv1", [P, TPB, 2], f32)
        vin = sb("vin", [P, 2 * TPB], f32)
        rs = sb("rs", [P, 2, 2 * TPB], f32)
        nb1 = sb("nb1", [P, TPB], f32)
        st2 = sb("st2", [P, TPB, 6], f32)
        mv2 = sb("mv2", [P, TPB, 2], f32)
        vin2 = sb("vin2", [P, TPB], f32)
        rs2 = sb("rs2", [P, TPB], f32)
        nb2 = sb("nb2", [P, TPB], f32)
        logits = sb("logits", [P, TPB, E], f32)
        top = sb("top", [P, TPB, 8], f32)
        topi = sb("topi", [P, TPB, 8], u32)
        topf = sb("topf", [P, 2, TPB], f32)
        oh = sb("oh", [P, 2, TPB, E], f32)
        ohw = sb("ohw", [P, 2, TPB, E], f32)
        picked = sb("picked", [P, TPB, E], f32)
        gap = sb("gap", [P, TPB], f32)
        egap = sb("egap", [P, TPB], f32)
        den = sb("den", [P, TPB], f32)
        wts = sb("wts", [P, 2, TPB], f32)
        base = sb("base", [P, E], f32)
        posf = sb("posf", [P, TPB, E], f32)
        posm = sb("posm", [P, 2, TPB, E], f32)
        poss = sb("poss", [P, 2, TPB], f32)
        posi = sb("posi", [P, 2, 2, TPB], i32)
        padi = sb("padi", [P, E], i32)
        dg = sb("dg", [P, 2, TPB, D], f32)

        NBC = B * CH
        ln_i = sb("ln_i", [P, B, CH], i32)
        ln_f = sb("ln_f", [P, 4, B, CH], f32)
        keep = sb("keep", [P, 4 * NBC], f32)
        ln_s = sb("ln_s", [P, 4, B, CH], f32)
        ln_c = sb("ln_c", [P, 4, NBC], i32)
        ln_t = sb("ln_t", [P, NBC], i32)
        ln_b = sb("ln_b", [P, 4, NBC], i32)
        ln_v = sb("ln_v", [P, 8, NBC], f32)
        ln_p = sb("ln_p", [P, 3, NBC], i32)
        onehot_hi = sb("onehot_hi", [P, NBC, TPB], bf16)
        bmask = sb("bmask", [P, B, TPB], f32)
        plugf = sb("plugf", [P, B, TPB], f32)
        plugi = sb("plugi", [P, B * TPB], i32)

        n_i = sb("n_i", [1, E], i32)
        nblk = sb("nblk", [1, E], f32)
        cum = sb("cum", [1, E], f32)
        stepm = sb("stepm", [1, TABLE, E], f32)
        stepv = sb("stepv", [1, 14, TABLE], f32)
        stepi = sb("stepi", [1, TABLE], i32)
        table = sb("table", [1, TABLE, COLS], i32)
        held = sb("held", [P, 2, E + 1], f32)
        wtok = sb("wtok", [P, 2], f32)
        itok = sb("itok", [P, 2], i32)

        xblk = sb("xblk", [P, 2, ROW], f32)
        xT_hi = sb("xT_hi", [P, 2, KD, P], f32r)
        xT_lo = sb("xT_lo", [P, 2, KD, P], f32r)
        gact = sb("gact", [P, F], f32)
        hmul = sb("hmul", [P, F], f32)
        hT_hi = sb("hT_hi", [P, 2, KF, P], f32r)
        hT_lo = sb("hT_lo", [P, 2, KF, P], f32r)
        yblk = sb("yblk", [P, 2, D], f32)

        bank = [stack.enter_context(nc.psum_tensor(f"bank{n}", [P, HALF], f32)) for n in range(8)]
        pT, pH, pD = bank[0:2], bank[2:4], bank[4:6]
        p_logit = bank[6][:, 0:TPB * E]
        p_rank = bank[6][:, 64:64 + TPB * E]
        p_total = bank[6][:, 128:128 + E]
        p_prefix = bank[7][:, 0:4 * B]
        p_count = bank[7][:, 64:64 + B * TPB]
        p_plug = bank[7][:, 128:128 + B * TPB]
        p_win = bank[4]
        p_gate, p_lin = [bank[0], bank[2]], [bank[1], bank[3]]
        p_hT = bank[4:6]
        p_xT = bank[6][:, 0:D]
        p_y = bank[7][:, 0:D]

        names = """lens_in small_in consts keep_ready bytes_ready iota_ready wT_ready scan_ready prefix_ready
            carry_step onehot_ready count_ready bmask_ready plugmm_ready plug_ready gw_ready pad_ready
            ids_ready base_step sq_ready st1_ready mv1_ready vin_ready rs_ready nb1_ready
            hn_ready tn_ready hnT_ready hp_ready depmm_ready dep_ready hmm_ready xd_ready x1_ready
            st2_ready mv2_ready vin2_ready rs2_ready nb2_ready z_ready tz_ready zT_ready logit_mm
            logit_ready top_ready topi_ready topf_ready gap_ready egap_ready den_ready
            wts_ready oh_ready picked_ready wi_step wi_ready rank_mm posf_ready posm_ready poss_ready
            posi_ready padf_ready padi_ready pad_rows tbl_step table_ready
            raw_first raw_ready hi_ready lo_ready x1_rows added_rows
            up0_done up1_done pad_step silu0_done silu1_done h0_done h1_done th0_done th1_done
            hT0hi_ready hT0lo_ready hT1hi_ready hT1lo_ready xT_done xThi_ready xTlo_ready
            held_ready meta_ready y_done y_ready affine_step
            settled_pool settled_sp""".split()
        s = {n: sem(n) for n in names}
        x_in = [sem(f"x_in{b}") for b in range(B)]
        ctx_in = [sem(f"ctx_in{b}") for b in range(B)]
        dep_rows = [sem(f"dep_rows{b}") for b in range(B)]
        dg_in = [sem(f"dg_in{b}") for b in range(B)]
        xs_rows = [sem(f"xs_rows{b}") for b in range(B)]
        blk_in = [sem(f"blk_in{q}") for q in range(2)]

        block = stack.enter_context(nc.Block())

        def pair(t, n):
            return t[:, 2 * n:2 * n + 2, :].rearrange("p j d -> p (j d)")

        def raw_load(eng, e, slot, signal):
            for m, w in enumerate((w1, w3)):
                eng.dma_start(raw_up[:, ds(slot, 1), m], w[ds(e, 1)].rearrange("o (k p) f -> p (o k) f", p=P))\
                   .then_inc(signal, 16)
            eng.dma_start(raw_dn[:, ds(slot, 1)], w2[ds(e, 1)].rearrange("o (k p) d -> p (o k) d", p=P))\
               .then_inc(signal, 16)

        def step_value(eng, i, col, low, high):
            return eng.value_load(table[0:1, ds(i, 1), col:col + 1].rearrange("a b c -> a (b c)"), min_val=low, max_val=high)

        def step_word(eng, i):
            return step_value(eng, i, C_WORD, 0, (3 << CHUNK_BIT) - 1)

        def expert(word):
            return word & (E - 1)

        def chunk_of(word):
            return (word >> CHUNK_BIT).with_bounds(min_val=0, max_val=2)

        def expert_before(word):
            return (word >> PREV_BIT) & (E - 1)

        def settle(eng):
            eng.sem_inc(s[f"settled_{'pool' if eng is nc.gpsimd else 'sp'}"], 1)

        def over_steps(eng, body):
            body(0, 0, 0, step_word(eng, 0))
            with eng.Fori(0, STEP_PAIRS) as pair:
                word = step_word(eng, pair * 2 + 1)
                with eng.If(word & F_RUN):
                    body(pair * 2 + 1, 1, pair, word)
                    body(pair * 2 + 2, 0, pair + 1, step_word(eng, pair * 2 + 2))

        def split_hi(act, raw3, m):
            act.activation(split_chunk[:, ds(raw3 * 2 + m, 1)], raw_chunk[:, ds(raw3 + m, 1)], ACT.Copy)\
               .then_inc(s["hi_ready"], 1)

        def split_lo(dve, e, raw3, m):
            dve.wait_ge(s["hi_ready"], e * 3 + m + 1)
            dve.tensor_tensor(split_chunk[:, ds(raw3 * 2 + m + 3, 1)], raw_chunk[:, ds(raw3 + m, 1)],
                              split_chunk[:, ds(raw3 * 2 + m, 1)].bitcast(f32), ALU.subtract)\
               .then_inc(s["lo_ready"], 1)

        @block.sync
        def _(sp):
            sp.wait_ge(s["keep_ready"], 1)
            sp.dma_start(ln_i[0:FULL, :, :], lens[:, 0:FULL * CH].rearrange("b (p c) -> p b c", c=CH))\
              .then_inc(s["lens_in"], 16)
            sp.dma_start(ln_i[FULL:FULL + 1, :, 0:S2 - FULL * CH],
                         lens[:, FULL * CH:S2].unsqueeze(0)).then_inc(s["lens_in"], 16)

            def load_batch(b):
                sp.dma_start(ctx_sb[:, b % 2], ctx[b, 0:S, :].rearrange("(j p) d -> p j d", p=P))\
                  .then_inc(ctx_in[b], 16)
                sp.dma_start(x_all[:, b * TPB:(b + 1) * TPB, :], x[b].rearrange("(j p) d -> p j d", p=P))\
                  .then_inc(x_in[b], 16)

            load_batch(0)
            sp.dma_start(win[:, :, :], w_in.rearrange("(k p) n -> p k n", p=P)).then_inc(s["small_in"], 16)
            sp.dma_start(ginit[:, :], g_init[0:D].unsqueeze(0).broadcast_to([P, D])).then_inc(s["small_in"], 16)
            sp.dma_start(bin_[:, :], b_in.unsqueeze(0).broadcast_to([P, D])).then_inc(s["small_in"], 16)
            with nc.allow_non_contiguous_dma(reason="256 elements"):
                sp.dma_start(gres[:, :], g_res.rearrange("(k p) -> p k", p=P)).then_inc(s["small_in"], 16)
            sp.dma_start(gate[:, :, :], gate_w.rearrange("(k p) n -> p k n", p=P)).then_inc(s["small_in"], 16)
            load_batch(1)
            raw_load(sp, 0, 0, s["raw_first"])

            for b in range(B):
                sp.wait_ge(s["dep_ready"], PAIRS * (b + 1))
                sp.dma_start(depool_dram[b].rearrange("(j p) d -> p j d", p=P), dep)\
                  .then_inc(dep_rows[b], 16)
                if b + 2 < B:
                    sp.wait_ge(s["hp_ready"], TPB * (b + 1))
                    sp.wait_ge(s["sq_ready"], TPB * (b + 1))
                    load_batch(b + 2)
            for b in range(B):
                sp.wait_ge(s["x1_ready"], PAIRS * (b + 1))
                sp.dma_start(out[b * S:(b + 1) * S, :].rearrange("(j p) d -> p j d", p=P),
                             x_all[:, b * TPB:(b + 1) * TPB, :]).then_inc(s["x1_rows"], 16)
                if b == 1:
                    sp.wait_ge(s["lo_ready"], 3)
                    raw_load(sp, 2, 0, s["raw_ready"])

            sp.wait_ge(s["x1_rows"], 16 * B)
            sp.wait_ge(s["z_ready"], B * TPB)
            sp.wait_ge(s["table_ready"], 1)
            for b in range(B):
                sp.wait_ge(xs_rows[b], 2 * TPB * 16)
            sp.wait_ge(s["pad_rows"], 16 * (E + 1))

            def load_rows(i, q):
                row = step_value(sp, i, C_ROW, 0, PAD_ROW)
                sp.dma_start(xblk[:, q], xs[ds(row, P), :]).then_inc(blk_in[q], 16)

            load_rows(0, 0)
            load_rows(1, 1)
            sp.wait_ge(s["logit_mm"], B)
            sp.wait_ge(s["raw_ready"], RAW_SEM)
            raw_load(sp, 1, 1, s["raw_ready"])
            sp.wait_ge(s["xT_done"], 1)
            sp.wait_ge(s["held_ready"], 1)
            load_rows(2, 0)

            def step(i, q, half, word):
                sp.wait_ge(s["xT_done"], i + 2)
                sp.wait_ge(s["held_ready"], i + 2)
                settle(sp)
                load_rows(i + 3, 1 - q)
                with sp.If(word & F_LOAD):
                    e = expert(word).with_bounds(min_val=0, max_val=E - 4)
                    sp.wait_ge(s["lo_ready"], e * 3 + 6)
                    settle(sp)
                    sp.wait_ge(s["raw_ready"], RAW_SEM * (e + 2))
                    settle(sp)
                    raw_load(sp, e + 3, (e + 1) & 1, s["raw_ready"])

            over_steps(sp, step)
            end = step_value(sp, 0, C_END, 32 * (E // 2), 32 * STEP_PAIRS)
            for q in range(2):
                sp.wait_ge(blk_in[q], (end >> 1) + 32)
                settle(sp)

        @block.gpsimd
        def _(pool):
            pool.memset(ident[:, :], 0.0).then_inc(s["affine_step"], 1)
            pool.memset(ones[:, :], 1.0).then_inc(s["affine_step"], 1)
            pool.memset(decayT[:, :], 0.0).then_inc(s["affine_step"], 1)
            pool.iota(iota_i[:, :], pattern=[[1, P]], base=0, channel_multiplier=0).then_inc(s["affine_step"], 1)
            pool.iota(ids_i[:, :], pattern=[[P, T // P + 1]], base=0, channel_multiplier=1)\
                .then_inc(s["affine_step"], 1)
            pool.memset(neg_half[:, :], -0.5).then_inc(s["affine_step"], 1)
            pool.wait_ge(s["affine_step"], 6)
            pool.affine_select(out=ident[:, :], in_=ident[:, :], compare_op=ALU.not_equal, fill=1.0,
                               base=0, pattern=[[-1, P]], channel_multiplier=1).then_inc(s["consts"], 1)
            pool.affine_select(out=tri[:, :], in_=ones[:, :], compare_op=ALU.is_gt, fill=0.0,
                               base=0, pattern=[[1, P]], channel_multiplier=-1).then_inc(s["consts"], 1)
            for k, v in enumerate(decay):
                if k:
                    pool.wait_ge(s["affine_step"], 6 + k)
                pool.affine_select(out=decayT[:, :], in_=decayT[:, :], compare_op=ALU.not_equal, fill=v,
                                   base=-k, pattern=[[1, 2 * P]], channel_multiplier=-1)\
                    .then_inc(s["affine_step"], 1)

            pool.wait_ge(s["pad_ready"], 1)
            pool.dma_start(xs[PAD_ROW:PAD_ROW + P, :], padrow[:, :]).then_inc(s["pad_rows"], 16)
            for n in range(2):
                pool.dma_start(out[T + n * P // 2:T + (n + 1) * P // 2, :], padrow[0:P // 2, 0:D])\
                    .then_inc(s["added_rows"], OUT_INIT // 2)

            def pow1(b):
                pool.wait_ge(s["vin_ready"], 2 * (b + 1))
                pool.tensor_tensor(rs[:, b % 2], vin[:, :], neg_half[:, :], ALU.pow).then_inc(s["rs_ready"], 1)

            def gather(b):
                pool.wait_ge(s["plug_ready"], 1)
                pool.wait_ge(dep_rows[b], 16)
                if b >= 2:
                    pool.wait_ge(s["xd_ready"], b - 1)
                for j in range(TPB):
                    n = b * TPB + j
                    pool.indirect_dma_start(dg[:, b % 2, j, :], None, depool_dram[b][:, :],
                                            bass.IndirectOffsetOnAxis(ap=plugi[:, n:n + 1], axis=0))\
                        .then_inc(dg_in[b], 16)

            def pow2(b):
                pool.wait_ge(s["vin2_ready"], b + 1)
                pool.tensor_tensor(rs2[:, :], vin2[:, :], neg_half[:, 0:TPB], ALU.pow)\
                    .then_inc(s["rs2_ready"], 1)

            def scatter(b):
                pool.wait_ge(s["z_ready"], TPB * (b + 1))
                pool.wait_ge(s["wi_ready"], b + 1)
                pool.wait_ge(s["posi_ready"], b + 1)
                for j in range(TPB):
                    for r in range(2):
                        pool.indirect_dma_start(xs[:, :], bass.IndirectOffsetOnAxis(
                            ap=posi[:, b % 2, r, j:j + 1], axis=0), payload[:, b % 2, j, :], None)\
                            .then_inc(xs_rows[b], 16)

            pow1(0)
            for b in range(B):
                if b + 1 < B:
                    pow1(b + 1)
                gather(b)
                pow2(b)
                scatter(b)
            pool.wait_ge(s["padi_ready"], 1)
            for e in range(E):
                pool.indirect_dma_start(xs[:, :], bass.IndirectOffsetOnAxis(ap=padi[:, e:e + 1], axis=0),
                                        padrow[:, :], None).then_inc(s["pad_rows"], 16)

            def add_rows(i, q):
                pool.wait_ge(s["y_ready"], i + 1)
                pool.wait_ge(s["added_rows"], OUT_INIT + 16 * i)
                settle(pool)
                pool.indirect_dma_start(out[:, :], bass.IndirectOffsetOnAxis(ap=itok[:, q:q + 1], axis=0),
                                        yblk[:, q, :], None, compute_op=ALU.add).then_inc(s["added_rows"], 16)

            pool.wait_ge(s["table_ready"], 1)
            pool.wait_ge(s["x1_rows"], 16 * B)
            with pool.Fori(0, STEP_PAIRS) as pair:
                word = step_word(pool, pair * 2 + 1)
                with pool.If(word & F_RUN):
                    add_rows(pair * 2, 0)
                    add_rows(pair * 2 + 1, 1)
            end = step_value(pool, 0, C_END, 32 * (E // 2), 32 * STEP_PAIRS)
            pool.wait_ge(s["added_rows"], OUT_INIT + end)
            settle(pool)

        @block.scalar
        def _(act):
            def norm_first(b):
                act.wait_ge(ctx_in[b], 16)
                if b >= 1:
                    act.wait_ge(s["depmm_ready"], TPB * b)
                for j in range(TPB):
                    act.activation(hp[:, j, :].bitcast(bf16), ctx_sb[:, b % 2, j, :], ACT.Square,
                                   accum_out=sumsq[:, b % 2, j:j + 1]).then_inc(s["sq_ready"], 1)
                act.wait_ge(s["nb1_ready"], b + 1)
                for j in range(TPB):
                    if b >= 1:
                        act.wait_ge(s["tn_ready"], TPB * b)
                    act.activation(hn[:, j, :], x_all[:, b * TPB + j, :], ACT.Identity,
                                   scale=rs[:, b % 2, TPB + j:TPB + j + 1], bias=nb1[:, j:j + 1])\
                       .then_inc(s["hn_ready"], 1)
                for n in range(PAIRS):
                    act.wait_ge(s["tn_ready"], b * TPB + 2 * n + 2)
                    act.activation(pair(hnT[b % 2], n), pT[n][:, :], ACT.Copy)\
                       .then_inc(s["hnT_ready"], 1)

            def norm_second(b):
                act.wait_ge(s["nb2_ready"], b + 1)
                if b >= 2:
                    act.wait_ge(xs_rows[b - 2], 2 * TPB * 16)
                for j in range(TPB):
                    act.activation(payload[:, b % 2, j, 0:D], x_all[:, b * TPB + j, :], ACT.Identity,
                                   scale=rs2[:, j:j + 1], bias=nb2[:, j:j + 1]).then_inc(s["z_ready"], 1)
                for n in range(PAIRS):
                    act.wait_ge(s["tz_ready"], b * TPB + 2 * n + 2)
                    act.activation(pair(zT, n), pT[n][:, :], ACT.Copy)\
                       .then_inc(s["zT_ready"], 1)
                act.wait_ge(s["gap_ready"], b + 1)
                act.activation(egap[:, :], gap[:, :], ACT.Exp).then_inc(s["egap_ready"], 1)

            norm_first(0)
            for b in range(B):
                if b + 1 < B:
                    norm_first(b + 1)
                norm_second(b)
                if b == 0:
                    act.wait_ge(s["raw_first"], RAW_SEM)
                    for m in range(3):
                        split_hi(act, 0, m)

            act.wait_ge(s["table_ready"], 1)
            act.wait_ge(s["x1_rows"], 16 * B)

            def xT(i, q):
                act.wait_ge(s["xT_done"], i + 1)
                act.activation(xT_hi[:, q], p_xT, ACT.Copy).then_inc(s["xThi_ready"], 1)

            def hT(i, q, half):
                act.wait_ge(s[f"th{half}_done"], i + 1)
                act.activation(hT_hi[:, q, half * KF // 2:(half + 1) * KF // 2], p_hT[half][:, :], ACT.Copy)\
                   .then_inc(s[f"hT{half}hi_ready"], 1)

            def silu(i, half):
                act.wait_ge(s[f"up{half}_done"], i + 1)
                act.activation(gact[:, half * HALF:(half + 1) * HALF], p_gate[half][:, :], ACT.Silu)\
                   .then_inc(s[f"silu{half}_done"], 1)

            def y(i, q):
                act.wait_ge(s["y_done"], i + 1)
                act.wait_ge(s["added_rows"], OUT_INIT + 16 * (i - 1))
                act.wait_ge(s["meta_ready"], i + 1)
                act.activation(yblk[:, q, :], p_y, ACT.Copy, scale=wtok[:, q:q + 1]).then_inc(s["y_ready"], 1)

            def step(i, q, half, word):
                later = not isinstance(i, int) or i > 0
                silu(i, 0)
                if later:
                    hT(i - 1, 1 - q, 1)
                xT(i + 1, 1 - q)
                silu(i, 1)
                hT(i, q, 0)
                with act.If(word & F_CHUNK):
                    e = expert(word)
                    act.wait_ge(s["raw_ready"], RAW_SEM * (e + 1) if later else RAW_SEM * 2)
                    raw3 = ((e + 1) & 1) * 3
                    split_hi(act, raw3, chunk_of(word))
                    with act.If(word & F_W2):
                        with act.If(word & F_W3):
                            split_hi(act, raw3, 1)
                        if later:
                            act.wait_ge(s["y_done"], i)
                        split_hi(act, raw3, 2)
                if later:
                    y(i - 1, 1 - q)

            xT(0, 0)
            over_steps(act, step)

        @block.vector
        def _(dve):
            dve.memset(ln_i[:, :, :], 0).then_inc(s["keep_ready"], 1)
            dve.memset(keep[:, :], 1.0).then_inc(s["keep_ready"], 1)
            dve.wait_ge(s["keep_ready"], 2)
            dve.memset(keep[:, :].rearrange("p (n c) -> p n c", c=CH)[:, :, 0:1], 0.0).then_inc(s["keep_ready"], 1)
            dve.memset(padrow[:, :], 0.0).then_inc(s["pad_step"], 1)
            dve.wait_ge(s["affine_step"], 5)
            dve.tensor_copy(iota_f[:, :], iota_i[:, :]).then_inc(s["iota_ready"], 1)
            dve.tensor_copy(ids_f[:, :], ids_i[:, :]).then_inc(s["ids_ready"], 1)
            dve.wait_ge(s["iota_ready"], 1)
            dve.wait_ge(s["ids_ready"], 1)
            dve.wait_ge(s["pad_step"], 1)
            dve.tensor_copy(padrow[:, ROW_ID:ROW_ID + 1], ids_f[:, T // P:T // P + 1]).then_inc(s["pad_ready"], 1)
            dve.tensor_scalar(iota_m8[:, :], iota_f[:, 0:TPB], -8.0, None, ALU.add).then_inc(s["iota_ready"], 1)
            dve.tensor_scalar(regions[:, :], iota_f[:, 0:E], float(REGION), None, ALU.mult).then_inc(s["base_step"], 1)
            dve.tensor_scalar(base[:, :], iota_f[:, 0:E], float(REGION), None, ALU.mult).then_inc(s["base_step"], 1)

            def lengths():
                dve.wait_ge(s["lens_in"], 32)
                dve.wait_ge(s["keep_ready"], 3)
                dve.tensor_copy(ln_f[:, :, :, :], ln_i[:, :, :].bitcast(u8).rearrange("p b (c k) -> p k b c", k=4))\
                   .then_inc(s["bytes_ready"], 1)
                dve.wait_ge(s["bytes_ready"], 1)
                dve.tensor_tensor_scan(ln_s[:, :, :, :].rearrange("p k b c -> p (k b c)"), keep[:, :],
                                       ln_f[:, :, :, :].rearrange("p k b c -> p (k b c)"), 0.0, ALU.mult, ALU.add)\
                   .then_inc(s["scan_ready"], 1)
                dve.wait_ge(s["prefix_ready"], 1)
                dve.tensor_tensor(ln_c[:, :, :].rearrange("p k (b c) -> p (k b) c", c=CH),
                                  ln_s[:, :, :, :].rearrange("p k b c -> p (k b) c"),
                                  p_prefix.unsqueeze(2).broadcast_to([P, 4 * B, CH]), ALU.add)\
                   .then_inc(s["carry_step"], 1)
                n = 1
                for k in range(4):
                    dve.wait_ge(s["carry_step"], n)
                    dve.tensor_scalar(ln_b[:, k, :], ln_c[:, k, :], 255, None, ALU.bitwise_and)\
                       .then_inc(s["carry_step"], 1)
                    n += 1
                    if k < 3:
                        dve.tensor_scalar(ln_t[:, :], ln_c[:, k, :], 8, None, ALU.logical_shift_right)\
                           .then_inc(s["carry_step"], 1)
                        dve.wait_ge(s["carry_step"], n + 1)
                        dve.tensor_tensor(ln_c[:, k + 1, :], ln_c[:, k + 1, :], ln_t[:, :], ALU.add)\
                           .then_inc(s["carry_step"], 1)
                        n += 2
                low, high, lowok, lowneg, ok0, ok1, ok, hif = (ln_v[:, n_, :] for n_ in range(8))
                idx, lo_i, hi_i = (ln_p[:, n_, :] for n_ in range(3))
                dve.wait_ge(s["carry_step"], n)
                dve.scalar_tensor_tensor(low, ln_b[:, 1, :], 256.0, ln_b[:, 0, :], ALU.mult, ALU.add)\
                   .then_inc(s["carry_step"], 1)
                dve.scalar_tensor_tensor(high, ln_b[:, 3, :], 256.0, ln_b[:, 2, :], ALU.mult, ALU.add)\
                   .then_inc(s["carry_step"], 1)
                dve.wait_ge(s["carry_step"], n + 2)
                dve.tensor_scalar(lowok, low, float(S), None, ALU.is_le).then_inc(s["carry_step"], 1)
                dve.tensor_scalar(lowneg, low, float(65536 + 1 - S), None, ALU.is_ge).then_inc(s["carry_step"], 1)
                dve.tensor_scalar(idx, low, float(S - 1), None, ALU.add).then_inc(s["carry_step"], 1)
                dve.wait_ge(s["carry_step"], n + 5)
                dve.scalar_tensor_tensor(ok0, high, 0.0, lowok, ALU.is_equal, ALU.mult).then_inc(s["carry_step"], 1)
                dve.scalar_tensor_tensor(ok1, high, 65535.0, lowneg, ALU.is_equal, ALU.mult)\
                   .then_inc(s["carry_step"], 1)
                dve.tensor_scalar(lo_i, idx, P - 1, None, ALU.bitwise_and).then_inc(s["carry_step"], 1)
                dve.tensor_scalar(hi_i, idx, 7, TPB - 1, ALU.logical_shift_right, ALU.bitwise_and)\
                   .then_inc(s["carry_step"], 1)
                dve.wait_ge(s["carry_step"], n + 9)
                dve.tensor_tensor(ok, ok0, ok1, ALU.add).then_inc(s["carry_step"], 1)
                dve.tensor_copy(low, lo_i).then_inc(s["carry_step"], 1)
                dve.wait_ge(s["carry_step"], n + 11)
                dve.scalar_tensor_tensor(hif, ok, -8.0, hi_i, ALU.mult, ALU.add).then_inc(s["carry_step"], 1)
                dve.wait_ge(s["carry_step"], n + 12)
                dve.wait_ge(s["iota_ready"], 2)
                dve.tensor_tensor(onehot_hi[:, :, :], iota_m8[:, :].unsqueeze(1).broadcast_to([P, NBC, TPB]),
                                  hif.unsqueeze(2).broadcast_to([P, NBC, TPB]), ALU.is_equal)\
                   .then_inc(s["onehot_ready"], 1)
                for b in range(B):
                    if b >= 2:
                        dve.wait_ge(s["count_ready"], b - 1)
                    dve.tensor_tensor(onehot_lo[:, b % 2], iota_f[:, :].unsqueeze(1).broadcast_to([P, CH, P]),
                                      low[:, b * CH:(b + 1) * CH].unsqueeze(2).broadcast_to([P, CH, P]),
                                      ALU.is_equal).then_inc(s["onehot_ready"], 1)
                dve.wait_ge(s["count_ready"], B)
                dve.tensor_scalar(bmask[:, :, :].rearrange("p b j -> p (b j)"), p_count, 0.5, None, ALU.is_gt)\
                   .then_inc(s["bmask_ready"], 1)
                dve.wait_ge(s["plugmm_ready"], 1)
                dve.tensor_scalar(plugf[:, :, :].rearrange("p b j -> p (b j)"), p_plug, -1.0, 0.0, ALU.add, ALU.max)\
                   .then_inc(s["bmask_ready"], 1)
                dve.wait_ge(s["bmask_ready"], 2)
                dve.tensor_scalar(plugi[:, :], plugf[:, :, :].rearrange("p b j -> p (b j)"), float(S2 - 1), None,
                                  ALU.min).then_inc(s["plug_ready"], 1)

            def first(b):
                dve.wait_ge(x_in[b], 16)
                for j in range(TPB):
                    dve.bn_stats(st1[:, j, :], x_all[:, b * TPB + j, :]).then_inc(s["st1_ready"], 1)
                dve.wait_ge(s["st1_ready"], TPB * (b + 1))
                for j in range(TPB):
                    dve.bn_aggr(mv1[:, j, :], st1[:, j, :]).then_inc(s["mv1_ready"], 1)
                dve.wait_ge(s["sq_ready"], TPB * (b + 1))
                if b >= 1:
                    dve.wait_ge(s["rs_ready"], b)
                dve.tensor_scalar(vin[:, 0:TPB], sumsq[:, b % 2, :], 1.0 / CD, EPS_RMS, ALU.mult, ALU.add)\
                   .then_inc(s["vin_ready"], 1)
                dve.wait_ge(s["mv1_ready"], TPB * (b + 1))
                dve.tensor_scalar(vin[:, TPB:2 * TPB], mv1[:, :, 1], 1.0 + EPS_RMS, EPS_LN * EPS_RMS,
                                  ALU.mult, ALU.add).then_inc(s["vin_ready"], 1)
                dve.wait_ge(s["rs_ready"], b + 1)
                if b >= 1:
                    dve.wait_ge(s["hn_ready"], TPB * b)
                dve.scalar_tensor_tensor(nb1[:, :], mv1[:, :, 0], -1.0, rs[:, b % 2, TPB:2 * TPB],
                                         ALU.mult, ALU.mult).then_inc(s["nb1_ready"], 1)
                dve.wait_ge(ctx_in[b], 16)
                dve.wait_ge(s["small_in"], 16 * 5)
                if b >= 1:
                    dve.wait_ge(s["depmm_ready"], TPB * b)
                for j in range(TPB):
                    dve.scalar_tensor_tensor(hp[:, j, :], ctx_sb[:, b % 2, j, 0:D], rs[:, b % 2, j:j + 1],
                                             ginit[:, :], ALU.mult, ALU.mult).then_inc(s["hp_ready"], 1)

            def depooled(b):
                if b >= 1:
                    dve.wait_ge(dep_rows[b - 1], 16)
                for n in range(PAIRS):
                    dve.wait_ge(s["depmm_ready"], b * TPB + 2 * n + 2)
                    dve.tensor_tensor(dep[:, 2 * n:2 * n + 2, :], pD[n][:, :].rearrange("p (j d) -> p j d", d=D),
                                      bin_[:, :].unsqueeze(1).broadcast_to([P, 2, D]), ALU.add)\
                       .then_inc(s["dep_ready"], 1)

            def second(b):
                dve.wait_ge(dg_in[b], 16 * TPB)
                dve.wait_ge(s["hn_ready"], TPB * (b + 1))
                flat = x_all[:, b * TPB:(b + 1) * TPB, :].rearrange("p j d -> p (j d)")
                dve.tensor_tensor(flat, flat, dg[:, b % 2].rearrange("p j d -> p (j d)"), ALU.add)\
                   .then_inc(s["xd_ready"], 1)
                dve.wait_ge(s["xd_ready"], b + 1)
                xb = x_all[:, b * TPB:(b + 1) * TPB, :]
                for n in range(PAIRS):
                    dve.wait_ge(s["hmm_ready"], b * TPB + 2 * n + 2)
                    dve.tensor_tensor(pair(xb, n), pair(xb, n), pH[n][:, :], ALU.add).then_inc(s["x1_ready"], 1)
                for j in range(TPB):
                    dve.wait_ge(s["x1_ready"], b * PAIRS + j // 2 + 1)
                    dve.bn_stats(st2[:, j, :], x_all[:, b * TPB + j, :]).then_inc(s["st2_ready"], 1)
                dve.wait_ge(s["st2_ready"], TPB * (b + 1))
                for j in range(TPB):
                    dve.bn_aggr(mv2[:, j, :], st2[:, j, :]).then_inc(s["mv2_ready"], 1)
                dve.wait_ge(s["mv2_ready"], TPB * (b + 1))
                if b >= 1:
                    dve.wait_ge(s["z_ready"], TPB * b)
                dve.tensor_scalar(vin2[:, :], mv2[:, :, 1], EPS_LN, None, ALU.add).then_inc(s["vin2_ready"], 1)
                dve.wait_ge(s["rs2_ready"], b + 1)
                dve.scalar_tensor_tensor(nb2[:, :], mv2[:, :, 0], -1.0, rs2[:, :], ALU.mult, ALU.mult)\
                   .then_inc(s["nb2_ready"], 1)

            def route(b):
                dve.wait_ge(s["logit_mm"], b + 1)
                dve.tensor_copy(logits[:, :, :].rearrange("p j e -> p (j e)"), p_logit).then_inc(s["logit_ready"], 1)
                dve.wait_ge(s["logit_ready"], b + 1)
                for j in range(TPB):
                    dve.max(top[:, j, :], logits[:, j, :]).then_inc(s["top_ready"], 1)
                dve.wait_ge(s["top_ready"], TPB * (b + 1))
                for j in range(TPB):
                    dve.max_index(topi[:, j, :], top[:, j, :], logits[:, j, :]).then_inc(s["topi_ready"], 1)
                dve.tensor_tensor(gap[:, :], top[:, :, 1], top[:, :, 0], ALU.subtract).then_inc(s["gap_ready"], 1)
                dve.wait_ge(s["topi_ready"], TPB * (b + 1))
                dve.tensor_copy(topf[:, :, :], topi[:, :, 0:2].rearrange("p j r -> p r j")).then_inc(s["topf_ready"], 1)
                dve.wait_ge(s["topf_ready"], b + 1)
                oh_v = oh[:, :, :, :].rearrange("p r j e -> p (r j) e")
                dve.tensor_tensor(oh_v, iota_f[:, 0:E].unsqueeze(1).broadcast_to([P, 2 * TPB, E]),
                                  topf[:, :, :].rearrange("p r j -> p (r j)").unsqueeze(2)
                                  .broadcast_to([P, 2 * TPB, E]), ALU.is_equal).then_inc(s["oh_ready"], 1)
                dve.wait_ge(s["oh_ready"], b + 1)
                dve.tensor_tensor(picked[:, :, :], oh[:, 0], oh[:, 1], ALU.add).then_inc(s["picked_ready"], 1)
                dve.wait_ge(s["egap_ready"], b + 1)
                dve.tensor_scalar(den[:, :], egap[:, :], 1.0, None, ALU.add).then_inc(s["den_ready"], 1)
                dve.wait_ge(s["den_ready"], b + 1)
                dve.reciprocal(wts[:, 0, :], den[:, :]).then_inc(s["wts_ready"], 1)
                dve.wait_ge(s["wts_ready"], 2 * b + 1)
                dve.tensor_tensor(wts[:, 1, :], egap[:, :], wts[:, 0, :], ALU.mult).then_inc(s["wts_ready"], 1)
                dve.wait_ge(s["wts_ready"], 2 * b + 2)
                dve.tensor_tensor(ohw[:, :, :, :].rearrange("p r j e -> p (r j) e"), oh_v,
                                  wts[:, :, :].rearrange("p r j -> p (r j)").unsqueeze(2)
                                  .broadcast_to([P, 2 * TPB, E]), ALU.mult).then_inc(s["wi_step"], 1)
                dve.wait_ge(s["wi_step"], b + 1)
                if b >= 2:
                    dve.wait_ge(xs_rows[b - 2], 2 * TPB * 16)
                dve.tensor_copy(payload[:, b % 2, :, ROW_ID], ids_f[:, b * TPB:(b + 1) * TPB])
                dve.tensor_tensor(payload[:, b % 2, :, ROW_W:ROW_W + E], ohw[:, 0], ohw[:, 1], ALU.add)\
                   .then_inc(s["wi_ready"], 1)
                dve.wait_ge(s["rank_mm"], b + 1)
                dve.wait_ge(s["base_step"], 2 + b)
                dve.tensor_tensor(posf[:, :, :], p_rank.rearrange("p (j e) -> p j e", e=E),
                                  base[:, :].unsqueeze(1).broadcast_to([P, TPB, E]), ALU.add)\
                   .then_inc(s["posf_ready"], 1)
                dve.wait_ge(s["posf_ready"], b + 1)
                dve.tensor_tensor(base[:, :], base[:, :], p_total, ALU.add).then_inc(s["base_step"], 1)
                for r in range(2):
                    dve.tensor_tensor(posm[:, r], oh[:, r], posf[:, :, :], ALU.mult).then_inc(s["posm_ready"], 1)
                dve.wait_ge(s["posm_ready"], 2 * (b + 1))
                dve.tensor_reduce(poss[:, :, :].rearrange("p r j -> p (r j)"),
                                  posm[:, :, :, :].rearrange("p r j e -> p (r j) e"), AX.X, ALU.add)\
                   .then_inc(s["poss_ready"], 1)
                dve.wait_ge(s["poss_ready"], b + 1)
                dve.tensor_copy(posi[:, b % 2, :, :], poss[:, :, :]).then_inc(s["posi_ready"], 1)

            lengths()
            dve.wait_ge(s["small_in"], 16 * 5)
            dve.wait_ge(s["wT_ready"], 1)
            for k in range(KD):
                dve.tensor_scalar(win[:, k, :], p_win[:, k * D:(k + 1) * D], gres[:, k:k + 1], None, ALU.mult)\
                   .then_inc(s["gw_ready"], 1)
            first(0)
            depooled(0)
            for b in range(B):
                if b + 1 < B:
                    first(b + 1)
                    depooled(b + 1)
                second(b)
                route(b)
                if b == 0:
                    for m in range(3):
                        split_lo(dve, 0, 0, m)

            dve.wait_ge(s["base_step"], 2 + B)
            dve.tensor_scalar(padi[:, :], base[:, :], ids_f[:, 0:1], None, ALU.add).then_inc(s["padi_ready"], 1)
            count = [0]

            def tbl(ins):
                count[0] += 1
                ins.then_inc(s["tbl_step"], 1)
                dve.wait_ge(s["tbl_step"], count[0])

            tbl(dve.tensor_tensor(cum[:, :], base[0:1, :], regions[0:1, :], ALU.subtract))
            tbl(dve.tensor_scalar(n_i[:, :], cum[:, :], float(P - 1), None, ALU.add))
            tbl(dve.tensor_scalar(n_i[:, :], n_i[:, :], 7, None, ALU.logical_shift_right))
            tbl(dve.tensor_scalar(nblk[:, :], n_i[:, :], 1.0, None, ALU.max))
            tbl(dve.tensor_tensor_scan(cum[:, :], ones[0:1, 0:E], nblk[:, :], 0.0, ALU.mult, ALU.add))
            ef, stf, last, j_, j128, low6, low4, fst, two, three_, t0, i1, run, word_ = (stepv[:, n, :] for n in range(14))
            i_all = iota_f[0:1, 0:TABLE]
            full = [1, TABLE, E]
            cum_b, nb_b = (v[:, :].unsqueeze(1).broadcast_to(full) for v in (cum, nblk))
            tbl(dve.tensor_tensor(stepm[:, :, :], i_all.unsqueeze(2).broadcast_to(full), cum_b, ALU.is_ge))
            tbl(dve.tensor_reduce(ef, stepm[:, :, :], AX.X, ALU.add))
            tbl(dve.tensor_tensor(stepm[:, :, :], stepm[:, :, :], nb_b, ALU.mult))
            tbl(dve.tensor_reduce(stf, stepm[:, :, :], AX.X, ALU.add))
            tbl(dve.tensor_scalar(i1, i_all, 1.0, None, ALU.add))
            tbl(dve.tensor_tensor(stepm[:, :, :], i1.unsqueeze(2).broadcast_to(full), cum_b, ALU.is_equal))
            tbl(dve.tensor_reduce(last, stepm[:, :, :], AX.X, ALU.add))
            tbl(dve.tensor_tensor(j_, i_all, stf, ALU.subtract))
            tbl(dve.tensor_scalar(j128, j_, float(P), None, ALU.mult))
            tbl(dve.scalar_tensor_tensor(t0, ef, float(REGION), j128, ALU.mult, ALU.add))
            tbl(dve.tensor_scalar(table[:, :, C_ROW], t0, float(PAD_ROW), None, ALU.min))
            tbl(dve.tensor_scalar(low4, ef, float(E - 4), None, ALU.is_le))
            tbl(dve.tensor_scalar(low6, ef, float(E - 2), None, ALU.is_le))
            tbl(dve.tensor_scalar(ef, ef, float(E - 1), None, ALU.min))
            tbl(dve.tensor_tensor(run, cum[:, E - 1:E].broadcast_to([1, TABLE]), i_all, ALU.is_ge))
            tbl(dve.tensor_scalar(two, j_, 1.0, None, ALU.is_le))
            tbl(dve.tensor_tensor(two, two, last, ALU.mult))
            tbl(dve.scalar_tensor_tensor(fst, j_, 0.0, two, ALU.is_equal, ALU.mult))
            tbl(dve.scalar_tensor_tensor(three_, j_, 2.0, two, ALU.is_equal, ALU.add))
            tbl(dve.tensor_tensor(three_, three_, low4, ALU.mult))
            tbl(dve.scalar_tensor_tensor(low4, j_, 2.0, low6, ALU.is_le, ALU.mult))
            tbl(dve.tensor_scalar(j_, j_, 2.0, float(1 << CHUNK_BIT), ALU.min, ALU.mult))
            tbl(dve.scalar_tensor_tensor(word_, run, float(F_RUN), j_, ALU.mult, ALU.add))
            for weight, bits in ((F_CHUNK, low4), (F_W2, two), (F_W3, fst), (F_LOAD, three_), (1, ef)):
                tbl(dve.scalar_tensor_tensor(word_, bits, float(weight), word_, ALU.mult, ALU.add))
            tbl(dve.scalar_tensor_tensor(word_[:, 1:TABLE], ef[:, 0:TABLE - 1], float(1 << PREV_BIT),
                                         word_[:, 1:TABLE], ALU.mult, ALU.add))
            tbl(dve.tensor_copy(table[:, :, C_WORD], word_))
            tbl(dve.tensor_scalar(stepi[:, :], cum[:, E - 1:E].broadcast_to([1, TABLE]), 1.0, None, ALU.add))
            tbl(dve.tensor_scalar(stepi[:, :], stepi[:, :], 1, None, ALU.logical_shift_right))
            dve.tensor_scalar(table[:, :, C_END], stepi[:, :], 5, None, ALU.logical_shift_left)\
               .then_inc(s["table_ready"], 1)

            def xT(i, q):
                dve.wait_ge(s["xThi_ready"], i + 1)
                dve.tensor_tensor(xT_lo[:, q].rearrange("p k t -> p (k t)"), p_xT,
                                  xT_hi[:, q].bitcast(f32).rearrange("p k t -> p (k t)"), ALU.subtract)\
                   .then_inc(s["xTlo_ready"], 1)

            def h(i, part):
                cols = slice(part * HALF, (part + 1) * HALF)
                dve.wait_ge(s[f"silu{part}_done"], i + 1)
                if not isinstance(i, int) or i > 0:
                    dve.wait_ge(s[f"th{part}_done"], i)
                dve.tensor_tensor(hmul[:, cols], gact[:, cols], p_lin[part][:, :], ALU.mult)\
                   .then_inc(s[f"h{part}_done"], 1)

            def hT(i, q, part):
                ks = slice(part * KF // 2, (part + 1) * KF // 2)
                dve.wait_ge(s[f"hT{part}hi_ready"], i + 1)
                dve.tensor_tensor(hT_lo[:, q, ks].rearrange("p k t -> p (k t)"), p_hT[part][:, :],
                                  hT_hi[:, q, ks].bitcast(f32).rearrange("p k t -> p (k t)"), ALU.subtract)\
                   .then_inc(s[f"hT{part}lo_ready"], 1)

            def hold(q, half):
                dve.wait_ge(blk_in[q], 16 * (half + 1))
                dve.tensor_copy(held[:, q, :], xblk[:, q, D:ROW]).then_inc(s["held_ready"], 1)

            def meta(i, q, e):
                dve.wait_ge(s["held_ready"], i + 1)
                dve.wait_ge(s["added_rows"], OUT_INIT + 16 * (i - 1))
                dve.tensor_copy(wtok[:, q:q + 1], held[:, q, ds(e, 1)])
                dve.tensor_copy(itok[:, q:q + 1], held[:, q, E:E + 1]).then_inc(s["meta_ready"], 1)

            def step(i, q, half, word):
                later = not isinstance(i, int) or i > 0
                h(i, 0)
                if later:
                    hT(i - 1, 1 - q, 1)
                    meta(i - 1, 1 - q, expert_before(word))
                xT(i + 1, 1 - q)
                if later:
                    dve.wait_ge(s["meta_ready"], i)
                hold(1 - q, half + q)
                h(i, 1)
                hT(i, q, 0)
                with dve.If(word & F_CHUNK):
                    e = expert(word)
                    raw3 = ((e + 1) & 1) * 3
                    split_lo(dve, e + 1, raw3, chunk_of(word))
                    with dve.If(word & F_W2):
                        with dve.If(word & F_W3):
                            split_lo(dve, e + 1, raw3, 1)
                        split_lo(dve, e + 1, raw3, 2)

            dve.wait_ge(s["table_ready"], 1)
            dve.wait_ge(s["x1_rows"], 16 * B)
            xT(0, 0)
            hold(0, 0)
            over_steps(dve, step)

        @block.tensor
        def _(pe):
            def lengths():
                pe.wait_ge(s["consts"], 2)
                pe.wait_ge(s["scan_ready"], 1)
                pe.matmul(p_prefix, tri[:, :], ln_s[:, :, :, CH - 1].rearrange("p k b -> p (k b)"),
                          start=True, stop=True).then_inc(s["prefix_ready"], 1)
                for b in range(B):
                    pe.wait_ge(s["onehot_ready"], b + 2)
                    for k in range(CH):
                        mm = pe.matmul(p_count[:, b * TPB:(b + 1) * TPB], onehot_lo[:, b % 2, k, :],
                                       onehot_hi[:, b * CH + k, :], start=(k == 0), stop=(k == CH - 1))
                    mm.then_inc(s["count_ready"], 1)
                pe.wait_ge(s["bmask_ready"], 1)
                flat = bmask[:, :, :].rearrange("p b j -> p (b j)")
                pe.matmul(p_plug, tri[:, :], flat, start=True, stop=False)
                pe.matmul(p_plug, ident[:, :], flat, start=False, stop=False)
                for j in range(TPB - 1):
                    more = TPB - 1 - j
                    mm = pe.matmul(p_plug.rearrange("p (b j) -> p b j", j=TPB)[:, :, j + 1:TPB], ones[:, :],
                                   bmask[:, :, j:j + 1].broadcast_to([P, B, more]),
                                   start=False, stop=(j == TPB - 2))
                mm.then_inc(s["plugmm_ready"], 1)

            def transposes(src, j, signal):
                for k in range(KD):
                    mm = pe.transpose(pT[j // 2][:, (j % 2) * D + k * P:(j % 2) * D + (k + 1) * P],
                                      src[:, j, k * P:(k + 1) * P], ident[:, :])
                mm.then_inc(signal, 1)

            def first(b):
                if b == 1:
                    pe.wait_ge(s["hnT_ready"], PAIRS)
                elif b >= 2:
                    pe.wait_ge(s["zT_ready"], PAIRS * (b - 1))
                for j in range(TPB):
                    pe.wait_ge(s["hn_ready"], b * TPB + j + 1)
                    transposes(hn, j, s["tn_ready"])
                if b == 0:
                    pe.wait_ge(s["gw_ready"], KD)
                    pe.wait_ge(s["affine_step"], 6 + len(decay))
                if b >= 1:
                    pe.wait_ge(s["dep_ready"], PAIRS * b)
                for j in range(TPB):
                    pe.wait_ge(s["hp_ready"], b * TPB + j + 1)
                    acc = pD[j // 2][:, (j % 2) * D:(j % 2 + 1) * D]
                    mm = pe.matmul(acc, decayT[:, 0:P], hp[:, j, :], start=True, stop=(j == 0))
                    if j:
                        mm = pe.matmul(acc, decayT[:, P:2 * P], hp[:, j - 1, :], start=False, stop=True)
                    mm.then_inc(s["depmm_ready"], 1)

            def second(b):
                if b == 0:
                    pe.wait_ge(s["gw_ready"], KD)
                else:
                    pe.wait_ge(s["x1_ready"], PAIRS * b)
                for j in range(TPB):
                    pe.wait_ge(s["hnT_ready"], b * PAIRS + j // 2 + 1)
                    for k in range(KD):
                        mm = pe.matmul(pH[j // 2][:, (j % 2) * D:(j % 2 + 1) * D],
                                       hnT[b % 2][:, j, k * P:(k + 1) * P], win[:, k, :],
                                       start=(k == 0), stop=(k == KD - 1))
                    mm.then_inc(s["hmm_ready"], 1)
                pe.wait_ge(s["hnT_ready"], PAIRS * min(b + 2, B))
                for j in range(TPB):
                    pe.wait_ge(s["z_ready"], b * TPB + j + 1)
                    transposes(payload[:, b % 2], j, s["tz_ready"])
                if b >= 1:
                    pe.wait_ge(s["base_step"], 2 + b)
                for j in range(TPB):
                    pe.wait_ge(s["zT_ready"], b * PAIRS + j // 2 + 1)
                    for k in range(KD):
                        mm = pe.matmul(p_logit[:, j * E:(j + 1) * E], zT[:, j, k * P:(k + 1) * P], gate[:, k, :],
                                       start=(k == 0), stop=(k == KD - 1))
                mm.then_inc(s["logit_mm"], 1)
                pe.wait_ge(s["picked_ready"], b + 1)
                pe.matmul(p_rank, tri[:, :], picked[:, :, :].rearrange("p j e -> p (j e)"), start=True, stop=False)
                for j in range(TPB - 1):
                    more = TPB - 1 - j
                    pe.matmul(p_rank.rearrange("p (j e) -> p j e", e=E)[:, j + 1:TPB, :], ones[:, :],
                              picked[:, j:j + 1, :].broadcast_to([P, more, E]), start=False, stop=(j == TPB - 2))
                for j in range(TPB):
                    mm = pe.matmul(p_total, ones[:, :], picked[:, j, :], start=(j == 0), stop=(j == TPB - 1))
                mm.then_inc(s["rank_mm"], 1)

            lengths()
            pe.wait_ge(s["small_in"], 16 * 5)
            for k in range(KD):
                for m in range(KD):
                    mm = pe.transpose(p_win[:, k * D + m * P:k * D + (m + 1) * P], win[:, m, k * P:(k + 1) * P],
                                      ident[:, :])
            mm.then_inc(s["wT_ready"], 1)
            first(0)
            for b in range(B):
                if b + 1 < B:
                    first(b + 1)
                second(b)

            def three(acc, x_hi, x_lo, w_hi, w_lo, start, stop):
                for n, (xp, wp) in enumerate(((x_hi, w_hi), (x_hi, w_lo), (x_lo, w_hi))):
                    for out_, w_ in zip(acc, wp):
                        mm = pe.matmul(out_, xp, w_, start=start and n == 0, stop=stop and n == 2)
                return mm

            def xT(i, q, half):
                pe.wait_ge(blk_in[q], 16 * (half + 1))
                for k in range(KD):
                    mm = pe.transpose(p_xT[:, k * P:(k + 1) * P], xblk[:, q, k * P:(k + 1) * P], ident[:, :])
                mm.then_inc(s["xT_done"], 1)

            def up(e, q, part):
                def weights(t, k):
                    return [t[:, ds(e & 1, 1), m, k, part * HALF:(part + 1) * HALF].rearrange("p o f -> p (o f)")
                            for m in range(2)]
                for k in range(KD):
                    mm = three((p_gate[part][:, :], p_lin[part][:, :]), xT_hi[:, q, k, :], xT_lo[:, q, k, :],
                               weights(up_hi, k), weights(up_lo, k), k == 0, k == KD - 1)
                mm.then_inc(s[f"up{part}_done"], 1)

            def hT(i, part):
                pe.wait_ge(s[f"h{part}_done"], i + 1)
                for k in range(KF // 2):
                    f0 = (part * KF // 2 + k) * P
                    mm = pe.transpose(p_hT[part][:, k * P:(k + 1) * P], hmul[:, f0:f0 + P], ident[:, :])
                mm.then_inc(s[f"th{part}_done"], 1)

            def down(i, q, e):
                pe.wait_ge(s["hT1lo_ready"], i + 1)
                pe.wait_ge(s["lo_ready"], e * 3 + 3)
                for k in range(KF):
                    w_hi, w_lo = ([t[:, ds(e & 1, 1), k, :].rearrange("p o d -> p (o d)")] for t in (dn_hi, dn_lo))
                    mm = three((p_y,), hT_hi[:, q, k, :], hT_lo[:, q, k, :], w_hi, w_lo, k == 0, k == KF - 1)
                mm.then_inc(s["y_done"], 1)

            def step(i, q, half, word):
                later = not isinstance(i, int) or i > 0
                e = expert(word)
                pe.wait_ge(s["xTlo_ready"], i + 1)
                pe.wait_ge(s["lo_ready"], e * 3 + 2)
                if later:
                    pe.wait_ge(s["h0_done"], i)
                up(e, q, 0)
                if later:
                    hT(i - 1, 1)
                xT(i + 1, 1 - q, half + q)
                if later:
                    pe.wait_ge(s["h1_done"], i)
                up(e, q, 1)
                hT(i, 0)
                if later:
                    down(i - 1, 1 - q, expert_before(word))

            pe.wait_ge(s["table_ready"], 1)
            pe.wait_ge(s["posi_ready"], B)
            xT(0, 0, 0)
            over_steps(pe, step)


_INS = ["x", "ctx_2048", "mask_BxS2_if0", "L0_xattn_W_in", "L0_xattn_b_in", "L0_xattn_g_res", "L0_xattn_g_init",
        "L0_ffn_gate_w", "L0_ffn_w1", "L0_ffn_w3", "L0_ffn_w2"]


def kernel(**inputs):
    import numpy as _np
    import concourse.bacc as _bacc
    from concourse import mybir as _mybir
    from concourse.bass_utils import run_bass_kernel_spmd as _run

    nc = _bacc.Bacc("TRN2", target_bir_lowering=False, num_devices=1)
    arrays, args = {}, []
    for name in _INS:
        a = _np.ascontiguousarray(inputs[name])
        arrays[f"in_{name}"] = a
        args.append(nc.dram_tensor(f"in_{name}", a.shape, _mybir.dt.from_np(a.dtype), kind="ExternalInput").ap())
    args.append(nc.dram_tensor("out_0", (T + P, D), _mybir.dt.float32, kind="ExternalOutput").ap())
    build(nc, *args)
    r = _run(nc, [arrays], core_ids=[0])
    return r.results[0]["out_0"][0:T].reshape(B, S, D)
```

```python
import math
from contextlib import ExitStack

import numpy as np
import concourse.bass as bass
from concourse import mybir

P = 128
B, S, D = 4, 512, 256
S2, CD = 1601, 512
E, F = 8, 1024
T = B * S
TPB = S // P
PAIRS = TPB // 2
KD, KF = D // P, F // P
HALF = F // 2

EPS_LN, EPS_RMS, EPS_LOGP = 1e-5, 1e-5, 1e-3

BLOCKS = (2 * T + E * (P - 1) + E - 1) // P
assert BLOCKS == 39
STEP_PAIRS = BLOCKS // 2
TABLE = 1 + 2 * STEP_PAIRS + 3
PREV_BIT = 3
F_CHUNK, F_W2, F_W3, F_LOAD, F_RUN = (1 << n for n in range(6, 11))
CHUNK_BIT = 11
OUT_INIT = 32

CH = -(-S2 // P)
FULL = S2 // CH
RAW_SEM = 48


def build(nc, x, ctx, lens, w_in, b_in, g_res, g_init, gate_w, w1, w3, w2, out):
    f32, f32r, bf16 = mybir.dt.float32, mybir.dt.float32r, mybir.dt.bfloat16
    i32, u8, u32 = mybir.dt.int32, mybir.dt.uint8, mybir.dt.uint32
    ALU, ACT, AX = mybir.AluOpType, mybir.ActivationFunctionType, mybir.AxisListType
    ds = bass.ds

    logp = np.float32(-EPS_LOGP)
    dt = np.float32(-np.log(-np.expm1(logp)))
    a, c = float(np.exp(-dt)), float(np.exp(logp))
    decay = [c * a ** k for k in range(P) if c * a ** k >= float(np.finfo(np.float32).tiny)]

    stack = ExitStack()
    with stack:
        def sb(name, shape, dtype, on=stack):
            return on.enter_context(nc.sbuf_tensor(name, shape, dtype))

        def sem(name):
            return stack.enter_context(nc.semaphore(name))

        z_dram = nc.dram_tensor("z_rows", (T + P, D), f32, kind="Internal").ap()
        depool_dram = [nc.dram_tensor(f"depool_rows{b}", (S, D), f32, kind="Internal").ap() for b in range(B)]

        ident = sb("ident", [P, P], f32)
        tri = sb("tri", [P, P], f32)
        ones = sb("ones", [P, E], f32)
        tri_b, ones_b, ident_b = (sb(n, [P, P], bf16) for n in ("tri_b", "ones_b", "ident_b"))
        decayT = sb("decayT", [P, 2 * P], f32)
        iota_f = sb("iota_f", [P, P], f32)
        ids_f = sb("ids_f", [P, T // P + 1], f32)
        neg_half = sb("neg_half", [P, 2 * TPB], f32)
        win = sb("win", [P, KD, D], f32)
        gres = sb("gres", [P, KD], f32)
        gate = sb("gate", [P, KD, E], f32)
        ginit = sb("ginit", [P, D], f32)
        bin_ = sb("bin", [P, D], f32)
        zeros = sb("zeros", [P, D], f32)

        UP = 2 * KD * F
        RAW = UP + KF * D
        raw = sb("raw", [P, 2, RAW], f32)
        raw_up = raw[:, :, 0:UP].rearrange("p s (m k f) -> p s m k f", m=2, k=KD)
        raw_dn = raw[:, :, UP:RAW].rearrange("p s (k d) -> p s k d", k=KF)

        raw_chunk = raw[:, :, :].rearrange("p s (m c) -> p (s m) c", m=3)

        with ExitStack() as early:
            batch = sb("batch", [P, 4, TPB, D], f32, early)
            hn, hnT, zT = batch[:, 0], [batch[:, 1], batch[:, 2]], batch[:, 3]
            N_LIST = 2 * B * TPB
            lists = batch[:, :, :, :].rearrange("p n j d -> p (n j d)").bitcast(bf16)
            hi_idx, hi_w = (lists[:, a:a + N_LIST * v * TABLE].rearrange("p (n v c) -> p n v c", v=v, c=TABLE)
                            for a, v in ((0, 2), (N_LIST * 2 * TABLE, 3)))
        hT = sb("hT", [P, 2, 2, KF, P], f32r)
        hT_hi, hT_lo = hT[:, 0], hT[:, 1]
        gact = sb("gact", [P, F], f32)
        hmul = sb("hmul", [P, F], f32)
        dep, hp = (t[:, :].rearrange("p (j d) -> p j d", d=D) for t in (gact, hmul))

        with ExitStack() as early:
            sb("first_slot", [P, 2, RAW], f32, early)
            x_all = sb("x_all", [P, B * TPB, D], f32, early)
            ctx_sb = sb("ctx_sb", [P, 2, TPB, CD], f32, early)
            z = sb("z", [P, 2, TPB, D], f32, early)
            onehot_lo = sb("onehot_lo", [P, 2, CH, P], bf16, early)
            lo_hot = ctx_sb[:, :, :, :].rearrange("p q j d -> p (q j d)")[:, 0:N_LIST * P // 2].bitcast(bf16)\
                .rearrange("p (n c) -> p n c", c=P)
            early_rows = onehot_lo[:, :, :, :].rearrange("p q k t -> p (q k t)")
            hi_eq = early_rows[:, 0:N_LIST * TABLE].rearrange("p (n c) -> p n c", c=TABLE)
            startm = early_rows[:, N_LIST * TABLE:N_LIST * (TABLE + 2 * E)].bitcast(f32)\
                .rearrange("p (n e) -> p n e", e=E)
        split = sb("split", [P, 2, 2, RAW], f32r)
        up_hi, up_lo = (split[:, :, n, 0:UP].rearrange("p s (m k f) -> p s m k f", m=2, k=KD) for n in range(2))
        split_chunk = split[:, :, :, :].rearrange("p s n (m c) -> p (s n m) c", m=3)
        dn_hi, dn_lo = (split[:, :, n, UP:RAW].rearrange("p s (k d) -> p s k d", k=KF) for n in range(2))

        iota_m8 = sb("iota_m8", [P, TPB], f32)
        sumsq = sb("sumsq", [P, 2, TPB], f32)
        st1 = sb("st1", [P, TPB, 6], f32)
        mv1 = sb("mv1", [P, TPB, 2], f32)
        vin = sb("vin", [P, 2 * TPB], f32)
        rs = sb("rs", [P, 2, 2 * TPB], f32)
        nb1 = sb("nb1", [P, TPB], f32)
        st2 = sb("st2", [P, TPB, 6], f32)
        mv2 = sb("mv2", [P, TPB, 2], f32)
        vin2 = sb("vin2", [P, TPB], f32)
        rs2 = sb("rs2", [P, TPB], f32)
        nb2 = sb("nb2", [P, TPB], f32)
        logits = sb("logits", [P, TPB, E], f32)
        top = sb("top", [P, TPB, 8], f32)
        topi = sb("topi", [P, TPB, 8], u32)
        topf = sb("topf", [P, 2, TPB], f32)
        oh = sb("oh", [P, 2, B * TPB, E], f32)
        picked = sb("picked", [P, TPB, E], bf16)
        gap = sb("gap", [P, TPB], f32)
        egap = sb("egap", [P, TPB], f32)
        den = sb("den", [P, TPB], f32)
        wts = sb("wts", [P, 2, B * TPB], f32)
        base = sb("base", [P, E], f32)
        posf = sb("posf", [P, TPB, E], f32)
        posm = sb("posm", [P, 2, TPB, E], f32)
        rank = sb("rank", [P, 2, B * TPB], i32)
        rank_lo = sb("rank_lo", [P, 2, B * TPB], i32)
        rank_hi = sb("rank_hi", [P, 2, B * TPB], i32)
        blk = sb("blk", [P, 2, B * TPB], f32)
        number = sb("number", [P, TABLE], f32)
        unused = sb("unused", [P, TABLE], f32)
        tiles_b = sb("tiles_b", [P, 2 * B * TPB], bf16)
        w_parts = sb("w_parts", [P, 3, 2 * B * TPB], bf16)
        w_rest = sb("w_rest", [P, 2, 2 * B * TPB], f32)
        idx_all = sb("idx_all", [P, TABLE], i32)
        w_all = sb("w_all", [P, TABLE], f32)

        NBC = B * CH
        with ExitStack() as early:
            ln_i = sb("ln_i", [P, B, CH], i32, early)
            ln_f = sb("ln_f", [P, 4, B, CH], f32, early)
            keep = sb("keep", [P, 4 * NBC], f32, early)
            ln_s = sb("ln_s", [P, 4, B, CH], f32, early)
            ln_c = sb("ln_c", [P, 4, NBC], i32, early)
            ln_t = sb("ln_t", [P, NBC], i32, early)
            ln_b = sb("ln_b", [P, 4, NBC], i32, early)
            ln_v = sb("ln_v", [P, 8, NBC], f32, early)
            ln_p = sb("ln_p", [P, 3, NBC], i32, early)
        dg = sb("dg", [P, 2, TPB, D], f32)
        onehot_hi = sb("onehot_hi", [P, NBC, TPB], bf16)
        bmask = sb("bmask", [P, B, TPB], bf16)
        plugf = sb("plugf", [P, B, TPB], f32)
        plugi = sb("plugi", [P, B * TPB], i32)

        n_i = sb("n_i", [P, E], i32)
        nblk = sb("nblk", [P, E], f32)
        cum = sb("cum", [P, E], f32)
        start = sb("start", [P, E], f32)
        stepm = sb("stepm", [P, 4, E], f32)
        steps = sb("steps", [P, 4], f32)
        low = sb("low", [P, 4], f32)
        fields = sb("fields", [P, 8], f32)
        weights = sb("weights", [P, 8], f32)
        word = sb("word", [P, 1], f32)
        table = sb("table", [1, TABLE], i32)
        blocks_i = sb("blocks_i", [1, 1], i32)
        gidx = sb("gidx", [P, 2], i32)
        wtok = sb("wtok", [P, 2], f32)
        itok = sb("itok", [P, 2], i32)

        xblk = sb("xblk", [P, 2, D], f32)
        xT_hi = sb("xT_hi", [P, 2, KD, P], f32r)
        xT_lo = sb("xT_lo", [P, 2, KD, P], f32r)
        yblk = sb("yblk", [P, 2, D], f32)
        iota_i = yblk[:, 0, 0:P].bitcast(i32)
        ids_i = yblk[:, 1, 0:T // P + 1].bitcast(i32)

        bank = [stack.enter_context(nc.psum_tensor(f"bank{n}", [P, HALF], f32)) for n in range(8)]
        pT, pH, pD = bank[0:2], bank[2:4], bank[4:6]
        p_logit = bank[6][:, 0:TPB * E]
        p_rank = bank[6][:, 64:64 + TPB * E]
        p_total = bank[6][:, 128:128 + E]
        p_prefix = bank[7][:, 0:4 * B]
        p_count = bank[7][:, 64:64 + B * TPB]
        p_plug = bank[7][:, 128:128 + B * TPB]
        p_idx = bank[7][:, 256:256 + 2 * TABLE]
        p_w = bank[5][:, 0:3 * TABLE]
        p_word = bank[4][0:1, 0:TABLE]
        p_win = bank[2]
        p_gate, p_lin = [bank[0], bank[2]], [bank[1], bank[3]]
        p_hT = bank[4:6]
        p_xT = bank[6][:, 0:D]
        p_y = bank[7][:, 0:D]

        names = """lens_in small_in consts keep_ready bytes_ready iota_ready wT_ready scan_ready prefix_ready
            carry_step onehot_ready count_ready bmask_ready plugmm_ready plug_ready gw_ready pad_ready
            ids_ready base_step affine_step sq_ready st1_ready mv1_ready vin_ready rs_ready nb1_ready
            hn_ready tn_ready hnT_ready hp_ready depmm_ready dep_ready hmm_ready xd_ready x1_ready
            st2_ready mv2_ready vin2_ready rs2_ready nb2_ready z_ready tz_ready zT_ready logit_mm
            logit_ready top_ready topi_ready topf_ready gap_ready egap_ready den_ready
            wts_ready oh_ready picked_ready rank_mm posf_ready posm_ready rank_ready
            lohot_ready hi_step tile_step part_step list_mm idx_step fields_ready word_ready word_mm
            blocks_ready bf16_ready idx_ready z_rows tbl_step table_ready
            raw_first raw_ready hi_ready lo_first lo_ready x1_rows added_rows
            up0_done up1_done silu0_done silu1_done h0_done h1_done th0_done th1_done
            hT0hi_ready hT0lo_ready hT1hi_ready hT1lo_ready xT_done xThi_ready xTlo_ready
            gidx_ready meta_ready y_done y_ready settled_pool settled_sp""".split()
        s = {n: sem(n) for n in names}
        x_in = [sem(f"x_in{b}") for b in range(B)]
        ctx_in = [sem(f"ctx_in{b}") for b in range(B)]
        dep_rows = [sem(f"dep_rows{b}") for b in range(B)]
        dg_in = [sem(f"dg_in{b}") for b in range(B)]
        z_out = [sem(f"z_out{b}") for b in range(B)]
        blk_in = [sem(f"blk_in{q}") for q in range(2)]

        block = stack.enter_context(nc.Block())

        def pair(t, n):
            return t[:, 2 * n:2 * n + 2, :].rearrange("p j d -> p (j d)")

        def raw_load(eng, e, slot, signal, parts=(0, 1, 2)):
            for m in parts:
                to = raw_dn[:, ds(slot, 1)] if m == 2 else raw_up[:, ds(slot, 1), m]
                eng.dma_start(to, (w1, w3, w2)[m][ds(e, 1)].rearrange("o (k p) n -> p (o k) n", p=P))\
                   .then_inc(signal, 16)

        def step_word(eng, i):
            entry, top = table[0:1, ds(i, 1)], (3 << CHUNK_BIT) - 1
            if eng is nc.tensor:
                return eng.value_load(entry).with_bounds(min_val=0, max_val=top)
            return eng.value_load(entry, min_val=0, max_val=top)

        def expert(word):
            return word & (E - 1)

        def chunk_of(word):
            return (word >> CHUNK_BIT).with_bounds(min_val=0, max_val=2)

        def expert_before(word):
            return (word >> PREV_BIT) & (E - 1)

        def settle(eng):
            eng.sem_inc(s[f"settled_{'pool' if eng is nc.gpsimd else 'sp'}"], 1)

        def over_steps(eng, body):
            body(0, 0, 0, step_word(eng, 0))
            with eng.Fori(0, STEP_PAIRS) as pair:
                word = step_word(eng, pair * 2 + 1)
                with eng.If(word & F_RUN):
                    body(pair * 2 + 1, 1, pair, word)
                    word = step_word(eng, pair * 2 + 2)
                    with eng.If(word & F_RUN):
                        body(pair * 2 + 2, 0, pair + 1, word)

        def block_count(eng):
            eng.wait_ge(s["blocks_ready"], 1)
            return eng.value_load(blocks_i[:, :], min_val=E, max_val=BLOCKS)

        def at_end(eng, blocks, drain):
            with eng.If(blocks & 1):
                drain(blocks - 1, 0)
            with eng.If((blocks + 1) & 1):
                drain(blocks - 1, 1)

        def split_hi(act, raw3, m):
            act.activation(split_chunk[:, ds(raw3 * 2 + m, 1)], raw_chunk[:, ds(raw3 + m, 1)], ACT.Copy)\
               .then_inc(s["hi_ready"], 1)

        def split_lo(dve, e, raw3, m, signal="lo_ready"):
            dve.wait_ge(s["hi_ready"], e * 3 + m + 1)
            dve.tensor_tensor(split_chunk[:, ds(raw3 * 2 + m + 3, 1)], raw_chunk[:, ds(raw3 + m, 1)],
                              split_chunk[:, ds(raw3 * 2 + m, 1)].bitcast(f32), ALU.subtract)\
               .then_inc(s[signal], 1)

        @block.sync
        def _(sp):
            sp.wait_ge(s["keep_ready"], 1)
            sp.dma_start(ln_i[0:FULL, :, :], lens[:, 0:FULL * CH].rearrange("b (p c) -> p b c", c=CH))\
              .then_inc(s["lens_in"], 16)
            sp.dma_start(ln_i[FULL:FULL + 1, :, 0:S2 - FULL * CH],
                         lens[:, FULL * CH:S2].unsqueeze(0)).then_inc(s["lens_in"], 16)

            def load_ctx(b):
                sp.dma_start(ctx_sb[:, b % 2], ctx[b, 0:S, :].rearrange("(j p) d -> p j d", p=P))\
                  .then_inc(ctx_in[b], 16)

            def load_x(b):
                sp.dma_start(x_all[:, b * TPB:(b + 1) * TPB, :], x[b].rearrange("(j p) d -> p j d", p=P))\
                  .then_inc(x_in[b], 16)

            load_x(0)
            load_ctx(0)
            sp.dma_start(ginit[:, :], g_init[0:D].unsqueeze(0).broadcast_to([P, D])).then_inc(s["small_in"], 16)
            sp.dma_start(bin_[:, :], b_in.unsqueeze(0).broadcast_to([P, D])).then_inc(s["small_in"], 16)
            sp.dma_start(win[:, :, :], w_in.rearrange("(k p) n -> p k n", p=P)).then_inc(s["small_in"], 16)
            with nc.allow_non_contiguous_dma(reason="256 elements"):
                sp.dma_start(gres[:, :], g_res.rearrange("(k p) -> p k", p=P)).then_inc(s["small_in"], 16)
            sp.dma_start(gate[:, :, :], gate_w.rearrange("(k p) n -> p k n", p=P)).then_inc(s["small_in"], 16)
            load_x(1)
            load_ctx(1)
            load_x(2)
            load_x(3)
            sp.wait_ge(s["pad_ready"], 1)
            sp.dma_start(z_dram[T:T + P, :], zeros[:, :]).then_inc(s["z_rows"], 16)

            parts = [(e, m) for e in range(2) for m in range(3)]
            for k in range(B + 2):
                if k >= 2:
                    b = k - 2
                    sp.wait_ge(s["x1_ready"], PAIRS * (b + 1))
                    sp.dma_start(out[b * S:(b + 1) * S, :].rearrange("(j p) d -> p j d", p=P),
                                 x_all[:, b * TPB:(b + 1) * TPB, :]).then_inc(s["x1_rows"], 16)
                if k + 2 < B:
                    sp.wait_ge(s["hp_ready"], TPB * (k + 1))
                    sp.wait_ge(s["sq_ready"], TPB * (k + 1))
                    load_ctx(k + 2)
                if k < B:
                    sp.wait_ge(s["dep_ready"], PAIRS * (k + 1))
                    sp.dma_start(depool_dram[k].rearrange("(j p) d -> p j d", p=P), dep)\
                      .then_inc(dep_rows[k], 16)
                if k >= 2:
                    sp.wait_ge(s["z_ready"], TPB * (b + 1))
                    sp.dma_start(z_dram[b * S:(b + 1) * S, :].rearrange("(j p) d -> p j d", p=P), z[:, b % 2])\
                      .then_inc(z_out[b], 16)
                for e, m in parts[max(k - 1, 0):k] if k < B + 1 else parts[k - 1:]:
                    raw_load(sp, e, e, s["raw_ready"] if e else s["raw_first"], (m,))

            sp.wait_ge(s["lo_first"], 3)
            sp.wait_ge(s["raw_ready"], RAW_SEM)
            sp.wait_ge(s["xT_done"], 1)
            raw_load(sp, 2, 0, s["raw_ready"])
            sp.wait_ge(s["table_ready"], 1)

            def step(i, q, half, word):
                with sp.If(word & F_LOAD):
                    e = expert(word).with_bounds(min_val=0, max_val=E - 4)
                    sp.wait_ge(s["lo_ready"], e * 3 + 6)
                    settle(sp)
                    sp.wait_ge(s["raw_ready"], RAW_SEM * (e + 2))
                    settle(sp)
                    raw_load(sp, e + 3, (e + 1) & 1, s["raw_ready"])

            over_steps(sp, step)

        @block.gpsimd
        def _(pool):
            pool.memset(ident[:, :], 0.0).then_inc(s["affine_step"], 1)
            pool.memset(tri[:, :], 1.0).then_inc(s["affine_step"], 1)
            pool.memset(decayT[:, :], 0.0).then_inc(s["affine_step"], 1)
            pool.iota(iota_i, pattern=[[1, P]], base=0, channel_multiplier=0).then_inc(s["affine_step"], 1)
            pool.iota(ids_i, pattern=[[P, T // P + 1]], base=1, channel_multiplier=1)\
                .then_inc(s["affine_step"], 1)
            pool.memset(neg_half[:, :], -0.5).then_inc(s["affine_step"], 1)
            pool.wait_ge(s["affine_step"], 6)
            pool.affine_select(out=ident[:, :], in_=ident[:, :], compare_op=ALU.not_equal, fill=1.0,
                               base=0, pattern=[[-1, P]], channel_multiplier=1).then_inc(s["consts"], 1)
            pool.affine_select(out=tri[:, :], in_=tri[:, :], compare_op=ALU.is_gt, fill=0.0,
                               base=0, pattern=[[1, P]], channel_multiplier=-1).then_inc(s["consts"], 1)
            for k, v in enumerate(decay):
                if k:
                    pool.wait_ge(s["affine_step"], 6 + k)
                pool.affine_select(out=decayT[:, :], in_=decayT[:, :], compare_op=ALU.not_equal, fill=v,
                                   base=-k, pattern=[[1, 2 * P]], channel_multiplier=-1)\
                    .then_inc(s["affine_step"], 1)

            def pad_out():
                pool.wait_ge(s["pad_ready"], 1)
                for n in range(2):
                    pool.dma_start(out[T + n * P // 2:T + (n + 1) * P // 2, :], zeros[0:P // 2, :])\
                        .then_inc(s["added_rows"], OUT_INIT // 2)

            def pow1(b):
                pool.wait_ge(s["vin_ready"], 2 * (b + 1))
                pool.tensor_tensor(rs[:, b % 2], vin[:, :], neg_half[:, :], ALU.pow).then_inc(s["rs_ready"], 1)

            def gather(b):
                pool.wait_ge(s["plug_ready"], 1)
                pool.wait_ge(dep_rows[b], 16)
                if b >= 2:
                    pool.wait_ge(s["xd_ready"], b - 1)
                for j in range(TPB):
                    n = b * TPB + j
                    pool.indirect_dma_start(dg[:, b % 2, j, :], None, depool_dram[b][:, :],
                                            bass.IndirectOffsetOnAxis(ap=plugi[:, n:n + 1], axis=0))\
                        .then_inc(dg_in[b], 16)

            def pow2(b):
                pool.wait_ge(s["vin2_ready"], b + 1)
                pool.tensor_tensor(rs2[:, :], vin2[:, :], neg_half[:, 0:TPB], ALU.pow)\
                    .then_inc(s["rs2_ready"], 1)

            for k in range(B + 2):
                if k < B:
                    pow1(k)
                if k == 0:
                    pad_out()
                if 1 <= k <= B:
                    gather(k - 1)
                if k >= 2:
                    pow2(k - 2)

            split_lo(pool, 0, 0, 0, "lo_first")
            split_lo(pool, 0, 0, 1, "lo_first")

            pool.wait_ge(s["hi_step"], 1)
            pool.wait_ge(s["bf16_ready"], 14)
            half = slice(0, B * TPB)
            pool.tensor_tensor(hi_idx[:, half, 1, :], hi_eq[:, half, :],
                               tiles_b[:, half].unsqueeze(2).broadcast_to([P, B * TPB, TABLE]), ALU.mult)\
                .then_inc(s["tile_step"], 1)
            split_lo(pool, 0, 0, 2, "lo_first")

            def block_rows(i, q):
                pool.wait_ge(s["gidx_ready"], i + 1)
                settle(pool)
                pool.indirect_dma_start(xblk[:, q, :], None, z_dram[:, :],
                                        bass.IndirectOffsetOnAxis(ap=gidx[:, q:q + 1], axis=0))\
                    .then_inc(blk_in[q], 16)

            def add_rows(i, q):
                pool.wait_ge(s["y_ready"], i + 2)
                pool.wait_ge(s["added_rows"], OUT_INIT + 16 * i)
                settle(pool)
                pool.indirect_dma_start(out[:, :], bass.IndirectOffsetOnAxis(ap=itok[:, q:q + 1], axis=0),
                                        yblk[:, q, :], None, compute_op=ALU.add).then_inc(s["added_rows"], 16)

            pool.wait_ge(s["z_rows"], 16)
            for b in range(B):
                pool.wait_ge(z_out[b], 16)
            pool.wait_ge(s["sq_ready"], B * TPB)
            block_rows(0, 0)
            block_rows(1, 1)
            blocks = block_count(pool)
            pool.wait_ge(s["table_ready"], 1)
            pool.wait_ge(s["xT_done"], 1)
            block_rows(2, 0)
            pool.wait_ge(s["x1_rows"], 16 * B)

            def step(i, q):
                pool.wait_ge(s["xT_done"], i + 2)
                block_rows(i + 3, 1 - q)
                if not isinstance(i, int):
                    add_rows(i - 1, 1 - q)

            step(0, 0)
            with pool.Fori(0, STEP_PAIRS) as pair:
                with pool.If(step_word(pool, pair * 2 + 1) & F_RUN):
                    step(pair * 2 + 1, 1)
                    with pool.If(step_word(pool, pair * 2 + 2) & F_RUN):
                        step(pair * 2 + 2, 0)
            at_end(pool, blocks, add_rows)
            pool.wait_ge(s["added_rows"], OUT_INIT + blocks * 16)
            settle(pool)
            for q in range(2):
                pool.wait_ge(blk_in[q], ((blocks + 4 - q) >> 1) * 16)
                settle(pool)

        @block.scalar
        def _(act):
            def squares(b):
                act.wait_ge(ctx_in[b], 16)
                for j in range(TPB):
                    n = b * TPB + j
                    if n >= 2:
                        act.wait_ge(s["sq_ready"], n - 1)
                    act.activation(xblk[:, n % 2, :].bitcast(bf16), ctx_sb[:, b % 2, j, :], ACT.Square,
                                   accum_out=sumsq[:, b % 2, j:j + 1]).then_inc(s["sq_ready"], 1)

            def norm_first(b):
                act.wait_ge(s["nb1_ready"], b + 1)
                for j in range(TPB):
                    if b >= 1:
                        act.wait_ge(s["tn_ready"], TPB * b)
                    act.activation(hn[:, j, :], x_all[:, b * TPB + j, :], ACT.Identity,
                                   scale=rs[:, b % 2, TPB + j:TPB + j + 1], bias=nb1[:, j:j + 1])\
                       .then_inc(s["hn_ready"], 1)

            def transposed_first(b):
                if b >= 2:
                    act.wait_ge(s["hmm_ready"], TPB * (b - 1))
                for n in range(PAIRS):
                    act.wait_ge(s["tn_ready"], b * TPB + 2 * n + 2)
                    act.activation(pair(hnT[b % 2], n), pT[n][:, :], ACT.Copy)\
                       .then_inc(s["hnT_ready"], 1)

            def norm_second(b):
                act.wait_ge(s["nb2_ready"], b + 1)
                if b >= 2:
                    act.wait_ge(z_out[b - 2], 16)
                    act.wait_ge(s["tz_ready"], TPB * (b - 1))
                for j in range(TPB):
                    act.activation(z[:, b % 2, j, :], x_all[:, b * TPB + j, :], ACT.Identity,
                                   scale=rs2[:, j:j + 1], bias=nb2[:, j:j + 1]).then_inc(s["z_ready"], 1)

            def transposed_second(b):
                if b >= 1:
                    act.wait_ge(s["logit_mm"], b)
                for n in range(PAIRS):
                    act.wait_ge(s["tz_ready"], b * TPB + 2 * n + 2)
                    act.activation(pair(zT, n), pT[n][:, :], ACT.Copy)\
                       .then_inc(s["zT_ready"], 1)

            def exp_gap(b):
                act.wait_ge(s["gap_ready"], b + 1)
                act.activation(egap[:, :], gap[:, :], ACT.Exp).then_inc(s["egap_ready"], 1)

            squares(0)
            for k in range(B + 3):
                if k < B:
                    norm_first(k)
                if k + 1 < B:
                    squares(k + 1)
                if 3 <= k <= B:
                    exp_gap(k - 3)
                if 2 <= k < B + 2:
                    norm_second(k - 2)
                if k < B:
                    transposed_first(k)
                if k == B:
                    act.wait_ge(s["raw_first"], RAW_SEM)
                    split_hi(act, 0, 0)
                if 2 <= k < B + 2:
                    transposed_second(k - 2)
                if k == B + 1:
                    exp_gap(k - 3)
                    split_hi(act, 0, 1)
                if k == B + 2:
                    exp_gap(k - 3)
            split_hi(act, 0, 2)

            act.wait_ge(s["table_ready"], 1)
            act.wait_ge(s["x1_rows"], 16 * B)
            for b in range(B):
                act.wait_ge(z_out[b], 16)

            def xT(i, q):
                act.wait_ge(s["xT_done"], i + 1)
                act.activation(xT_hi[:, q], p_xT, ACT.Copy).then_inc(s["xThi_ready"], 1)

            def hT(i, q, half):
                act.wait_ge(s[f"th{half}_done"], i + 1)
                act.activation(hT_hi[:, q, half * KF // 2:(half + 1) * KF // 2], p_hT[half][:, :], ACT.Copy)\
                   .then_inc(s[f"hT{half}hi_ready"], 1)

            def silu(i, half):
                act.wait_ge(s[f"up{half}_done"], i + 1)
                act.activation(gact[:, half * HALF:(half + 1) * HALF], p_gate[half][:, :], ACT.Silu)\
                   .then_inc(s[f"silu{half}_done"], 1)

            def y(i, q):
                act.wait_ge(s["y_done"], i + 1)
                act.wait_ge(s["added_rows"], OUT_INIT + 16 * (i - 1))
                act.wait_ge(s["meta_ready"], i + 1)
                act.activation(yblk[:, q, :], p_y, ACT.Copy, scale=wtok[:, q:q + 1]).then_inc(s["y_ready"], 1)

            def step(i, q, half, word):
                later = not isinstance(i, int) or i > 0
                silu(i, 0)
                if later:
                    hT(i - 1, 1 - q, 1)
                xT(i + 1, 1 - q)
                silu(i, 1)
                hT(i, q, 0)
                with act.If(word & F_CHUNK):
                    e = expert(word)
                    act.wait_ge(s["raw_ready"], RAW_SEM * (e + 1))
                    raw3 = ((e + 1) & 1) * 3
                    split_hi(act, raw3, chunk_of(word))
                    with act.If(word & F_W2):
                        with act.If(word & F_W3):
                            split_hi(act, raw3, 1)
                        if later:
                            act.wait_ge(s["y_done"], i)
                        split_hi(act, raw3, 2)
                if later:
                    y(i - 1, 1 - q)

            def drain(i, q):
                hT(i, q, 1)
                y(i, q)

            act.sem_inc(s["y_ready"], 1)
            blocks = block_count(act)
            xT(0, 0)
            over_steps(act, step)
            at_end(act, blocks, drain)

        @block.vector
        def _(dve):
            dve.memset(ln_i[:, :, :], 0).then_inc(s["keep_ready"], 1)
            dve.memset(keep[:, :], 1.0).then_inc(s["keep_ready"], 1)
            dve.wait_ge(s["keep_ready"], 2)
            dve.memset(keep[:, :].rearrange("p (n c) -> p n c", c=CH)[:, :, 0:1], 0.0).then_inc(s["keep_ready"], 1)
            dve.memset(zeros[:, :], 0.0).then_inc(s["pad_ready"], 1)
            dve.memset(base[:, :], 0.0).then_inc(s["base_step"], 1)
            dve.memset(ones[:, :], 1.0).then_inc(s["bf16_ready"], 1)
            dve.memset(ones_b[:, :], 1.0).then_inc(s["bf16_ready"], 1)
            dve.wait_ge(s["affine_step"], 5)
            dve.tensor_copy(iota_f[:, :], iota_i).then_inc(s["iota_ready"], 1)
            dve.tensor_copy(ids_f[:, :], ids_i).then_inc(s["ids_ready"], 1)
            dve.wait_ge(s["iota_ready"], 1)
            dve.tensor_scalar(iota_m8[:, :], iota_f[:, 0:TPB], -8.0, None, ALU.add).then_inc(s["iota_ready"], 1)

            for n, value in enumerate((1, 1 << PREV_BIT, F_CHUNK, F_W2, F_W3, F_LOAD, F_RUN, 1 << CHUNK_BIT)):
                dve.memset(weights[:, n:n + 1], float(value)).then_inc(s["bf16_ready"], 1)
            dve.wait_ge(s["consts"], 2)
            dve.tensor_copy(tri_b[:, :], tri[:, :]).then_inc(s["bf16_ready"], 1)
            dve.tensor_copy(ident_b[:, :], ident[:, :]).then_inc(s["bf16_ready"], 1)
            for r in range(2):
                dve.tensor_copy(tiles_b[:, r * B * TPB:(r + 1) * B * TPB], iota_f[:, 0:B * TPB])\
                   .then_inc(s["bf16_ready"], 1)

            low, high, lowok, lowneg, ok0, ok1, ok, hif = (ln_v[:, n_, :] for n_ in range(8))

            def lengths():
                dve.wait_ge(s["lens_in"], 32)
                dve.wait_ge(s["keep_ready"], 3)
                dve.tensor_copy(ln_f[:, :, :, :], ln_i[:, :, :].bitcast(u8).rearrange("p b (c k) -> p k b c", k=4))\
                   .then_inc(s["bytes_ready"], 1)
                dve.wait_ge(s["bytes_ready"], 1)
                dve.tensor_tensor_scan(ln_s[:, :, :, :].rearrange("p k b c -> p (k b c)"), keep[:, :],
                                       ln_f[:, :, :, :].rearrange("p k b c -> p (k b c)"), 0.0, ALU.mult, ALU.add)\
                   .then_inc(s["scan_ready"], 1)
                dve.wait_ge(s["prefix_ready"], 1)
                dve.tensor_tensor(ln_c[:, :, :].rearrange("p k (b c) -> p (k b) c", c=CH),
                                  ln_s[:, :, :, :].rearrange("p k b c -> p (k b) c"),
                                  p_prefix.unsqueeze(2).broadcast_to([P, 4 * B, CH]), ALU.add)\
                   .then_inc(s["carry_step"], 1)
                n = 1
                for k in range(4):
                    dve.wait_ge(s["carry_step"], n)
                    dve.tensor_scalar(ln_b[:, k, :], ln_c[:, k, :], 255, None, ALU.bitwise_and)\
                       .then_inc(s["carry_step"], 1)
                    n += 1
                    if k < 3:
                        dve.tensor_scalar(ln_t[:, :], ln_c[:, k, :], 8, None, ALU.logical_shift_right)\
                           .then_inc(s["carry_step"], 1)
                        dve.wait_ge(s["carry_step"], n + 1)
                        dve.tensor_tensor(ln_c[:, k + 1, :], ln_c[:, k + 1, :], ln_t[:, :], ALU.add)\
                           .then_inc(s["carry_step"], 1)
                        n += 2
                idx, lo_i, hi_i = (ln_p[:, n_, :] for n_ in range(3))
                dve.wait_ge(s["carry_step"], n)
                dve.scalar_tensor_tensor(low, ln_b[:, 1, :], 256.0, ln_b[:, 0, :], ALU.mult, ALU.add)\
                   .then_inc(s["carry_step"], 1)
                dve.scalar_tensor_tensor(high, ln_b[:, 3, :], 256.0, ln_b[:, 2, :], ALU.mult, ALU.add)\
                   .then_inc(s["carry_step"], 1)
                dve.wait_ge(s["carry_step"], n + 2)
                dve.tensor_scalar(lowok, low, float(S), None, ALU.is_le).then_inc(s["carry_step"], 1)
                dve.tensor_scalar(lowneg, low, float(65536 + 1 - S), None, ALU.is_ge).then_inc(s["carry_step"], 1)
                dve.tensor_scalar(idx, low, float(S - 1), None, ALU.add).then_inc(s["carry_step"], 1)
                dve.wait_ge(s["carry_step"], n + 5)
                dve.scalar_tensor_tensor(ok0, high, 0.0, lowok, ALU.is_equal, ALU.mult).then_inc(s["carry_step"], 1)
                dve.scalar_tensor_tensor(ok1, high, 65535.0, lowneg, ALU.is_equal, ALU.mult)\
                   .then_inc(s["carry_step"], 1)
                dve.tensor_scalar(lo_i, idx, P - 1, None, ALU.bitwise_and).then_inc(s["carry_step"], 1)
                dve.tensor_scalar(hi_i, idx, 7, TPB - 1, ALU.logical_shift_right, ALU.bitwise_and)\
                   .then_inc(s["carry_step"], 1)
                dve.wait_ge(s["carry_step"], n + 9)
                dve.tensor_tensor(ok, ok0, ok1, ALU.add).then_inc(s["carry_step"], 1)
                dve.tensor_copy(low, lo_i).then_inc(s["carry_step"], 1)
                dve.wait_ge(s["carry_step"], n + 11)
                dve.scalar_tensor_tensor(hif, ok, -8.0, hi_i, ALU.mult, ALU.add).then_inc(s["carry_step"], 1)
                dve.wait_ge(s["carry_step"], n + 12)
                dve.wait_ge(s["iota_ready"], 2)
                dve.tensor_tensor(onehot_hi[:, :, :], iota_m8[:, :].unsqueeze(1).broadcast_to([P, NBC, TPB]),
                                  hif.unsqueeze(2).broadcast_to([P, NBC, TPB]), ALU.is_equal)\
                   .then_inc(s["onehot_ready"], 1)

            def position(b):
                if b >= 2:
                    dve.wait_ge(s["count_ready"], b - 1)
                dve.tensor_tensor(onehot_lo[:, b % 2], iota_f[:, :].unsqueeze(1).broadcast_to([P, CH, P]),
                                  low[:, b * CH:(b + 1) * CH].unsqueeze(2).broadcast_to([P, CH, P]),
                                  ALU.is_equal).then_inc(s["onehot_ready"], 1)

            def plugs():
                dve.wait_ge(s["count_ready"], B)
                dve.tensor_scalar(bmask[:, :, :].rearrange("p b j -> p (b j)"), p_count, 0.5, None, ALU.is_gt)\
                   .then_inc(s["bmask_ready"], 1)

            def plugs_end():
                dve.wait_ge(s["plugmm_ready"], 1)
                dve.tensor_scalar(plugf[:, :, :].rearrange("p b j -> p (b j)"), p_plug, -1.0, 0.0, ALU.add, ALU.max)\
                   .then_inc(s["bmask_ready"], 1)
                dve.wait_ge(s["bmask_ready"], 2)
                dve.tensor_scalar(plugi[:, :], plugf[:, :, :].rearrange("p b j -> p (b j)"), float(S2 - 1), None,
                                  ALU.min).then_inc(s["plug_ready"], 1)

            def stats_first(b):
                dve.wait_ge(x_in[b], 16)
                for j in range(TPB):
                    dve.bn_stats(st1[:, j, :], x_all[:, b * TPB + j, :]).then_inc(s["st1_ready"], 1)
                dve.wait_ge(s["st1_ready"], TPB * (b + 1))
                for j in range(TPB):
                    dve.bn_aggr(mv1[:, j, :], st1[:, j, :]).then_inc(s["mv1_ready"], 1)
                dve.wait_ge(s["sq_ready"], TPB * (b + 1))
                if b >= 1:
                    dve.wait_ge(s["rs_ready"], b)
                dve.tensor_scalar(vin[:, 0:TPB], sumsq[:, b % 2, :], 1.0 / CD, EPS_RMS, ALU.mult, ALU.add)\
                   .then_inc(s["vin_ready"], 1)
                dve.wait_ge(s["mv1_ready"], TPB * (b + 1))
                dve.tensor_scalar(vin[:, TPB:2 * TPB], mv1[:, :, 1], 1.0 + EPS_RMS, EPS_LN * EPS_RMS,
                                  ALU.mult, ALU.add).then_inc(s["vin_ready"], 1)

            def norm_first(b):
                dve.wait_ge(s["rs_ready"], b + 1)
                if b >= 1:
                    dve.wait_ge(s["hn_ready"], TPB * b)
                dve.scalar_tensor_tensor(nb1[:, :], mv1[:, :, 0], -1.0, rs[:, b % 2, TPB:2 * TPB],
                                         ALU.mult, ALU.mult).then_inc(s["nb1_ready"], 1)
                dve.wait_ge(ctx_in[b], 16)
                if b == 0:
                    dve.wait_ge(s["small_in"], 16 * 5)
                if b >= 1:
                    dve.wait_ge(s["depmm_ready"], TPB * b)
                for j in range(TPB):
                    dve.scalar_tensor_tensor(hp[:, j, :], ctx_sb[:, b % 2, j, 0:D], rs[:, b % 2, j:j + 1],
                                             ginit[:, :], ALU.mult, ALU.mult).then_inc(s["hp_ready"], 1)

            def depooled(b):
                if b >= 1:
                    dve.wait_ge(dep_rows[b - 1], 16)
                for n in range(PAIRS):
                    dve.wait_ge(s["depmm_ready"], b * TPB + 2 * n + 2)
                    dve.tensor_tensor(dep[:, 2 * n:2 * n + 2, :], pD[n][:, :].rearrange("p (j d) -> p j d", d=D),
                                      bin_[:, :].unsqueeze(1).broadcast_to([P, 2, D]), ALU.add)\
                       .then_inc(s["dep_ready"], 1)

            def second(b):
                dve.wait_ge(dg_in[b], 16 * TPB)
                dve.wait_ge(s["hn_ready"], TPB * (b + 1))
                flat = x_all[:, b * TPB:(b + 1) * TPB, :].rearrange("p j d -> p (j d)")
                dve.tensor_tensor(flat, flat, dg[:, b % 2].rearrange("p j d -> p (j d)"), ALU.add)\
                   .then_inc(s["xd_ready"], 1)
                dve.wait_ge(s["xd_ready"], b + 1)
                xb = x_all[:, b * TPB:(b + 1) * TPB, :]
                for n in range(PAIRS):
                    dve.wait_ge(s["hmm_ready"], b * TPB + 2 * n + 2)
                    dve.tensor_tensor(pair(xb, n), pair(xb, n), pH[n][:, :], ALU.add).then_inc(s["x1_ready"], 1)
                for j in range(TPB):
                    dve.wait_ge(s["x1_ready"], b * PAIRS + j // 2 + 1)
                    dve.bn_stats(st2[:, j, :], x_all[:, b * TPB + j, :]).then_inc(s["st2_ready"], 1)
                dve.wait_ge(s["st2_ready"], TPB * (b + 1))
                for j in range(TPB):
                    dve.bn_aggr(mv2[:, j, :], st2[:, j, :]).then_inc(s["mv2_ready"], 1)
                dve.wait_ge(s["mv2_ready"], TPB * (b + 1))
                if b >= 1:
                    dve.wait_ge(s["z_ready"], TPB * b)
                dve.tensor_scalar(vin2[:, :], mv2[:, :, 1], EPS_LN, None, ALU.add).then_inc(s["vin2_ready"], 1)

            def norm_second(b):
                dve.wait_ge(s["rs2_ready"], b + 1)
                dve.scalar_tensor_tensor(nb2[:, :], mv2[:, :, 0], -1.0, rs2[:, :], ALU.mult, ALU.mult)\
                   .then_inc(s["nb2_ready"], 1)

            def route(b):
                dve.wait_ge(s["logit_mm"], b + 1)
                dve.tensor_copy(logits[:, :, :].rearrange("p j e -> p (j e)"), p_logit).then_inc(s["logit_ready"], 1)
                dve.wait_ge(s["logit_ready"], b + 1)
                for j in range(TPB):
                    dve.max(top[:, j, :], logits[:, j, :]).then_inc(s["top_ready"], 1)
                dve.wait_ge(s["top_ready"], TPB * (b + 1))
                for j in range(TPB):
                    dve.max_index(topi[:, j, :], top[:, j, :], logits[:, j, :]).then_inc(s["topi_ready"], 1)
                dve.tensor_tensor(gap[:, :], top[:, :, 1], top[:, :, 0], ALU.subtract).then_inc(s["gap_ready"], 1)
                dve.wait_ge(s["topi_ready"], TPB * (b + 1))
                if b >= 1:
                    dve.wait_ge(s["oh_ready"], b)
                dve.tensor_copy(topf[:, :, :], topi[:, :, 0:2].rearrange("p j r -> p r j")).then_inc(s["topf_ready"], 1)
                dve.wait_ge(s["topf_ready"], b + 1)
                tiles = slice(b * TPB, (b + 1) * TPB)
                dve.tensor_tensor(oh[:, :, tiles, :], iota_f[:, 0:E].unsqueeze(1).unsqueeze(1)
                                  .broadcast_to([P, 2, TPB, E]),
                                  topf[:, :, :].unsqueeze(3).broadcast_to([P, 2, TPB, E]),
                                  ALU.is_equal).then_inc(s["oh_ready"], 1)
                dve.wait_ge(s["oh_ready"], b + 1)
                dve.tensor_tensor(picked[:, :, :], oh[:, 0, tiles], oh[:, 1, tiles], ALU.add)\
                   .then_inc(s["picked_ready"], 1)

            def places(b):
                tiles = slice(b * TPB, (b + 1) * TPB)
                dve.wait_ge(s["egap_ready"], b + 1)
                dve.tensor_scalar(den[:, :], egap[:, :], 1.0, None, ALU.add).then_inc(s["den_ready"], 1)
                dve.wait_ge(s["den_ready"], b + 1)
                dve.reciprocal(wts[:, 0, tiles], den[:, :]).then_inc(s["wts_ready"], 1)
                dve.wait_ge(s["wts_ready"], 2 * b + 1)
                dve.tensor_tensor(wts[:, 1, tiles], egap[:, :], wts[:, 0, tiles], ALU.mult)\
                   .then_inc(s["wts_ready"], 1)
                dve.wait_ge(s["rank_mm"], b + 1)
                dve.wait_ge(s["base_step"], 1 + b)
                dve.tensor_tensor(posf[:, :, :], p_rank.rearrange("p (j e) -> p j e", e=E),
                                  base[:, :].unsqueeze(1).broadcast_to([P, TPB, E]), ALU.add)\
                   .then_inc(s["posf_ready"], 1)
                dve.wait_ge(s["posf_ready"], b + 1)
                dve.tensor_tensor(base[:, :], base[:, :], p_total, ALU.add).then_inc(s["base_step"], 1)
                if b >= 1:
                    dve.wait_ge(s["rank_ready"], 4 * b)
                for r in range(2):
                    dve.tensor_tensor(posm[:, r], oh[:, r, tiles], posf[:, :, :], ALU.mult)\
                       .then_inc(s["posm_ready"], 1)
                dve.wait_ge(s["posm_ready"], 2 * (b + 1))
                dve.tensor_reduce(blk[:, :, tiles], posm[:, :, :, :], AX.X, ALU.add).then_inc(s["rank_ready"], 1)
                dve.wait_ge(s["rank_ready"], 4 * b + 1)
                dve.tensor_copy(rank[:, :, tiles], blk[:, :, tiles]).then_inc(s["rank_ready"], 1)
                dve.wait_ge(s["rank_ready"], 4 * b + 2)
                dve.tensor_scalar(rank_lo[:, :, tiles], rank[:, :, tiles], P - 1, None, ALU.bitwise_and)\
                   .then_inc(s["rank_ready"], 1)
                dve.tensor_scalar(rank_hi[:, :, tiles], rank[:, :, tiles], 7, None, ALU.logical_shift_right)\
                   .then_inc(s["rank_ready"], 1)

            def place_rows(b):
                tiles = slice(b * TPB, (b + 1) * TPB)
                dve.wait_ge(s["rank_ready"], 4 * (b + 1))
                for r in range(2):
                    dve.tensor_tensor(lo_hot[:, r * B * TPB + b * TPB:r * B * TPB + (b + 1) * TPB, :],
                                      iota_f[:, :].unsqueeze(1).broadcast_to([P, TPB, P]),
                                      rank_lo[:, r, tiles].unsqueeze(2).broadcast_to([P, TPB, P]),
                                      ALU.is_equal).then_inc(s["lohot_ready"], 1)

            def scale_win():
                dve.wait_ge(s["small_in"], 16 * 5)
                dve.wait_ge(s["wT_ready"], 1)
                for k in range(KD):
                    dve.tensor_scalar(win[:, k, :], p_win[:, k * D:(k + 1) * D], gres[:, k:k + 1], None, ALU.mult)\
                       .then_inc(s["gw_ready"], 1)

            lengths()
            stats_first(0)
            position(0)
            norm_first(0)
            position(1)
            position(2)
            stats_first(1)
            depooled(0)
            position(3)
            norm_first(1)
            plugs()
            scale_win()
            plugs_end()
            stats_first(2)
            depooled(1)
            for k in range(2, B + 3):
                if k < B:
                    norm_first(k)
                if 4 <= k != B + 1:
                    places(k - 4)
                if k < B + 2:
                    second(k - 2)
                if k == B + 1:
                    places(k - 4)
                    norm_second(k - 2)
                    place_rows(0)
                if k == B + 2:
                    place_rows(1)
                    place_rows(2)
                if k >= 3:
                    route(k - 3)
                if k <= B:
                    norm_second(k - 2)
                if k + 1 < B:
                    stats_first(k + 1)
                if k < B:
                    depooled(k)
                if k == B:
                    dve.wait_ge(s["hp_ready"], B * TPB)
                    dve.wait_ge(s["sq_ready"], B * TPB)
            places(B - 1)

            count = [0]

            def tbl(ins):
                count[0] += 1
                ins.then_inc(s["tbl_step"], 1)
                dve.wait_ge(s["tbl_step"], count[0])

            dve.wait_ge(s["base_step"], 1 + B)
            dve.wait_ge(s["bf16_ready"], 14)
            tbl(dve.tensor_scalar(n_i[:, :], base[:, :], float(P - 1), None, ALU.add))
            tbl(dve.tensor_scalar(n_i[:, :], n_i[:, :], 7, None, ALU.logical_shift_right))
            tbl(dve.tensor_scalar(nblk[:, :], n_i[:, :], 1.0, None, ALU.max))
            tbl(dve.tensor_tensor_scan(cum[:, :], ones[:, 0:E], nblk[:, :], 0.0, ALU.mult, ALU.add))
            tbl(dve.tensor_tensor(start[:, :], cum[:, :], nblk[:, :], ALU.subtract))
            dve.wait_ge(s["count_ready"], B)
            tbl(dve.tensor_tensor(startm, oh[:, :, :, :].rearrange("p r j e -> p (r j) e"),
                                  start[:, :].unsqueeze(1).broadcast_to([P, N_LIST, E]), ALU.mult))
            blk_v = blk[:, :, :].rearrange("p r j -> p (r j)")
            tbl(dve.tensor_reduce(blk_v, startm, AX.X, ALU.add))
            tbl(dve.tensor_tensor(blk_v, blk_v, rank_hi[:, :, :].rearrange("p r j -> p (r j)"), ALU.add))
            place_rows(3)
            dve.wait_ge(s["logit_mm"], B)
            dve.wait_ge(s["ids_ready"], 1)
            halves = [slice(r * B * TPB, (r + 1) * B * TPB) for r in range(2)]
            full3 = [P, B * TPB, TABLE]
            for r, half in enumerate(halves):
                dve.tensor_tensor(hi_eq[:, half, :], iota_f[:, 0:TABLE].unsqueeze(1).broadcast_to(full3),
                                  blk[:, r, :].unsqueeze(2).broadcast_to(full3), ALU.is_equal)\
                   .then_inc(s["hi_step"], 1)
                dve.wait_ge(s["hi_step"], 2 * r + 1)
                dve.tensor_scalar(hi_idx[:, half, 0, :], hi_eq[:, half, :], ids_f[:, 0:1], None, ALU.mult)\
                   .then_inc(s["hi_step"], 1)
                if r == 1:
                    dve.tensor_tensor(hi_idx[:, half, 1, :], hi_eq[:, half, :],
                                      tiles_b[:, half].unsqueeze(2).broadcast_to(full3), ALU.mult)\
                       .then_inc(s["hi_step"], 1)
            wts_v = wts[:, :, :].rearrange("p r j -> p (r j)")
            rests = (wts_v, w_rest[:, 0, :], w_rest[:, 1, :])
            for n in range(3):
                if n:
                    dve.wait_ge(s["part_step"], 2 * n)
                dve.tensor_copy(w_parts[:, n, :], rests[n]).then_inc(s["part_step"], 1)
                if n < 2:
                    dve.wait_ge(s["part_step"], 2 * n + 1)
                    dve.tensor_tensor(rests[n + 1], rests[n], w_parts[:, n, :], ALU.subtract)\
                       .then_inc(s["part_step"], 1)

            dve.wait_ge(s["list_mm"], 1)
            dve.tensor_copy(number[:, :], p_idx[:, 0:TABLE]).then_inc(s["idx_step"], 1)
            dve.wait_ge(s["idx_step"], 1)
            dve.scalar_tensor_tensor(number[:, :], p_idx[:, TABLE:2 * TABLE], float(P), number[:, :],
                                     ALU.mult, ALU.add).then_inc(s["idx_step"], 1)
            dve.wait_ge(s["idx_step"], 2)
            dve.scalar_tensor_tensor(unused[:, :], number[:, :], 0.0, ids_f[:, B * TPB:B * TPB + 1]
                                     .broadcast_to([P, TABLE]), ALU.is_equal, ALU.mult).then_inc(s["idx_step"], 1)
            dve.wait_ge(s["idx_step"], 3)
            dve.scalar_tensor_tensor(idx_all[:, :], number[:, :], -1.0, unused[:, :], ALU.add, ALU.add)\
               .then_inc(s["idx_ready"], 1)
            dve.wait_ge(s["idx_ready"], 1)
            dve.tensor_copy(gidx[:, :], idx_all[:, 0:2]).then_inc(s["gidx_ready"], 2)

            dve.tensor_copy(blocks_i[:, :], cum[0:1, E - 1:E]).then_inc(s["blocks_ready"], 1)
            at = ids_f[:, 0:1]
            done, last_, done_blocks, done_before = (stepm[:, n, :] for n in range(4))
            dve.tensor_scalar(done, cum[:, :], at, None, ALU.is_lt).then_inc(s["fields_ready"], 1)
            dve.tensor_scalar(last_, cum[:, :], at, None, ALU.is_equal).then_inc(s["fields_ready"], 1)
            dve.scalar_tensor_tensor(done_blocks, cum[:, :], at, nblk[:, :], ALU.is_lt, ALU.mult)\
               .then_inc(s["fields_ready"], 1)
            dve.tensor_scalar(done_before, cum[:, :], -1.0, at, ALU.subtract, ALU.is_lt)\
               .then_inc(s["fields_ready"], 1)
            dve.wait_ge(s["fields_ready"], 4)
            dve.tensor_reduce(steps[:, :], stepm[:, :, :], AX.X, ALU.add).then_inc(s["fields_ready"], 1)
            dve.wait_ge(s["fields_ready"], 5)
            e_, last_, before_, e_before = (steps[:, n:n + 1] for n in range(4))
            j_, low6, low4, two_ = (low[:, n:n + 1] for n in range(4))
            f_e, f_before, f_chunk, f_w2, f_w3, f_load, f_run, f_m = (fields[:, n:n + 1] for n in range(8))
            dve.scalar_tensor_tensor(j_, at, 1.0, before_, ALU.subtract, ALU.subtract).then_inc(s["fields_ready"], 1)
            dve.tensor_scalar(f_e, e_, float(E - 1), None, ALU.min).then_inc(s["fields_ready"], 1)
            dve.tensor_scalar(f_before, e_before, float(E - 1), None, ALU.min).then_inc(s["fields_ready"], 1)
            dve.tensor_scalar(low6, e_, float(E - 2), None, ALU.is_le).then_inc(s["fields_ready"], 1)
            dve.tensor_scalar(low4, e_, float(E - 4), None, ALU.is_le).then_inc(s["fields_ready"], 1)
            dve.tensor_scalar(f_run, cum[:, E - 1:E], at, None, ALU.is_ge).then_inc(s["fields_ready"], 1)
            dve.wait_ge(s["fields_ready"], 11)
            dve.scalar_tensor_tensor(f_w2, j_, 1.0, last_, ALU.is_le, ALU.mult).then_inc(s["fields_ready"], 1)
            dve.scalar_tensor_tensor(f_w3, j_, 0.0, last_, ALU.is_equal, ALU.mult).then_inc(s["fields_ready"], 1)
            dve.scalar_tensor_tensor(f_chunk, j_, 2.0, low6, ALU.is_le, ALU.mult).then_inc(s["fields_ready"], 1)
            dve.tensor_scalar(f_m, j_, 2.0, None, ALU.min).then_inc(s["fields_ready"], 1)
            dve.wait_ge(s["fields_ready"], 15)
            dve.scalar_tensor_tensor(two_, j_, 2.0, f_w2, ALU.is_equal, ALU.add).then_inc(s["fields_ready"], 1)
            dve.wait_ge(s["fields_ready"], 16)
            dve.tensor_tensor(f_load, two_, low4, ALU.mult).then_inc(s["fields_ready"], 1)
            dve.wait_ge(s["fields_ready"], 17)
            dve.tensor_tensor(fields[:, :], fields[:, :], weights[:, :], ALU.mult).then_inc(s["fields_ready"], 1)
            dve.wait_ge(s["fields_ready"], 18)
            dve.tensor_reduce(word[:, :], fields[:, :], AX.X, ALU.add).then_inc(s["word_ready"], 1)

            dve.wait_ge(s["word_mm"], 1)
            dve.tensor_copy(table[:, :], p_word).then_inc(s["table_ready"], 1)

            def weight_rows(r):
                dve.wait_ge(s["part_step"], 5)
                for n in range(3):
                    dve.tensor_tensor(hi_w[:, halves[r], n, :], hi_eq[:, halves[r], :],
                                      w_parts[:, n, halves[r]].unsqueeze(2).broadcast_to(full3), ALU.mult)\
                       .then_inc(s["hi_step"], 1)

            def weights_out():
                dve.wait_ge(s["list_mm"], 2)
                dve.tensor_copy(w_all[:, :], p_w[:, 2 * TABLE:3 * TABLE]).then_inc(s["idx_ready"], 1)
                for n in (1, 0):
                    dve.wait_ge(s["idx_ready"], 3 - n)
                    dve.tensor_tensor(w_all[:, :], w_all[:, :], p_w[:, n * TABLE:(n + 1) * TABLE], ALU.add)\
                       .then_inc(s["idx_ready"], 1)

            def xT(i, q):
                dve.wait_ge(s["xThi_ready"], i + 1)
                dve.tensor_tensor(xT_lo[:, q].rearrange("p k t -> p (k t)"), p_xT,
                                  xT_hi[:, q].bitcast(f32).rearrange("p k t -> p (k t)"), ALU.subtract)\
                   .then_inc(s["xTlo_ready"], 1)

            def h(i, part):
                cols = slice(part * HALF, (part + 1) * HALF)
                dve.wait_ge(s[f"silu{part}_done"], i + 1)
                if not isinstance(i, int) or i > 0:
                    dve.wait_ge(s[f"th{part}_done"], i)
                dve.tensor_tensor(hmul[:, cols], gact[:, cols], p_lin[part][:, :], ALU.mult)\
                   .then_inc(s[f"h{part}_done"], 1)

            def hT(i, q, part):
                ks = slice(part * KF // 2, (part + 1) * KF // 2)
                dve.wait_ge(s[f"hT{part}hi_ready"], i + 1)
                dve.tensor_tensor(hT_lo[:, q, ks].rearrange("p k t -> p (k t)"), p_hT[part][:, :],
                                  hT_hi[:, q, ks].bitcast(f32).rearrange("p k t -> p (k t)"), ALU.subtract)\
                   .then_inc(s[f"hT{part}lo_ready"], 1)

            def next_index(i, q, half):
                dve.wait_ge(blk_in[q], 16 * half)
                dve.tensor_copy(gidx[:, q:q + 1], idx_all[:, ds(i, 1)]).then_inc(s["gidx_ready"], 1)

            def meta(i, q):
                dve.wait_ge(s["idx_ready"], 4)
                dve.wait_ge(s["added_rows"], OUT_INIT + 16 * (i - 1))
                dve.tensor_copy(wtok[:, q:q + 1], w_all[:, ds(i, 1)])
                dve.tensor_copy(itok[:, q:q + 1], idx_all[:, ds(i, 1)]).then_inc(s["meta_ready"], 1)

            def step(i, q, half, word):
                later = not isinstance(i, int) or i > 0
                h(i, 0)
                if later:
                    hT(i - 1, 1 - q, 1)
                    meta(i - 1, 1 - q)
                xT(i + 1, 1 - q)
                next_index(i + 3, 1 - q, half + q + 1)
                if not later:
                    weights_out()
                h(i, 1)
                hT(i, q, 0)
                with dve.If(word & F_CHUNK):
                    e = expert(word)
                    raw3 = ((e + 1) & 1) * 3
                    split_lo(dve, e + 1, raw3, chunk_of(word))
                    with dve.If(word & F_W2):
                        with dve.If(word & F_W3):
                            split_lo(dve, e + 1, raw3, 1)
                        split_lo(dve, e + 1, raw3, 2)

            dve.wait_ge(s["table_ready"], 1)
            dve.wait_ge(s["x1_rows"], 16 * B)
            for b in range(B):
                dve.wait_ge(z_out[b], 16)
            dve.wait_ge(s["lo_first"], 3)
            dve.sem_inc(s["lo_ready"], 3)
            xT(0, 0)
            next_index(2, 0, 1)
            weight_rows(0)
            weight_rows(1)
            def drain(i, q):
                hT(i, q, 1)
                meta(i, q)

            blocks = block_count(dve)
            over_steps(dve, step)
            at_end(dve, blocks, drain)

        @block.tensor
        def _(pe):
            def prefix():
                pe.wait_ge(s["consts"], 2)
                pe.wait_ge(s["scan_ready"], 1)
                pe.matmul(p_prefix, tri[:, :], ln_s[:, :, :, CH - 1].rearrange("p k b -> p (k b)"),
                          start=True, stop=True).then_inc(s["prefix_ready"], 1)

            def boundaries(b):
                pe.wait_ge(s["onehot_ready"], b + 2)
                for k in range(CH):
                    mm = pe.matmul(p_count[:, b * TPB:(b + 1) * TPB], onehot_lo[:, b % 2, k, :],
                                   onehot_hi[:, b * CH + k, :], start=(k == 0), stop=(k == CH - 1))
                mm.then_inc(s["count_ready"], 1)

            def plugs():
                pe.wait_ge(s["bmask_ready"], 1)
                pe.wait_ge(s["bf16_ready"], 12)
                flat = bmask[:, :, :].rearrange("p b j -> p (b j)")
                pe.matmul(p_plug, tri_b[:, :], flat, start=True, stop=False)
                pe.matmul(p_plug, ident_b[:, :], flat, start=False, stop=False)
                for j in range(TPB - 1):
                    more = TPB - 1 - j
                    mm = pe.matmul(p_plug.rearrange("p (b j) -> p b j", j=TPB)[:, :, j + 1:TPB], ones_b[:, :],
                                   bmask[:, :, j:j + 1].broadcast_to([P, B, more]),
                                   start=False, stop=(j == TPB - 2))
                mm.then_inc(s["plugmm_ready"], 1)

            def transposes(src, j, signal):
                for k in range(KD):
                    mm = pe.transpose(pT[j // 2][:, (j % 2) * D + k * P:(j % 2) * D + (k + 1) * P],
                                      src[:, j, k * P:(k + 1) * P], ident[:, :])
                mm.then_inc(signal, 1)

            def first(b):
                if b == 0:
                    pe.wait_ge(s["affine_step"], 6 + len(decay))
                if b >= 1:
                    pe.wait_ge(s["dep_ready"], PAIRS * b)
                for j in range(TPB):
                    pe.wait_ge(s["hp_ready"], b * TPB + j + 1)
                    acc = pD[j // 2][:, (j % 2) * D:(j % 2 + 1) * D]
                    mm = pe.matmul(acc, decayT[:, 0:P], hp[:, j, :], start=True, stop=(j == 0))
                    if j:
                        mm = pe.matmul(acc, decayT[:, P:2 * P], hp[:, j - 1, :], start=False, stop=True)
                    mm.then_inc(s["depmm_ready"], 1)
                if 1 <= b <= 2:
                    pe.wait_ge(s["hnT_ready"], PAIRS * b)
                elif b > 2:
                    pe.wait_ge(s["zT_ready"], PAIRS * (b - 2))
                for j in range(TPB):
                    pe.wait_ge(s["hn_ready"], b * TPB + j + 1)
                    transposes(hn, j, s["tn_ready"])

            def through_win(b):
                if b == 0:
                    pe.wait_ge(s["gw_ready"], KD)
                else:
                    pe.wait_ge(s["x1_ready"], PAIRS * b)
                for j in range(TPB):
                    pe.wait_ge(s["hnT_ready"], b * PAIRS + j // 2 + 1)
                    for k in range(KD):
                        mm = pe.matmul(pH[j // 2][:, (j % 2) * D:(j % 2 + 1) * D],
                                       hnT[b % 2][:, j, k * P:(k + 1) * P], win[:, k, :],
                                       start=(k == 0), stop=(k == KD - 1))
                    mm.then_inc(s["hmm_ready"], 1)

            def router(b):
                pe.wait_ge(s["hnT_ready"], PAIRS * min(b + 3, B))
                if b >= 1:
                    pe.wait_ge(s["zT_ready"], PAIRS * b)
                for j in range(TPB):
                    pe.wait_ge(s["z_ready"], b * TPB + j + 1)
                    transposes(z[:, b % 2], j, s["tz_ready"])

            def logits_of(b):
                if b >= 1:
                    pe.wait_ge(s["base_step"], 1 + b)
                for j in range(TPB):
                    pe.wait_ge(s["zT_ready"], b * PAIRS + j // 2 + 1)
                    for k in range(KD):
                        mm = pe.matmul(p_logit[:, j * E:(j + 1) * E], zT[:, j, k * P:(k + 1) * P], gate[:, k, :],
                                       start=(k == 0), stop=(k == KD - 1))
                mm.then_inc(s["logit_mm"], 1)

            def ranks(b):
                pe.wait_ge(s["picked_ready"], b + 1)
                pe.matmul(p_rank, tri_b[:, :], picked[:, :, :].rearrange("p j e -> p (j e)"), start=True, stop=False)
                for j in range(TPB - 1):
                    more = TPB - 1 - j
                    pe.matmul(p_rank.rearrange("p (j e) -> p j e", e=E)[:, j + 1:TPB, :], ones_b[:, :],
                              picked[:, j:j + 1, :].broadcast_to([P, more, E]), start=False, stop=(j == TPB - 2))
                for j in range(TPB):
                    mm = pe.matmul(p_total, ones_b[:, :], picked[:, j, :], start=(j == 0), stop=(j == TPB - 1))
                mm.then_inc(s["rank_mm"], 1)

            def lists(acc, rows, steps):
                for r in range(2):
                    pe.wait_ge(s["hi_step"], steps[r])
                    for n in range(r * B * TPB, (r + 1) * B * TPB):
                        mm = pe.matmul(acc, lo_hot[:, n, :], rows[:, n].rearrange("p v c -> p (v c)"),
                                       start=(n == 0), stop=(n == N_LIST - 1))
                mm.then_inc(s["list_mm"], 1)

            prefix()
            pe.wait_ge(s["small_in"], 16 * 5)
            for k in range(KD):
                for m in range(KD):
                    mm = pe.transpose(p_win[:, k * D + m * P:k * D + (m + 1) * P], win[:, m, k * P:(k + 1) * P],
                                      ident[:, :])
            mm.then_inc(s["wT_ready"], 1)
            boundaries(0)
            first(0)
            for b in range(1, B):
                boundaries(b)
            plugs()
            first(1)
            through_win(0)
            for k in range(2, B + 3):
                if k < B:
                    first(k)
                if k == B + 1:
                    router(k - 2)
                if k == B:
                    through_win(k - 1)
                if k >= 3:
                    ranks(k - 3)
                if k < B:
                    through_win(k - 1)
                if k < B + 1:
                    router(k - 2)
                if k < B + 2:
                    logits_of(k - 2)
            pe.wait_ge(s["lohot_ready"], 2 * B)
            pe.wait_ge(s["tile_step"], 1)
            lists(p_idx, hi_idx, (2, 5))
            pe.wait_ge(s["word_ready"], 1)
            pe.matmul(p_word, word[:, :], ident[:, 0:TABLE], start=True, stop=True).then_inc(s["word_mm"], 1)

            def three(acc, x_hi, x_lo, w_hi, w_lo, start, stop):
                for n, (xp, wp) in enumerate(((x_hi, w_hi), (x_hi, w_lo), (x_lo, w_hi))):
                    for out_, w_ in zip(acc, wp):
                        mm = pe.matmul(out_, xp, w_, start=start and n == 0, stop=stop and n == 2)
                return mm

            def xT(i, q, half):
                pe.wait_ge(blk_in[q], 16 * (half + 1))
                for k in range(KD):
                    mm = pe.transpose(p_xT[:, k * P:(k + 1) * P], xblk[:, q, k * P:(k + 1) * P], ident[:, :])
                mm.then_inc(s["xT_done"], 1)

            def up(slot, q, part):
                def weights(t, k):
                    return [t[:, ds(slot, 1), m, k, part * HALF:(part + 1) * HALF].rearrange("p o f -> p (o f)")
                            for m in range(2)]
                for k in range(KD):
                    mm = three((p_gate[part][:, :], p_lin[part][:, :]), xT_hi[:, q, k, :], xT_lo[:, q, k, :],
                               weights(up_hi, k), weights(up_lo, k), k == 0, k == KD - 1)
                mm.then_inc(s[f"up{part}_done"], 1)

            def hT(i, part):
                pe.wait_ge(s[f"h{part}_done"], i + 1)
                for k in range(KF // 2):
                    f0 = (part * KF // 2 + k) * P
                    mm = pe.transpose(p_hT[part][:, k * P:(k + 1) * P], hmul[:, f0:f0 + P], ident[:, :])
                mm.then_inc(s[f"th{part}_done"], 1)

            def down(i, q, e, slot, by_halves=False):
                if by_halves:
                    pe.wait_ge(s["hT0lo_ready"], i + 1)
                    pe.wait_ge(s["y_ready"], i + 1)
                else:
                    pe.wait_ge(s["hT1lo_ready"], i + 1)
                pe.wait_ge(s["lo_ready"], e * 3 + 3)
                for k in range(KF):
                    if by_halves and k == KF // 2:
                        pe.wait_ge(s["hT1lo_ready"], i + 1)
                    w_hi, w_lo = ([t[:, ds(slot, 1), k, :].rearrange("p o d -> p (o d)")] for t in (dn_hi, dn_lo))
                    mm = three((p_y,), hT_hi[:, q, k, :], hT_lo[:, q, k, :], w_hi, w_lo, k == 0, k == KF - 1)
                mm.then_inc(s["y_done"], 1)

            def step(i, q, half, word):
                later = not isinstance(i, int) or i > 0
                slot = word & 1
                pe.wait_ge(s["xTlo_ready"], i + 1)
                pe.wait_ge(s["lo_ready"], expert(word) * 3 + 2)
                up(slot, q, 0)
                if not later:
                    lists(p_w, hi_w, (8, 11))
                if later:
                    hT(i - 1, 1)
                xT(i + 1, 1 - q, half + q)
                up(slot, q, 1)
                hT(i, 0)
                if later:
                    down(i - 1, 1 - q, expert_before(word), (word >> PREV_BIT) & 1)

            def drain(i, q):
                hT(i, 1)
                down(i, q, E - 1, (E - 1) & 1, by_halves=True)

            pe.wait_ge(s["table_ready"], 1)
            blocks = block_count(pe)
            xT(0, 0, 0)
            over_steps(pe, step)
            at_end(pe, blocks, drain)


_INS = ["x", "ctx_2048", "mask_BxS2_if0", "L0_xattn_W_in", "L0_xattn_b_in", "L0_xattn_g_res", "L0_xattn_g_init",
        "L0_ffn_gate_w", "L0_ffn_w1", "L0_ffn_w3", "L0_ffn_w2"]


def kernel(**inputs):
    import numpy as _np
    import concourse.bacc as _bacc
    from concourse import mybir as _mybir
    from concourse.bass_utils import run_bass_kernel_spmd as _run

    nc = _bacc.Bacc("TRN2", target_bir_lowering=False, num_devices=1)
    arrays, args = {}, []
    for name in _INS:
        a = _np.ascontiguousarray(inputs[name])
        arrays[f"in_{name}"] = a
        args.append(nc.dram_tensor(f"in_{name}", a.shape, _mybir.dt.from_np(a.dtype), kind="ExternalInput").ap())
    args.append(nc.dram_tensor("out_0", (T + P, D), _mybir.dt.float32, kind="ExternalOutput").ap())
    build(nc, *args)
    r = _run(nc, [arrays], core_ids=[0])
    return r.results[0]["out_0"][0:T].reshape(B, S, D)
```
